# Optimizing a Trainium2 kernel written in Bass

```python
import numpy as np
import jax
import jax.numpy as jnp

def _softmax(x, axis=-1):
    return jax.nn.softmax(x, axis=axis)

def _gelu(x):
    return jax.nn.gelu(x, approximate=True)

def _silu(x):
    return jax.nn.silu(x)

def _sigmoid(x):
    return jax.nn.sigmoid(x)

def _layernorm(x, axis=-1, eps=1e-05):
    m = jnp.mean(x, axis=axis, keepdims=True)
    v = jnp.var(x, axis=axis, keepdims=True)
    return (x - m) / jnp.sqrt(v + eps)

def _scatter_add(tgt, idx, src, axis=0):
    return tgt.at[idx].add(src)

def _segment_sum(src, seg, n):
    return jax.ops.segment_sum(src, seg, n)
kernel_name = 'mk_macaron_d2_jaxref_r8_1704b8'

def setup_inputs(seed: int=0):
    np.random.seed(seed)
    _w = jnp.asarray

    def _L0_attn_setup():
        import jax, jax.numpy as jnp
        import numpy as np
        HEADS = 16
        DIM_HEAD = 64
        SEG = 32
        SCALE = DIM_HEAD ** (-0.5)
        INNER = HEADS * DIM_HEAD

        def elu1(x):
            return jax.nn.elu(x) + 1.0

        def rope(t, pos):
            d = t.shape[-1]
            freqs = 10000.0 ** (-jnp.arange(0, d, 2, dtype=jnp.float32) / d)
            ang = pos[:, None] * freqs
            cos = jnp.repeat(jnp.cos(ang), 2, axis=-1)
            sin = jnp.repeat(jnp.sin(ang), 2, axis=-1)
            t2 = t.reshape(t.shape[:-1] + (d // 2, 2))
            rot = jnp.stack((-t2[..., 1], t2[..., 0]), axis=-1).reshape(t.shape)
            return t * cos + rot * sin

        def _reference_tuple_inner(x, w_qkv, w_out, ln_g, ln_b, mem_beta):
            B, N, D = x.shape
            mu = x.mean(-1, keepdims=True)
            var = x.var(-1, keepdims=True)
            xn = (x - mu) / jnp.sqrt(var + 1e-05) * ln_g + ln_b
            qkv = xn @ w_qkv
            q, k, v = jnp.split(qkv, 3, axis=-1)

            def to_heads(t):
                return t.reshape(B, N, HEADS, DIM_HEAD).transpose(0, 2, 1, 3)
            q, k, v = map(to_heads, (q, k, v))
            next_k, next_v = (k, v)
            pos = jnp.arange(N, dtype=jnp.float32)
            qr, kr = (rope(q, pos), rope(k, pos))
            W = N // SEG

            def to_segs(t):
                return t.reshape(B, HEADS, W, SEG, DIM_HEAD).transpose(2, 0, 1, 3, 4)
            qs, ks, vs, qnope, knope = map(to_segs, (qr, kr, v, q, k))
            mask = jnp.tril(jnp.ones((SEG, SEG), bool))
            beta = jax.nn.sigmoid(mem_beta)
            mem0 = jnp.zeros((B, HEADS, DIM_HEAD, DIM_HEAD), x.dtype)
            z0 = jnp.full((B, HEADS, DIM_HEAD), 1e-06, x.dtype)

            def step(carry, inp):
                mem, z = carry
                q_s, k_s, v_s, qn_s, kn_s = inp
                scores = jnp.einsum('bhnd,bhmd->bhnm', q_s, k_s) * SCALE
                scores = jnp.where(mask, scores, -jnp.inf)
                sdpa = jnp.einsum('bhnm,bhmd->bhnd', jax.nn.softmax(scores, axis=-1), v_s)
                sq = elu1(qn_s)
                num = jnp.einsum('bhnk,bhkv->bhnv', sq, mem)
                den = jnp.einsum('bhnk,bhk->bhn', sq, z)[..., None]
                mem_out = num / (den + 1e-06)
                out = beta * mem_out + (1.0 - beta) * sdpa
                sk = elu1(kn_s)
                prev_v = jnp.einsum('bhnk,bhkv->bhnv', sk, mem) / jnp.einsum('bhnk,bhk->bhn', sk, z)[..., None]
                mem = mem + jnp.einsum('bhnk,bhnv->bhkv', sk, v_s - prev_v)
                z = z + sk.sum(axis=2)
                return ((mem, z), out)
            _, outs = jax.lax.scan(step, (mem0, z0), (qs, ks, vs, qnope, knope))
            o = outs.transpose(1, 0, 3, 2, 4).reshape(B, N, INNER)
            out = o @ w_out
            return (out, next_k, next_v)
        key = jax.random.key(seed)
        k1, k2, k3 = jax.random.split(key, 3)
        B, N, D = (4, 512, 128)
        x = jax.random.normal(k1, (B, N, D), dtype=jnp.float32)
        w_qkv = jax.random.normal(k2, (D, 3 * INNER), dtype=jnp.float32) * 0.02
        w_out = jax.random.normal(k3, (INNER, D), dtype=jnp.float32) * 0.02
        ln_g = jnp.ones((D,), jnp.float32)
        ln_b = jnp.zeros((D,), jnp.float32)
        mem_beta = jnp.zeros((1, HEADS, 1, 1), jnp.float32)
        return {'x': x, 'w_qkv': w_qkv, 'w_out': w_out, 'ln_g': ln_g, 'ln_b': ln_b, 'mem_beta': mem_beta}
    _L0_attn_in = _L0_attn_setup()

    def _L0_ffn_setup():
        import jax, jax.numpy as jnp
        import numpy as np
        E = 8
        TOP_K = 2
        ROUTE_SCALE = 1.0
        ALPHA = 1.702
        LIMIT = 7.0
        D = 128
        F = 128
        B, S = (2, 128)

        def swiglu(h):
            g = jnp.minimum(h[..., ::2], LIMIT)
            l = jnp.clip(h[..., 1::2], -LIMIT, LIMIT)
            return g * jax.nn.sigmoid(ALPHA * g) * (l + 1.0)
        if __name__ == '__main__':
            out = reference(**setup_inputs())
            print(out.shape, out.dtype)
        key = jax.random.key(seed)
        ks = jax.random.split(key, 16)
        sd = 1.0 / np.sqrt(D)
        sf = 1.0 / np.sqrt(F)
        return {'x': jax.random.normal(ks[0], (B, S, D), jnp.float32), 'gate_w': jax.random.normal(ks[1], (E, D), jnp.float32) * sd, 'gate_b': jax.random.normal(ks[2], (E,), jnp.float32) * 0.01, 'w1': jax.random.normal(ks[3], (E, 2 * F, D), jnp.float32) * sd, 'b1': jax.random.normal(ks[4], (E, 2 * F), jnp.float32) * 0.01, 'w3': jax.random.normal(ks[5], (E, 2 * F, D), jnp.float32) * sd, 'b3': jax.random.normal(ks[6], (E, 2 * F), jnp.float32) * 0.01, 'w2': jax.random.normal(ks[7], (E, D, F), jnp.float32) * sf, 'b2': jax.random.normal(ks[8], (E, D), jnp.float32) * 0.01, 'sw1': jax.random.normal(ks[9], (2 * F, D), jnp.float32) * sd, 'sb1': jax.random.normal(ks[10], (2 * F,), jnp.float32) * 0.01, 'sw3': jax.random.normal(ks[11], (2 * F, D), jnp.float32) * sd, 'sb3': jax.random.normal(ks[12], (2 * F,), jnp.float32) * 0.01, 'sw2': jax.random.normal(ks[13], (D, F), jnp.float32) * sf, 'sb2': jax.random.normal(ks[14], (D,), jnp.float32) * 0.01}
    _L0_ffn_in = _L0_ffn_setup()

    def _L1_attn_setup():
        import jax, jax.numpy as jnp
        import numpy as np
        D_MODEL = 128
        N_HEADS = 8
        RADIUS = 32
        TEMP = 0.5
        ALPHA = 0.5
        KINDNESS_W = 0.3
        ENT_THRESH = 0.15
        GAUGE_THRESH = 0.3
        NEG = -1000000000.0

        def _linear(x, w, b):
            return x @ w.T + b
        key = jax.random.key(seed)
        ks = jax.random.split(key, 9)
        B, S, D = (4, 128, D_MODEL)
        s = 1.0 / np.sqrt(D)
        inp = {'x': jax.random.normal(ks[0], (B, S, D), jnp.float32)}
        for i, n in enumerate(['q', 'k', 'v', 'o', 'proj']):
            inp['W' + n] = jax.random.uniform(ks[i + 1], (D, D), jnp.float32, -s, s)
            inp['b' + n] = jnp.zeros((D,), jnp.float32)
        inp['W1'] = jax.random.uniform(ks[6], (D // 2, D), jnp.float32, -s, s)
        inp['b1'] = jnp.zeros((D // 2,), jnp.float32)
        inp['W2'] = jax.random.uniform(ks[7], (1, D // 2), jnp.float32, -1.0 / np.sqrt(D // 2), 1.0 / np.sqrt(D // 2))
        inp['b2'] = jnp.zeros((1,), jnp.float32)
        return inp
    _L1_attn_in = _L1_attn_setup()

    def _L1_ffn_setup():
        import jax, jax.numpy as jnp
        import numpy as np
        B, T, C = (2, 64, 128)
        I = 512
        E = 8
        K = 2
        key = jax.random.key(seed)
        ks = jax.random.split(key, 8)
        s = 0.02
        return {'x': jax.random.normal(ks[0], (B, T, C), jnp.float32), 'Wr1': jax.random.normal(ks[1], (C, C // 4), jnp.float32) * s, 'br1': jnp.zeros((C // 4,), jnp.float32), 'Wr2': jax.random.normal(ks[2], (C // 4, E), jnp.float32) * s, 'br2': jnp.zeros((E,), jnp.float32), 'Ws1': jax.random.normal(ks[3], (C, I), jnp.float32) * s, 'bs1': jnp.zeros((I,), jnp.float32), 'Ws2': jax.random.normal(ks[4], (I, C), jnp.float32) * s, 'bs2': jnp.zeros((C,), jnp.float32), 'We1': jax.random.normal(ks[5], (E, C, I), jnp.float32) * s, 'be1': jnp.zeros((E, I), jnp.float32), 'We2': jax.random.normal(ks[6], (E, I, C), jnp.float32) * s, 'be2': jnp.zeros((E, C), jnp.float32)}
    _L1_ffn_in = _L1_ffn_setup()
    _d = {'L0_attn_x': _L0_attn_in['x'], 'L0_attn_w_qkv': _L0_attn_in['w_qkv'], 'L0_attn_w_out': _L0_attn_in['w_out'], 'L0_attn_ln_g': _L0_attn_in['ln_g'], 'L0_attn_ln_b': _L0_attn_in['ln_b'], 'L0_attn_mem_beta': _L0_attn_in['mem_beta'], 'L0_ffn_gate_w': _L0_ffn_in['gate_w'], 'L0_ffn_gate_b': _L0_ffn_in['gate_b'], 'L0_ffn_w1': _L0_ffn_in['w1'], 'L0_ffn_b1': _L0_ffn_in['b1'], 'L0_ffn_w3': _L0_ffn_in['w3'], 'L0_ffn_b3': _L0_ffn_in['b3'], 'L0_ffn_w2': _L0_ffn_in['w2'], 'L0_ffn_b2': _L0_ffn_in['b2'], 'L0_ffn_sw1': _L0_ffn_in['sw1'], 'L0_ffn_sb1': _L0_ffn_in['sb1'], 'L0_ffn_sw3': _L0_ffn_in['sw3'], 'L0_ffn_sb3': _L0_ffn_in['sb3'], 'L0_ffn_sw2': _L0_ffn_in['sw2'], 'L0_ffn_sb2': _L0_ffn_in['sb2'], 'L1_attn_Wq': _L1_attn_in['Wq'], 'L1_attn_bq': _L1_attn_in['bq'], 'L1_attn_Wk': _L1_attn_in['Wk'], 'L1_attn_bk': _L1_attn_in['bk'], 'L1_attn_Wv': _L1_attn_in['Wv'], 'L1_attn_bv': _L1_attn_in['bv'], 'L1_attn_Wo': _L1_attn_in['Wo'], 'L1_attn_bo': _L1_attn_in['bo'], 'L1_attn_Wproj': _L1_attn_in['Wproj'], 'L1_attn_bproj': _L1_attn_in['bproj'], 'L1_attn_W1': _L1_attn_in['W1'], 'L1_attn_b1': _L1_attn_in['b1'], 'L1_attn_W2': _L1_attn_in['W2'], 'L1_attn_b2': _L1_attn_in['b2'], 'L1_ffn_Wr1': _L1_ffn_in['Wr1'], 'L1_ffn_br1': _L1_ffn_in['br1'], 'L1_ffn_Wr2': _L1_ffn_in['Wr2'], 'L1_ffn_br2': _L1_ffn_in['br2'], 'L1_ffn_Ws1': _L1_ffn_in['Ws1'], 'L1_ffn_bs1': _L1_ffn_in['bs1'], 'L1_ffn_Ws2': _L1_ffn_in['Ws2'], 'L1_ffn_bs2': _L1_ffn_in['bs2'], 'L1_ffn_We1': _L1_ffn_in['We1'], 'L1_ffn_be1': _L1_ffn_in['be1'], 'L1_ffn_We2': _L1_ffn_in['We2'], 'L1_ffn_be2': _L1_ffn_in['be2']}
    _x0 = _d['L0_attn_x']
    _d['L0_attn_x'] = jax.random.normal(jax.random.fold_in(jax.random.key(seed), 1), (4, 1024, 128), dtype=_x0.dtype)
    del _x0
    return _d

def reference(L0_attn_x, L0_attn_w_qkv, L0_attn_w_out, L0_attn_ln_g, L0_attn_ln_b, L0_attn_mem_beta, L0_ffn_gate_w, L0_ffn_gate_b, L0_ffn_w1, L0_ffn_b1, L0_ffn_w3, L0_ffn_b3, L0_ffn_w2, L0_ffn_b2, L0_ffn_sw1, L0_ffn_sb1, L0_ffn_sw3, L0_ffn_sb3, L0_ffn_sw2, L0_ffn_sb2, L1_attn_Wq, L1_attn_bq, L1_attn_Wk, L1_attn_bk, L1_attn_Wv, L1_attn_bv, L1_attn_Wo, L1_attn_bo, L1_attn_Wproj, L1_attn_bproj, L1_attn_W1, L1_attn_b1, L1_attn_W2, L1_attn_b2, L1_ffn_Wr1, L1_ffn_br1, L1_ffn_Wr2, L1_ffn_br2, L1_ffn_Ws1, L1_ffn_bs1, L1_ffn_Ws2, L1_ffn_bs2, L1_ffn_We1, L1_ffn_be1, L1_ffn_We2, L1_ffn_be2):

    def _L0_attn_ref(x, w_qkv, w_out, ln_g, ln_b, mem_beta):
        import jax, jax.numpy as jnp
        import numpy as np
        HEADS = 16
        DIM_HEAD = 64
        SEG = 32
        SCALE = DIM_HEAD ** (-0.5)
        INNER = HEADS * DIM_HEAD

        def elu1(x):
            return jax.nn.elu(x) + 1.0

        def rope(t, pos):
            d = t.shape[-1]
            freqs = 10000.0 ** (-jnp.arange(0, d, 2, dtype=jnp.float32) / d)
            ang = pos[:, None] * freqs
            cos = jnp.repeat(jnp.cos(ang), 2, axis=-1)
            sin = jnp.repeat(jnp.sin(ang), 2, axis=-1)
            t2 = t.reshape(t.shape[:-1] + (d // 2, 2))
            rot = jnp.stack((-t2[..., 1], t2[..., 0]), axis=-1).reshape(t.shape)
            return t * cos + rot * sin

        def _reference_tuple_inner(x, w_qkv, w_out, ln_g, ln_b, mem_beta):
            B, N, D = x.shape
            mu = x.mean(-1, keepdims=True)
            var = x.var(-1, keepdims=True)
            xn = (x - mu) / jnp.sqrt(var + 1e-05) * ln_g + ln_b
            qkv = xn @ w_qkv
            q, k, v = jnp.split(qkv, 3, axis=-1)

            def to_heads(t):
                return t.reshape(B, N, HEADS, DIM_HEAD).transpose(0, 2, 1, 3)
            q, k, v = map(to_heads, (q, k, v))
            next_k, next_v = (k, v)
            pos = jnp.arange(N, dtype=jnp.float32)
            qr, kr = (rope(q, pos), rope(k, pos))
            W = N // SEG

            def to_segs(t):
                return t.reshape(B, HEADS, W, SEG, DIM_HEAD).transpose(2, 0, 1, 3, 4)
            qs, ks, vs, qnope, knope = map(to_segs, (qr, kr, v, q, k))
            mask = jnp.tril(jnp.ones((SEG, SEG), bool))
            beta = jax.nn.sigmoid(mem_beta)
            mem0 = jnp.zeros((B, HEADS, DIM_HEAD, DIM_HEAD), x.dtype)
            z0 = jnp.full((B, HEADS, DIM_HEAD), 1e-06, x.dtype)

            def step(carry, inp):
                mem, z = carry
                q_s, k_s, v_s, qn_s, kn_s = inp
                scores = jnp.einsum('bhnd,bhmd->bhnm', q_s, k_s) * SCALE
                scores = jnp.where(mask, scores, -jnp.inf)
                sdpa = jnp.einsum('bhnm,bhmd->bhnd', jax.nn.softmax(scores, axis=-1), v_s)
                sq = elu1(qn_s)
                num = jnp.einsum('bhnk,bhkv->bhnv', sq, mem)
                den = jnp.einsum('bhnk,bhk->bhn', sq, z)[..., None]
                mem_out = num / (den + 1e-06)
                out = beta * mem_out + (1.0 - beta) * sdpa
                sk = elu1(kn_s)
                prev_v = jnp.einsum('bhnk,bhkv->bhnv', sk, mem) / jnp.einsum('bhnk,bhk->bhn', sk, z)[..., None]
                mem = mem + jnp.einsum('bhnk,bhnv->bhkv', sk, v_s - prev_v)
                z = z + sk.sum(axis=2)
                return ((mem, z), out)
            _, outs = jax.lax.scan(step, (mem0, z0), (qs, ks, vs, qnope, knope))
            o = outs.transpose(1, 0, 3, 2, 4).reshape(B, N, INNER)
            out = o @ w_out
            return (out, next_k, next_v)
        return _reference_tuple_inner(x, w_qkv, w_out, ln_g, ln_b, mem_beta)[0]

    def _L0_ffn_ref(x, gate_w, gate_b, w1, b1, w3, b3, w2, b2, sw1, sb1, sw3, sb3, sw2, sb2):
        import jax, jax.numpy as jnp
        import numpy as np
        E = 8
        TOP_K = 2
        ROUTE_SCALE = 1.0
        ALPHA = 1.702
        LIMIT = 7.0
        D = 128
        F = 128
        B, S = (2, 128)

        def swiglu(h):
            g = jnp.minimum(h[..., ::2], LIMIT)
            l = jnp.clip(h[..., 1::2], -LIMIT, LIMIT)
            return g * jax.nn.sigmoid(ALPHA * g) * (l + 1.0)
        if __name__ == '__main__':
            out = reference(**setup_inputs())
            print(out.shape, out.dtype)
        inp_shape = x.shape
        xt = x.reshape(-1, D)
        logits = xt @ gate_w.T
        scores = jax.nn.softmax(logits.astype(jnp.float32), axis=-1)
        biased = scores + gate_b.astype(jnp.float32)
        idx = jax.lax.top_k(biased, TOP_K)[1]
        weights = (jnp.take_along_axis(scores, idx, axis=-1) * ROUTE_SCALE).astype(x.dtype)
        cw = jnp.sum(jax.nn.one_hot(idx, E, dtype=x.dtype) * weights[..., None], axis=1)
        h1 = jnp.einsum('td,efd->etf', xt, w1) + b1[:, None, :]
        h3 = jnp.einsum('td,efd->etf', xt, w3) + b3[:, None, :]
        a = swiglu(h1 * h3)
        y = jnp.einsum('etf,edf->etd', a, w2) + b2[:, None, :]
        routed = jnp.einsum('te,etd->td', cw, y)
        sh = swiglu((xt @ sw1.T + sb1) * (xt @ sw3.T + sb3))
        shared = sh @ sw2.T + sb2
        return (routed + shared).reshape(inp_shape)

    def _L1_attn_ref(x, Wq, bq, Wk, bk, Wv, bv, Wo, bo, Wproj, bproj, W1, b1, W2, b2):
        import jax, jax.numpy as jnp
        import numpy as np
        D_MODEL = 128
        N_HEADS = 8
        RADIUS = 32
        TEMP = 0.5
        ALPHA = 0.5
        KINDNESS_W = 0.3
        ENT_THRESH = 0.15
        GAUGE_THRESH = 0.3
        NEG = -1000000000.0

        def _linear(x, w, b):
            return x @ w.T + b
        B, S, D = x.shape
        H = N_HEADS
        dk = D // H
        invariant = _linear(x, Wproj, bproj)
        residual = x - invariant
        gauge = jnp.mean(jnp.linalg.norm(residual, axis=-1) / (jnp.linalg.norm(x, axis=-1) + 1e-08))
        x_qk = jnp.where(gauge > GAUGE_THRESH, invariant, x)
        Q = _linear(x_qk, Wq, bq).reshape(B, S, H, dk).transpose(0, 2, 1, 3)
        K = _linear(x_qk, Wk, bk).reshape(B, S, H, dk).transpose(0, 2, 1, 3)
        V = _linear(x, Wv, bv).reshape(B, S, H, dk).transpose(0, 2, 1, 3)
        r = max(1, min(RADIUS, max(1, S // 4)))
        qn = Q / jnp.maximum(jnp.linalg.norm(Q, axis=-1, keepdims=True), 1e-12)
        kn = K / jnp.maximum(jnp.linalg.norm(K, axis=-1, keepdims=True), 1e-12)
        sim = jnp.einsum('bhid,bhjd->bhij', qn, kn)
        dist = jnp.sqrt(jnp.clip(2.0 * (1.0 - sim), 0.0, 4.0))
        idx = jnp.arange(S)
        band = jnp.abs(idx[:, None] - idx[None, :]) <= r
        scores = jnp.where(band[None, None], -ALPHA * dist, NEG)
        attn = jax.nn.softmax(scores / TEMP, axis=-1)
        Qs = jax.nn.softmax(Q, axis=-1)
        Ks = jax.nn.softmax(K, axis=-1)
        joint = jnp.einsum('bhid,bhjd->bhij', Qs, Ks)
        H_joint = -jnp.sum(joint * jnp.log(joint + 1e-10), axis=(-2, -1))
        p_q = jax.nn.softmax(Q.sum(axis=-2), axis=-1)
        p_k = jax.nn.softmax(K.sum(axis=-2), axis=-1)
        H_q = -jnp.sum(p_q * jnp.log(p_q + 1e-10), axis=-1)
        H_k = -jnp.sum(p_k * jnp.log(p_k + 1e-10), axis=-1)
        S_ent = (H_joint - H_q - H_k).mean(axis=1)
        gate = (S_ent > ENT_THRESH).astype(attn.dtype)[:, None, None, None]
        attn = attn * gate
        attn = attn / (attn.sum(axis=-1, keepdims=True) + 1e-10)
        out = jnp.einsum('bhij,bhjd->bhid', attn, V)
        out = out.transpose(0, 2, 1, 3).reshape(B, S, D)
        h = jax.nn.relu(_linear(out, W1, b1))
        curv = jax.nn.sigmoid(_linear(h, W2, b2))[..., 0]
        social = curv.mean()
        penalty = jnp.clip(jnp.exp(-social / max(TEMP, 0.001)), 0.5, 1.5)
        out = out * (1.0 - KINDNESS_W * (1.0 - penalty))
        return _linear(out, Wo, bo)

    def _L1_ffn_ref(x, Wr1, br1, Wr2, br2, Ws1, bs1, Ws2, bs2, We1, be1, We2, be2):
        import jax, jax.numpy as jnp
        import numpy as np
        B, T, C = (2, 64, 128)
        I = 512
        E = 8
        K = 2
        Bb, Tt, Cc = x.shape
        xf = x.reshape(-1, Cc)
        logits = jax.nn.relu(xf @ Wr1 + br1) @ Wr2 + br2
        gates = jax.nn.softmax(logits, axis=-1)
        tg, ti = jax.lax.top_k(gates, K)
        tg = jax.nn.softmax(tg / K, axis=-1)
        out = jax.nn.silu(xf @ Ws1 + bs1) @ Ws2 + bs2
        for e in range(E):
            h = jax.nn.silu(xf @ We1[e] + be1[e]) @ We2[e] + be2[e]
            w = jnp.sum(tg * (ti == e), axis=-1)
            out = out + w[:, None] * h
        return out.reshape(Bb, Tt, Cc)
    x = L0_attn_x
    x = x + 0.5 * _L0_ffn_ref(_layernorm(x, axis=-1), L0_ffn_gate_w, L0_ffn_gate_b, L0_ffn_w1, L0_ffn_b1, L0_ffn_w3, L0_ffn_b3, L0_ffn_w2, L0_ffn_b2, L0_ffn_sw1, L0_ffn_sb1, L0_ffn_sw3, L0_ffn_sb3, L0_ffn_sw2, L0_ffn_sb2)
    x = x + _L0_attn_ref(_layernorm(x, axis=-1), L0_attn_w_qkv, L0_attn_w_out, L0_attn_ln_g, L0_attn_ln_b, L0_attn_mem_beta)
    x = x + 0.5 * _L0_ffn_ref(_layernorm(x, axis=-1), L0_ffn_gate_w, L0_ffn_gate_b, L0_ffn_w1, L0_ffn_b1, L0_ffn_w3, L0_ffn_b3, L0_ffn_w2, L0_ffn_b2, L0_ffn_sw1, L0_ffn_sb1, L0_ffn_sw3, L0_ffn_sb3, L0_ffn_sw2, L0_ffn_sb2)
    x = x + 0.5 * _L1_ffn_ref(_layernorm(x, axis=-1), L1_ffn_Wr1, L1_ffn_br1, L1_ffn_Wr2, L1_ffn_br2, L1_ffn_Ws1, L1_ffn_bs1, L1_ffn_Ws2, L1_ffn_bs2, L1_ffn_We1, L1_ffn_be1, L1_ffn_We2, L1_ffn_be2)
    x = x + _L1_attn_ref(_layernorm(x, axis=-1), L1_attn_Wq, L1_attn_bq, L1_attn_Wk, L1_attn_bk, L1_attn_Wv, L1_attn_bv, L1_attn_Wo, L1_attn_bo, L1_attn_Wproj, L1_attn_bproj, L1_attn_W1, L1_attn_b1, L1_attn_W2, L1_attn_b2)
    x = x + 0.5 * _L1_ffn_ref(_layernorm(x, axis=-1), L1_ffn_Wr1, L1_ffn_br1, L1_ffn_Wr2, L1_ffn_br2, L1_ffn_Ws1, L1_ffn_bs1, L1_ffn_Ws2, L1_ffn_bs2, L1_ffn_We1, L1_ffn_be1, L1_ffn_We2, L1_ffn_be2)
    return x

_drawn_inputs = setup_inputs


def setup_inputs(seed=0):
    import zlib

    import numpy as np

    out = dict(_drawn_inputs(seed))
    spreads = {'L0_attn_ln_g': (1.0, 0.6),
     'L0_attn_ln_b': (0.0, 0.545),
     'L0_attn_mem_beta': (0.0, 0.8),
     'L1_attn_bq': (0.0, 0.8),
     'L1_attn_bk': (0.0, 0.8),
     'L1_attn_bv': (0.0, 0.1),
     'L1_attn_bo': (0.0, 0.1),
     'L1_attn_bproj': (0.0, 0.8),
     'L1_attn_b1': (0.0, 0.1),
     'L1_ffn_br1': (0.0, 0.451),
     'L1_ffn_br2': (0.0, 0.1),
     'L1_ffn_bs1': (0.0, 0.54),
     'L1_ffn_bs2': (0.0, 0.1),
     'L1_ffn_be1': (0.0, 0.7),
     'L1_ffn_be2': (0.0, 0.1)}
    factors = {'L0_ffn_b1': 8.0,
     'L0_ffn_b3': 8.0,
     'L0_ffn_b2': 8.0,
     'L0_ffn_sb1': 5.356,
     'L0_ffn_sb3': 5.984,
     'L0_ffn_sb2': 5.779,
     'L1_attn_Wq': 8.0,
     'L1_attn_Wk': 8.0,
     'L1_attn_Wproj': 8.0}
    for name, (base, spread) in spreads.items():
        noise = np.random.default_rng([zlib.crc32(name.encode()), seed]).standard_normal(out[name].shape)
        drawn = base * np.exp(spread * noise) if base else spread * noise
        out[name] = jnp.asarray(drawn.astype(out[name].dtype))
    for name, factor in factors.items():
        out[name] = (out[name] * factor).astype(out[name].dtype)
    return out
```

```python
from collections import namedtuple
from contextlib import ExitStack

import numpy as np
import concourse.bass as bass
from concourse import mybir

F32 = mybir.dt.float32
U32 = mybir.dt.uint32
ALU = mybir.AluOpType
ACT = mybir.ActivationFunctionType
AX = mybir.AxisListType

P = 128
BATCH, SEQ, D = 4, 1024, 128
SEG = 32
TILES = SEQ // SEG
GROUP = 4
TRIPS = TILES // GROUP
BLOCK = GROUP * P
HEADS, DH = 16, 64
PAIRS = HEADS // 2
INNER = HEADS * DH
E = 8
NE = E + 1
LN_EPS = 1e-5


def at(trip, per_trip, n):
    return trip * per_trip + n


def wait(eng, sem, value):
    if not isinstance(value, int) or value > 0:
        eng.wait_ge(sem, value)


def wait_alone(eng, sem, value, passed):
    if not isinstance(value, int) or value > 0:
        eng.wait_ge(sem, value)
        eng.sem_inc(passed, 1)


class Named:
    pass


def make_sems(nc, ctx, prefix, names, lists=""):
    make = lambda n: ctx.enter_context(nc.semaphore(f"{prefix}_{n}"))
    return namedtuple(prefix, (names + " " + lists).split())(*(make(n) for n in names.split()),
                                                             *([make(f"{n}{k}") for k in range(4)] for n in lists.split()))


def stage_sems(nc, ctx, prefix, names):
    s = namedtuple(prefix, names)(*(nc.alloc_semaphore(name=f"{prefix}_{n}") for n in names.split()))

    def give_back():
        nc.clear_and_free_semaphores(list(s))
        nc.all_engine_barrier()

    ctx.callback(give_back)
    return s


def in_trips(eng, one_trip):
    one_trip(0, 0)
    with eng.Fori(0, TRIPS // 2 - 1) as i:
        one_trip(2 * i + 1, 1)
        one_trip(2 * i + 2, 0)
    one_trip(TRIPS - 1, 1)
ORDER = [E] + list(range(E))

ROUTE_SEMS = ("ln_stats ln_mv ln_var ln_rstd xn_ready xnT_ps xnT_ready hid_ps hid_ready logits_ps "
              "passed gate_step shift_ready exp_ready pair_ready pair_exp cw_ready cwT_ps cwT_ready")


def route_buffers(sb, ps, kind):
    r = Named()
    r.stats = sb("ln_stats", [P, GROUP, 6])
    r.mv = sb("ln_mv", [P, GROUP, 2])
    r.var = sb("ln_var", [P, GROUP])
    r.rstd = sb("ln_rstd", [P, GROUP])
    r.xn = sb("xn", [P, GROUP, D])
    r.xnT = [sb(f"xnT{i}", [P, BLOCK]) for i in range(2)]
    r.logits = sb("logits", [P, GROUP, E])
    r.shift = sb("shift", [P, GROUP, E])
    r.expd = sb("expd", [P, GROUP, E])
    r.score = sb("score", [P, GROUP, E])
    r.biased = sb("biased", [P, GROUP, E])
    r.top = sb("top", [P, GROUP, 8])
    r.index = sb("index", [P, GROUP, 8], U32)
    r.indexf = sb("indexf", [P, GROUP, 8])
    r.hot = sb("hot", [P, 2, GROUP, E])
    r.small = sb("small", [P, 8, GROUP])
    r.cw = [sb(f"cw{i}", [P, GROUP, NE]) for i in range(2)]
    r.cwT = [sb(f"cwT{i}", [NE, BLOCK]) for i in range(2)]
    r.hidden = sb("router_hidden", [32, BLOCK]) if kind == 1 else None
    r.ps_x = ps("route_ps_x")
    r.ps_l = ps("route_ps_l")
    return r


GATE_STEPS = {0: 9, 1: 12}


class Route:

    def __init__(self, nc, kind, X, r, s, c, w):
        self.nc, self.kind, self.X, self.r, self.s, self.c, self.w = nc, kind, X, r, s, c, w

    def dve_stats(self, dve, j, n, p):
        nc, X, r, s = self.nc, self.X, self.r, self.s
        for t in range(GROUP):
            last = nc.vector.bn_stats(r.stats[:, t, :], X[:, j * GROUP + t, :])
        last.then_inc(s.ln_stats, 1)
        wait_alone(dve, s.ln_stats, n + 1, s.passed)
        for t in range(GROUP):
            last = nc.vector.bn_aggr(r.mv[:, t, :], r.stats[:, t, :])
        last.then_inc(s.ln_mv, 1)

    def pool_rstd(self, pool, j, n, p):
        nc, r, s = self.nc, self.r, self.s
        pool.wait_ge(s.ln_mv, n + 1)
        nc.gpsimd.tensor_tensor(r.var[:, :], r.mv[:, :, 1], self.c.eps[:, 0:GROUP], ALU.add).then_inc(s.ln_var, 1)
        pool.wait_ge(s.ln_var, n + 1)
        nc.gpsimd.tensor_tensor(r.rstd[:, :], r.var[:, :], self.c.minus_half[:, 0:GROUP], ALU.pow).then_inc(s.ln_rstd, 1)

    def dve_normalise(self, dve, j, n, p):
        nc, X, r, s = self.nc, self.X, self.r, self.s
        dve.wait_ge(s.ln_rstd, n + 1)
        wait(dve, s.xnT_ps, n)
        for t in range(GROUP):
            last = nc.vector.tensor_scalar(r.xn[:, t, :], X[:, j * GROUP + t, :], r.mv[:, t, 0:1], r.rstd[:, t:t + 1],
                                           ALU.subtract, ALU.mult)
        last.then_inc(s.xn_ready, 1)

    def pe_transpose(self, pe, j, n, p):
        nc, r, s = self.nc, self.r, self.s
        pe.wait_ge(s.xn_ready, n + 1)
        wait(pe, s.hid_ready if self.kind else s.xnT_ready, n)
        for t in range(GROUP):
            last = nc.tensor.transpose(r.ps_x[:, t * P:(t + 1) * P], r.xn[:, t, :], self.c.ident[:, :])
        last.then_inc(s.xnT_ps, 1)

    def act_xnT(self, act, j, n, p):
        nc, r, s = self.nc, self.r, self.s
        act.wait_ge(s.xnT_ps, n + 1)
        nc.scalar.copy(r.xnT[p][:, :], r.ps_x[:, :]).then_inc(s.xnT_ready, 1)

    def pe_hidden(self, pe, j, n, p):
        nc, r, s = self.nc, self.r, self.s
        pe.wait_ge(s.xnT_ready, n + 1)
        nc.tensor.matmul(r.ps_x[0:32, :], self.w.router1[:, :], r.xnT[p][:, :], start=True, stop=True).then_inc(s.hid_ps, 1)

    def act_hidden(self, act, j, n, p):
        nc, r, s = self.nc, self.r, self.s
        act.wait_ge(s.hid_ps, n + 1)
        nc.scalar.activation(r.hidden[:, :], r.ps_x[0:32, :], ACT.Relu, bias=self.w.router1_bias[:, :]).then_inc(s.hid_ready, 1)

    def pe_logits(self, pe, j, n, p):
        nc, r, s = self.nc, self.r, self.s
        wait(pe, s.cwT_ready, n)
        if self.kind == 0:
            pe.wait_ge(s.xnT_ready, n + 1)
            lhs, rhs = r.xnT[p], self.w.router
        else:
            pe.wait_ge(s.hid_ready, n + 1)
            lhs, rhs = r.hidden, self.w.router2
        for t in range(GROUP):
            last = nc.tensor.matmul(r.ps_l[:, t * E:(t + 1) * E], lhs[:, t * P:(t + 1) * P], rhs[:, :], start=(t == 0), stop=True,
                                    skip_group_check=True)
        last.then_inc(s.logits_ps, 1)

    def dve_shift(self, dve, j, n, p):
        nc, r, s = self.nc, self.r, self.s
        k = lambda m: at(n, GATE_STEPS[self.kind], m)
        dve.wait_ge(s.logits_ps, n + 1)
        ps = r.ps_l[:, 0:GROUP * E].rearrange("p (t e) -> p t e", e=E)
        if self.kind == 0:
            nc.vector.tensor_copy(r.logits[:, :, :], ps).then_inc(s.gate_step, 1)
        else:
            nc.vector.tensor_tensor(r.logits[:, :, :], ps, self.w.router2_bias[:, :].unsqueeze(1).broadcast_to([P, GROUP, E]),
                                    ALU.add).then_inc(s.gate_step, 1)
        dve.wait_ge(s.gate_step, k(1))
        nc.vector.tensor_reduce(r.small[:, 0, :], r.logits[:, :, :], AX.X, ALU.max).then_inc(s.gate_step, 1)
        dve.wait_ge(s.gate_step, k(2))
        nc.vector.tensor_tensor(r.shift[:, :, :], r.logits[:, :, :], r.small[:, 0, :].unsqueeze(2).broadcast_to([P, GROUP, E]),
                                ALU.subtract).then_inc(s.shift_ready, 1)

    def act_exp(self, act, j, n, p):
        nc, r, s = self.nc, self.r, self.s
        act.wait_ge(s.shift_ready, n + 1)
        nc.scalar.activation(r.expd[:, :, :], r.shift[:, :, :], ACT.Exp).then_inc(s.exp_ready, 1)

    def dve_top2(self, dve, j, n, p):
        nc, r, s = self.nc, self.r, self.s
        k = lambda m: at(n, GATE_STEPS[self.kind], m)
        dve.wait_ge(s.exp_ready, n + 1)
        nc.vector.tensor_reduce(r.small[:, 1, :], r.expd[:, :, :], AX.X, ALU.add).then_inc(s.gate_step, 1)
        dve.wait_ge(s.gate_step, k(3))
        nc.vector.reciprocal(r.small[:, 2, :], r.small[:, 1, :]).then_inc(s.gate_step, 1)
        dve.wait_ge(s.gate_step, k(4))
        nc.vector.tensor_tensor(r.score[:, :, :], r.expd[:, :, :], r.small[:, 2, :].unsqueeze(2).broadcast_to([P, GROUP, E]),
                                ALU.mult).then_inc(s.gate_step, 1)
        ranked = r.score
        if self.kind == 0:
            dve.wait_ge(s.gate_step, k(5))
            ranked = r.biased
            nc.vector.tensor_tensor(r.biased[:, :, :], r.score[:, :, :], self.w.router_bias[:, :].unsqueeze(1).broadcast_to([P, GROUP, E]),
                                    ALU.add).then_inc(s.gate_step, 1)
        done = 6 if self.kind == 0 else 5
        wait_alone(dve, s.gate_step, k(done), s.passed)
        for t in range(GROUP):
            last = nc.vector.max(r.top[:, t, :], ranked[:, t, :])
        last.then_inc(s.gate_step, 1)
        wait_alone(dve, s.gate_step, k(done + 1), s.passed)
        for t in range(GROUP):
            last = nc.vector.max_index(r.index[:, t, :], r.top[:, t, :], ranked[:, t, :])
        last.then_inc(s.gate_step, 1)
        if self.kind == 1:
            nc.vector.tensor_tensor(r.small[:, 3, :], r.top[:, :, 1], r.top[:, :, 0], ALU.subtract).then_inc(s.pair_ready, 1)
        dve.wait_ge(s.gate_step, k(done + 2))
        nc.vector.tensor_copy(r.indexf[:, :, :], r.index[:, :, :]).then_inc(s.gate_step, 1)
        dve.wait_ge(s.gate_step, k(done + 3))
        for m in range(2):
            last = nc.vector.tensor_tensor(r.hot[:, m, :, :], self.c.iota[:, :].unsqueeze(1).broadcast_to([P, GROUP, E]),
                                           r.indexf[:, :, m].unsqueeze(2).broadcast_to([P, GROUP, E]), ALU.is_equal)
        if self.kind == 1:
            last.then_inc(s.gate_step, 1)
            return
        last.then_inc(s.pair_ready, 1)
        dve.wait_ge(s.pair_ready, n + 1)
        nc.vector.tensor_tensor(r.hot[:, 0, :, :], r.hot[:, 0, :, :], r.hot[:, 1, :, :], ALU.add).then_inc(s.pair_exp, 1)
        dve.wait_ge(s.pair_exp, n + 1)
        nc.vector.tensor_tensor(r.cw[p][:, :, 0:E], r.score[:, :, :], r.hot[:, 0, :, :], ALU.mult).then_inc(s.cw_ready, 1)

    def act_pair(self, act, j, n, p):
        nc, r, s = self.nc, self.r, self.s
        act.wait_ge(s.pair_ready, n + 1)
        nc.scalar.activation(r.small[:, 4, :], r.small[:, 3, :], ACT.Exp, scale=0.5).then_inc(s.pair_exp, 1)

    def dve_pair(self, dve, j, n, p):
        nc, r, s = self.nc, self.r, self.s
        k = lambda m: at(n, GATE_STEPS[1], m)
        dve.wait_ge(s.pair_exp, n + 1)
        nc.vector.tensor_scalar(r.small[:, 5, :], r.small[:, 4, :], 1.0, None, ALU.add).then_inc(s.gate_step, 1)
        dve.wait_ge(s.gate_step, k(10))
        nc.vector.reciprocal(r.small[:, 6, :], r.small[:, 5, :]).then_inc(s.gate_step, 1)
        dve.wait_ge(s.gate_step, k(11))
        nc.vector.tensor_tensor(r.small[:, 7, :], r.small[:, 6, :], r.small[:, 4, :], ALU.mult).then_inc(s.gate_step, 1)
        nc.vector.tensor_tensor(r.biased[:, :, :], r.hot[:, 0, :, :], r.small[:, 6, :].unsqueeze(2).broadcast_to([P, GROUP, E]),
                                ALU.mult)
        dve.wait_ge(s.gate_step, k(12))
        nc.vector.tensor_tensor(r.shift[:, :, :], r.hot[:, 1, :, :], r.small[:, 7, :].unsqueeze(2).broadcast_to([P, GROUP, E]),
                                ALU.mult).then_inc(s.pair_mult, 1)
        dve.wait_ge(s.pair_mult, n + 1)
        nc.vector.tensor_tensor(r.cw[p][:, :, 0:E], r.biased[:, :, :], r.shift[:, :, :], ALU.add).then_inc(s.cw_ready, 1)

    def pe_cwT(self, pe, j, n, p):
        nc, r, s = self.nc, self.r, self.s
        pe.wait_ge(s.cw_ready, n + 1)
        for t in range(GROUP):
            last = nc.tensor.transpose(r.ps_l[0:NE, t * P:(t + 1) * P], r.cw[p][:, t, :], self.c.ident[:, :])
        last.then_inc(s.cwT_ps, 1)

    def act_cwT(self, act, j, n, p):
        nc, r, s = self.nc, self.r, self.s
        act.wait_ge(s.cwT_ps, n + 1)
        nc.scalar.copy(r.cwT[p][:, :], r.ps_l[0:NE, :]).then_inc(s.cwT_ready, 1)


def expert_sum(nc, dve, s, r, buf, X, j, n, p, e):
    step = at(n, NE, e)
    b = (p + e) % 2
    dve.wait_ge(s.y_full, step + 1)
    wait(dve, s.y_done, step)
    if e == 0:
        wait(dve, s.x_done, n)
        last = nc.vector.tensor_copy(buf.acc[:, :, :], buf.ps_y[b][:, :].rearrange("p (t d) -> p t d", d=D))
    else:
        for t in range(GROUP):
            last = nc.vector.scalar_tensor_tensor(out=buf.acc[:, t, :], in0=buf.ps_y[b][:, t * D:(t + 1) * D],
                                                  scalar=r.cw[p][:, t, ORDER[e]:ORDER[e] + 1], in1=buf.acc[:, t, :],
                                                  op0=ALU.mult, op1=ALU.add)
    last.then_inc(s.y_done, 1)
    if e == NE - 1:
        dve.wait_ge(s.y_done, step + 1)
        x = X[:, bass.ds(j * GROUP, GROUP), :]
        nc.vector.scalar_tensor_tensor(out=x, in0=buf.acc[:, :, :], scalar=0.5, in1=x,
                                       op0=ALU.mult, op1=ALU.add).then_inc(s.x_done, 1)


def gated_stage(nc, K, call, io):
    F = 128
    X, c, w, s, base = K.X, K.c, K.w0, K.s0, call * TRIPS
    with ExitStack() as ctx:
        sb = lambda name, shape, dt=F32: ctx.enter_context(nc.sbuf_tensor(f"g{call}_{name}", shape, dt))
        ps = lambda name: ctx.enter_context(nc.psum_tensor(f"g{call}_{name}", [P, 512], F32))
        r = route_buffers(sb, ps, 0)
        buf = Named()
        h_full = {"g1": s.full_g1, "g3": s.full_g3, "l1": s.full_l1, "l3": s.full_l3}
        buf.ps_h = {h: ps(f"ps_{h}") for h in ("g1", "g3", "l1", "l3")}
        buf.ps_y = [ps(f"ps_y{i}") for i in range(2)]
        buf.t3 = {h: sb(f"t3{h}", [P, BLOCK]) for h in "gl"}
        buf.prod_g = sb("prod_g", [P, BLOCK])
        buf.prod_l = [sb(f"prod_l{i}", [P, BLOCK]) for i in range(2)]
        buf.g = [sb(f"g{i}", [P, BLOCK]) for i in range(2)]
        buf.l = [sb(f"l{i}", [P, BLOCK]) for i in range(2)]
        buf.sig = [sb(f"sig{i}", [P, BLOCK]) for i in range(2)]
        buf.gl = sb("gl", [P, BLOCK])
        buf.a = [sb(f"a{i}", [P, BLOCK]) for i in range(2)]
        buf.acc = sb("acc", [P, GROUP, D])
        route = Route(nc, 0, X, r, s, c, w)
        block = ctx.enter_context(nc.Block())

        def before(j, p, e):
            return (j, p, e - 1) if e else (j - 1, 1 - p, NE - 1)

        @block.tensor
        def _(pe):
            def outputs(j, p, e):
                n = base + j
                step = at(n, NE, e)
                b = (p + e) % 2
                pe.wait_ge(s.a_ready, step + 1)
                wait(pe, s.y_done, step - 1)
                for t in range(GROUP):
                    last = nc.tensor.matmul(buf.ps_y[b][:, t * D:(t + 1) * D], buf.a[b][:, t * P:(t + 1) * P], w.w2T[:, ORDER[e], :],
                                            start=(t == 0), stop=(e > 0), skip_group_check=True)
                if e == 0:
                    pe.wait_ge(s.cwT_ready, n + 1)
                    for t in range(GROUP):
                        last = nc.tensor.matmul(buf.ps_y[b][:, t * D:(t + 1) * D], r.cwT[p][:, t * P:(t + 1) * P], w.b2[:, :],
                                                start=False, stop=True, skip_group_check=True)
                last.then_inc(s.y_full, 1)

            def trip(j, p):
                n = base + j
                more = not (isinstance(j, int) and j == TRIPS - 1)
                pe.wait_ge(s.xnT_ready, n + 1)
                for e in range(NE):
                    step = at(n, NE, e)
                    for h, mat, part, freed in (("g3", 1, 0, s.t3g_ready), ("g1", 0, 0, s.pg_ready),
                                                ("l3", 1, 1, s.t3l_ready), ("l1", 0, 1, s.pl_ready)):
                        wait(pe, freed, step)
                        nc.tensor.matmul(buf.ps_h[h][:, :], w.w13T[:, mat, ORDER[e], part, :], r.xnT[p][:, :],
                                         start=True, stop=True).then_inc(h_full[h], 1)
                    if not (isinstance(j, int) and j == 0 and e == 0):
                        outputs(*before(j, p, e))
                    if more and e == 3:
                        route.pe_transpose(pe, j + 1, n + 1, 1 - p)
                    if more and e == 4:
                        route.pe_logits(pe, j + 1, n + 1, 1 - p)
                    if more and e == 7:
                        route.pe_cwT(pe, j + 1, n + 1, 1 - p)

            route.pe_transpose(pe, 0, base, 0)
            route.pe_logits(pe, 0, base, 0)
            route.pe_cwT(pe, 0, base, 0)
            in_trips(pe, trip)
            outputs(TRIPS - 1, 1, NE - 1)

        if call == 1:
            @block.sync
            def _(sp):
                load_silu_weights(nc, sp, io, K.w1, K.s1.loaded)

        @block.scalar
        def _(act):
            def trip(j, p):
                n = base + j
                more = not (isinstance(j, int) and j == TRIPS - 1)
                for e in range(NE):
                    step = at(n, NE, e)
                    b = (p + e) % 2
                    x = ORDER[e]
                    act.wait_ge(s.full_g3, step + 1)
                    wait(act, s.pg_ready, step)
                    nc.scalar.activation(buf.t3["g"][:, :], buf.ps_h["g3"][:, :], ACT.Identity, bias=w.b3[:, x, 0:1]).then_inc(s.t3g_ready, 1)
                    act.wait_ge(s.full_l3, step + 1)
                    wait(act, s.pl_ready, step)
                    nc.scalar.activation(buf.t3["l"][:, :], buf.ps_h["l3"][:, :], ACT.Identity, bias=w.b3[:, x, 1:2]).then_inc(s.t3l_ready, 1)
                    act.wait_ge(s.g_ready, step + 1)
                    wait(act, s.a_ready, step - 1)
                    nc.scalar.activation(buf.sig[b][:, :], buf.g[b][:, :], ACT.Sigmoid, scale=1.702).then_inc(s.sig_ready, 1)
                    if more and e == 3:
                        route.act_xnT(act, j + 1, n + 1, 1 - p)
                    if more and e == 5:
                        route.act_exp(act, j + 1, n + 1, 1 - p)
                    if more and e == 7:
                        route.act_cwT(act, j + 1, n + 1, 1 - p)

            route.act_xnT(act, 0, base, 0)
            route.act_exp(act, 0, base, 0)
            route.act_cwT(act, 0, base, 0)
            in_trips(act, trip)

        @block.gpsimd
        def _(pool):
            def trip(j, p):
                n = base + j
                more = not (isinstance(j, int) and j == TRIPS - 1)
                for e in range(NE):
                    step = at(n, NE, e)
                    b = (p + e) % 2
                    wait(pool, s.gl_ready, step - 1)
                    wait_alone(pool, s.pl_ready, step + 1, s.passed)
                    nc.gpsimd.tensor_scalar(buf.l[b][:, :], buf.prod_l[b][:, :], 7.0, -7.0, ALU.min, ALU.max).then_inc(s.l_ready, 1)
                    if more and e == 1:
                        route.pool_rstd(pool, j + 1, n + 1, 1 - p)

            route.pool_rstd(pool, 0, base, 0)
            in_trips(pool, trip)

        @block.vector
        def _(dve):
            def activate(j, p, e):
                step = at(base + j, NE, e)
                b = (p + e) % 2
                dve.wait_ge(s.l_ready, step + 1)
                dve.wait_ge(s.g_ready, step + 1)
                wait(dve, s.a_ready, step)
                nc.vector.scalar_tensor_tensor(out=buf.gl[:, :], in0=buf.l[b][:, :], scalar=1.0, in1=buf.g[b][:, :],
                                               op0=ALU.add, op1=ALU.mult).then_inc(s.gl_ready, 1)
                dve.wait_ge(s.sig_ready, step + 1)
                dve.wait_ge(s.gl_ready, step + 1)
                wait(dve, s.y_full, step - 1)
                nc.vector.tensor_tensor(buf.a[b][:, :], buf.gl[:, :], buf.sig[b][:, :], ALU.mult).then_inc(s.a_ready, 1)

            def trip(j, p):
                n = base + j
                more = not (isinstance(j, int) and j == TRIPS - 1)
                first = isinstance(j, int) and j == 0
                for e in range(NE):
                    step = at(n, NE, e)
                    b = (p + e) % 2
                    x = ORDER[e]
                    dve.wait_ge(s.t3g_ready, step + 1)
                    dve.wait_ge(s.full_g1, step + 1)
                    nc.vector.scalar_tensor_tensor(out=buf.prod_g[:, :], in0=buf.ps_h["g1"][:, :], scalar=w.b1[:, x, 0:1],
                                                   in1=buf.t3["g"][:, :], op0=ALU.add, op1=ALU.mult).then_inc(s.pg_ready, 1)
                    dve.wait_ge(s.t3l_ready, step + 1)
                    dve.wait_ge(s.full_l1, step + 1)
                    nc.vector.scalar_tensor_tensor(out=buf.prod_l[b][:, :], in0=buf.ps_h["l1"][:, :], scalar=w.b1[:, x, 1:2],
                                                   in1=buf.t3["l"][:, :], op0=ALU.add, op1=ALU.mult).then_inc(s.pl_ready, 1)
                    dve.wait_ge(s.pg_ready, step + 1)
                    wait(dve, s.sig_ready, step - 1)
                    nc.vector.tensor_scalar(buf.g[b][:, :], buf.prod_g[:, :], 7.0, None, ALU.min).then_inc(s.g_ready, 1)
                    if not (first and e == 0):
                        activate(*before(j, p, e))
                    if not (first and e <= 1):
                        jj, pp, ee = before(*before(j, p, e))
                        expert_sum(nc, dve, s, r, buf, X, jj, base + jj, pp, ee)
                    if more and e == 1:
                        route.dve_stats(dve, j + 1, n + 1, 1 - p)
                    if more and e == 2:
                        route.dve_normalise(dve, j + 1, n + 1, 1 - p)
                    if more and e == 5:
                        route.dve_shift(dve, j + 1, n + 1, 1 - p)
                    if more and e == 6:
                        route.dve_top2(dve, j + 1, n + 1, 1 - p)

            nc.vector.memset(r.cw[0][:, :, E:NE], 1.0)
            nc.vector.memset(r.cw[1][:, :, E:NE], 1.0)
            route.dve_stats(dve, 0, base, 0)
            route.dve_normalise(dve, 0, base, 0)
            route.dve_shift(dve, 0, base, 0)
            route.dve_top2(dve, 0, base, 0)
            in_trips(dve, trip)
            last = (TRIPS - 1, 1, NE - 1)
            activate(*last)
            for jj, pp, ee in (before(*last), last):
                expert_sum(nc, dve, s, r, buf, X, jj, base + jj, pp, ee)


def silu_stage(nc, K, call):
    CH = 4
    X, c, w, s, base = K.X, K.c, K.w1, K.s1, call * TRIPS
    with ExitStack() as ctx:
        sb = lambda name, shape, dt=F32: ctx.enter_context(nc.sbuf_tensor(f"s{call}_{name}", shape, dt))
        ps = lambda name: ctx.enter_context(nc.psum_tensor(f"s{call}_{name}", [P, 512], F32))
        r = route_buffers(sb, ps, 1)
        buf = Named()
        buf.ps_h = [ps(f"ps_h{k}") for k in range(CH)]
        buf.ps_y = [ps(f"ps_y{i}") for i in range(2)]
        buf.a = [sb(f"a{i}", [P, CH, BLOCK]) for i in range(2)]
        buf.acc = sb("acc", [P, GROUP, D])
        route = Route(nc, 1, X, r, s, c, w)
        block = ctx.enter_context(nc.Block())

        def before(j, p, e):
            return (j, p, e - 1) if e else (j - 1, 1 - p, NE - 1)

        @block.tensor
        def _(pe):
            def outputs(j, p, e):
                n = base + j
                step = at(n, NE, e)
                b = (p + e) % 2
                wait(pe, s.y_done, step - 1)
                for k in range(CH):
                    pe.wait_ge(s.a_ready[k], step + 1)
                    for t in range(GROUP):
                        last = nc.tensor.matmul(buf.ps_y[b][:, t * D:(t + 1) * D], buf.a[b][:, k, t * P:(t + 1) * P],
                                                w.we2[:, ORDER[e], k, :], start=(k == 0 and t == 0),
                                                stop=(e > 0 and k == CH - 1), skip_group_check=True)
                if e == 0:
                    pe.wait_ge(s.cwT_ready, n + 1)
                    for t in range(GROUP):
                        last = nc.tensor.matmul(buf.ps_y[b][:, t * D:(t + 1) * D], r.cwT[p][:, t * P:(t + 1) * P], w.be2[:, :],
                                                start=False, stop=True, skip_group_check=True)
                last.then_inc(s.y_full, 1)

            def trip(j, p):
                n = base + j
                more = not (isinstance(j, int) and j == TRIPS - 1)
                pe.wait_ge(s.xnT_ready, n + 1)
                for e in range(NE):
                    step = at(n, NE, e)
                    for k in range(CH):
                        wait(pe, s.a_ready[k], step)
                        nc.tensor.matmul(buf.ps_h[k][:, :], w.we1[:, ORDER[e], k * P:(k + 1) * P], r.xnT[p][:, :],
                                         start=True, stop=True).then_inc(s.h_full[k], 1)
                    if not (isinstance(j, int) and j == 0 and e == 0):
                        outputs(*before(j, p, e))
                    if more and e == 2:
                        route.pe_transpose(pe, j + 1, n + 1, 1 - p)
                    if more and e == 3:
                        route.pe_hidden(pe, j + 1, n + 1, 1 - p)
                    if more and e == 4:
                        route.pe_logits(pe, j + 1, n + 1, 1 - p)
                    if more and e == 8:
                        route.pe_cwT(pe, j + 1, n + 1, 1 - p)

            route.pe_transpose(pe, 0, base, 0)
            route.pe_hidden(pe, 0, base, 0)
            route.pe_logits(pe, 0, base, 0)
            route.pe_cwT(pe, 0, base, 0)
            in_trips(pe, trip)
            outputs(TRIPS - 1, 1, NE - 1)

        @block.scalar
        def _(act):
            def trip(j, p):
                n = base + j
                more = not (isinstance(j, int) and j == TRIPS - 1)
                for e in range(NE):
                    step = at(n, NE, e)
                    b = (p + e) % 2
                    wait(act, s.y_full, step - 1)
                    for k in range(CH):
                        act.wait_ge(s.h_full[k], step + 1)
                        nc.scalar.activation(buf.a[b][:, k, :], buf.ps_h[k][:, :], ACT.Silu,
                                             bias=w.be1[:, ORDER[e], k:k + 1]).then_inc(s.a_ready[k], 1)
                    if more and e == 2:
                        route.act_xnT(act, j + 1, n + 1, 1 - p)
                    if more and e == 3:
                        route.act_hidden(act, j + 1, n + 1, 1 - p)
                    if more and e == 5:
                        route.act_exp(act, j + 1, n + 1, 1 - p)
                        route.act_pair(act, j + 1, n + 1, 1 - p)
                    if more and e == 8:
                        route.act_cwT(act, j + 1, n + 1, 1 - p)

            route.act_xnT(act, 0, base, 0)
            route.act_hidden(act, 0, base, 0)
            route.act_exp(act, 0, base, 0)
            route.act_pair(act, 0, base, 0)
            route.act_cwT(act, 0, base, 0)
            in_trips(act, trip)

        @block.gpsimd
        def _(pool):
            for j in range(1):
                route.pool_rstd(pool, 0, base, 0)
            with pool.Fori(1, TRIPS) as j:
                route.pool_rstd(pool, j, base + j, None)

        @block.vector
        def _(dve):
            def trip(j, p):
                n = base + j
                more = not (isinstance(j, int) and j == TRIPS - 1)
                for e in range(NE):
                    if not (isinstance(j, int) and j == 0 and e == 0):
                        jj, pp, ee = before(j, p, e)
                        expert_sum(nc, dve, s, r, buf, X, jj, base + jj, pp, ee)
                    if more and e == 0:
                        route.dve_stats(dve, j + 1, n + 1, 1 - p)
                    if more and e == 1:
                        route.dve_normalise(dve, j + 1, n + 1, 1 - p)
                    if more and e == 4:
                        route.dve_shift(dve, j + 1, n + 1, 1 - p)
                        route.dve_top2(dve, j + 1, n + 1, 1 - p)
                        route.dve_pair(dve, j + 1, n + 1, 1 - p)

            nc.vector.memset(r.cw[0][:, :, E:NE], 1.0)
            nc.vector.memset(r.cw[1][:, :, E:NE], 1.0)
            route.dve_stats(dve, 0, base, 0)
            route.dve_normalise(dve, 0, base, 0)
            route.dve_shift(dve, 0, base, 0)
            route.dve_top2(dve, 0, base, 0)
            route.dve_pair(dve, 0, base, 0)
            in_trips(dve, trip)
            expert_sum(nc, dve, s, r, buf, X, TRIPS - 1, base + TRIPS - 1, 1, NE - 1)
FILLS, EMPTIED, BACKS = 15, 9, 8
SOFT_STEPS = 4


def in_tile_pairs(eng, one_tile):
    one_tile(0, 0)
    one_tile(1, 1)
    with eng.Fori(1, TILES // 2 - 1) as i:
        one_tile(2 * i, 0)
        one_tile(2 * i + 1, 1)
    one_tile(TILES - 2, 0)
    one_tile(TILES - 1, 1)


def memory_attention_stage(nc, K, io):
    X, c = K.X, K.c
    SCALE = DH ** -0.5
    AUG = DH + 1
    with ExitStack() as ctx:
        sb = lambda name, shape, dt=F32: ctx.enter_context(nc.sbuf_tensor(f"m_{name}", shape, dt))
        w_qkv = sb("w_qkv", [P, 3 * INNER])
        w_rot = sb("w_rot", [P, 2 * INNER])
        w_out = sb("w_out", [P, PAIRS, D])
        ln_g, ln_b = sb("ln_g", [P, 1]), sb("ln_b", [P, 1])
        beta_in, beta, one_less_beta = (sb(n, [P, HEADS]) for n in ("beta_in", "beta", "one_less_beta"))
        cos, sin = sb("cos", [P, P]), sb("sin", [P, P])
        causal = sb("causal", [P, SEG])
        mem = sb("mem", [P, BATCH, PAIRS, AUG])
        stats, mv = sb("stats", [P, 2, 6]), sb("mv", [P, 2, 2])
        var, rstd = sb("var", [P, 2]), sb("rstd", [P, 2])
        xn1, xn2 = sb("xn1", [P, D]), sb("xn2", [P, D])
        xnT = sb("xnT", [P, P])
        raw = [sb(f"raw_{n}", [P, PAIRS, P]) for n in "qk"]
        turned = [sb(f"turned_{n}", [P, PAIRS, P]) for n in "qk"]
        roped = [sb(f"roped_{n}", [P, PAIRS, P]) for n in "qk"]
        relu = [sb(f"relu{i}", [P, INNER]) for i in range(2)]
        expo = [sb(f"expo{i}", [P, INNER]) for i in range(2)]
        phi_qT = [sb(f"phi_qT{i}", [P, PAIRS, P]) for i in range(2)]
        phi_kT = [sb(f"phi_kT{i}", [P, PAIRS, P]) for i in range(2)]
        phi_k = [sb(f"phi_k{i}", [P, INNER]) for i in range(2)]
        v = [sb(f"v{i}", [P, INNER]) for i in range(2)]
        local = [sb(f"local{i}", [P, INNER]) for i in range(2)]
        s_sb, e_sb, eT = (sb(n, [P, HEADS, SEG]) for n in ("scores", "exps", "expsT"))
        smax, ssum, srec = (sb(n, [P, HEADS]) for n in ("smax", "ssum", "srec"))
        u = sb("u", [P, HEADS, AUG])
        rden = sb("rden", [P, 4, 2, 4])
        held = sb("held", [P, 2, 2, 4, DH])
        o, o_sum = sb("o", [P, INNER]), sb("o_sum", [P, INNER])
        oT = sb("oT", [P, PAIRS, P])
        front_ps = [ctx.enter_context(nc.psum_tensor(f"m_front{i}", [P, 512], F32)) for i in range(4)]
        back_ps = ctx.enter_context(nc.psum_tensor("m_back", [P, 4, 512], F32))
        s = stage_sems(nc, ctx, "m", "loaded set_up passed ln_stats ln_mv ln_var ln_rstd xn1_ready xn2_ready ps_full act_emptied rot_done cos_done "
                                    "rope_done elu_ready phi_ready scores_read soft_step soft_shift soft_exp pT_ready local_ready "
                                    "back_full back_step u_ready o_ready o_sum_ready mem_done oT_ready x_done")
        block = ctx.enter_context(nc.Block())
        halves = lambda ap: ap.rearrange("p (c r) d -> p r c d", r=2)
        LOADS = 9

        @block.sync
        def _(sp):
            with nc.allow_non_contiguous_dma(reason="one element per partition"):
                for dst, src in ((w_qkv[:, :], io["L0_attn_w_qkv"]), (w_out[:, :, :], io["L0_attn_w_out"].rearrange("(c p) d -> p c d", p=P)),
                                 (ln_g[:, :], io["L0_attn_ln_g"].unsqueeze(1)), (ln_b[:, :], io["L0_attn_ln_b"].unsqueeze(1)),
                                 (beta_in[:, :], io["L0_attn_mem_beta"].rearrange("a h b c -> (a h b c)").partition_broadcast(P)),
                                 (cos[:, :], io["c_cos"]), (sin[:, :], io["c_sin"]), (causal[:, :], io["c_causal"])):
                    sp.dma_start(dst, src).then_inc(s.loaded, 16)
            sp.wait_ge(s.loaded, 16 * (LOADS - 1))

        @block.tensor
        def _(pe):
            def fill(f, bank, weights, column):
                for k in range(4):
                    last = nc.tensor.matmul(front_ps[bank][:, k * P:(k + 1) * P], weights[:, column + k * P:column + (k + 1) * P], xnT[:, :],
                                            start=(k == 0), stop=True, skip_group_check=True)
                last.then_inc(s.ps_full, 1)

            def fill_tokens(f, bank, column):
                nc.tensor.matmul(front_ps[bank][:, :], xnT[:, :], w_qkv[:, column:column + 512], start=True, stop=True).then_inc(s.ps_full, 1)

            def front_a(f):
                pe.wait_ge(s.xn2_ready, f + 1)
                wait(pe, s.local_ready, f)
                nc.tensor.transpose(front_ps[0][:, 0:P], xn2[:, :], c.ident[:, :]).then_inc(s.ps_full, 1)
                pe.wait_ge(s.act_emptied, at(f, EMPTIED, 1))
                wait(pe, s.scores_read, f)
                fill(f, 1, w_qkv, 0)
                fill(f, 2, w_rot, 0)
                fill(f, 3, w_qkv, 512)
                fill(f, 0, w_rot, 512)

            def front_b(f, half):
                pe.wait_ge(s.act_emptied, at(f, EMPTIED, 2 + half))
                fill(f, (1, 3)[half], w_qkv, INNER + 512 * half)

            def front_c(f, p):
                for half, bank in ((0, 2), (1, 0)):
                    pe.wait_ge(s.rot_done, at(f, 4, 1 + half))
                    fill(f, bank, w_rot, INNER + 512 * half)
                pe.wait_ge(s.act_emptied, at(f, EMPTIED, 4))
                fill_tokens(f, 1, INNER)
                pe.wait_ge(s.rot_done, at(f, 4, 3))
                fill_tokens(f, 2, INNER + 512)
                pe.wait_ge(s.act_emptied, at(f, EMPTIED, 5))
                fill_tokens(f, 3, 2 * INNER)
                pe.wait_ge(s.rot_done, at(f, 4, 4))
                fill_tokens(f, 0, 2 * INNER + 512)
                pe.wait_ge(s.act_emptied, at(f, EMPTIED, 7))
                wait_alone(pe, s.rope_done, at(f, 2, 2), s.passed)
                for h in range(HEADS):
                    rows = slice(DH * (h % 2), DH * (h % 2 + 1))
                    for b in range(BATCH):
                        seg = slice(SEG * b, SEG * (b + 1))
                        last = nc.tensor.matmul(front_ps[1 + h % 2][seg, (h // 2) * SEG:(h // 2 + 1) * SEG], roped[0][rows, h // 2, seg],
                                                roped[1][rows, h // 2, seg], start=True, stop=True, skip_group_check=True)
                last.then_inc(s.ps_full, 1)

            def front_d(f, p):
                pe.wait_ge(s.act_emptied, at(f, EMPTIED, 9))
                wait_alone(pe, s.pT_ready, f + 1, s.passed)
                for h in range(HEADS):
                    for b in range(BATCH):
                        seg = slice(SEG * b, SEG * (b + 1))
                        last = nc.tensor.matmul(front_ps[(3, 0)[h // 8]][seg, (h % 8) * DH:(h % 8 + 1) * DH], eT[seg, h, :],
                                                v[p][seg, h * DH:(h + 1) * DH], start=True, stop=True, skip_group_check=True)
                last.then_inc(s.ps_full, 1)

            def recall(phiT, half):
                for k in range(4):
                    for r in range(2):
                        rows = slice(DH * r, DH * (r + 1))
                        for b in range(BATCH):
                            seg = slice(SEG * b, SEG * (b + 1))
                            last = nc.tensor.matmul(back_ps[seg, 2 * half + r, k * AUG:(k + 1) * AUG], phiT[rows, 4 * half + k, seg],
                                                    mem[rows, b, 4 * half + k, :], start=True, stop=True, skip_group_check=True)
                last.then_inc(s.back_full, 1)

            def back_a(w, p):
                wait(pe, s.mem_done, 2 * w)
                wait(pe, s.x_done, w)
                wait_alone(pe, s.phi_ready, at(w, 3, 3), s.passed)
                recall(phi_kT[p], 0)
                recall(phi_kT[p], 1)

            def back_b(w, p):
                for half in range(2):
                    wait_alone(pe, s.u_ready, at(w, 2, half + 1), s.passed)
                    recall(phi_qT[p], half)

            def back_c(w, p, half):
                if half == 0:
                    wait_alone(pe, s.o_ready, at(w, 2, 2), s.passed)
                else:
                    wait_alone(pe, s.mem_done, at(w, 2, 1), s.passed)
                for k in range(4):
                    for r in range(2):
                        h = 2 * (4 * half + k) + r
                        for b in range(BATCH):
                            seg = slice(SEG * b, SEG * (b + 1))
                            last = nc.tensor.matmul(back_ps[DH * r:DH * (r + 1), b, k * AUG:(k + 1) * AUG], phi_k[p][seg, h * DH:(h + 1) * DH],
                                                    u[seg, h, :], start=True, stop=True, skip_group_check=True)
                last.then_inc(s.back_full, 1)

            def back_d(w):
                wait(pe, s.mem_done, at(w, 2, 2))
                pe.wait_ge(s.o_sum_ready, w + 1)
                for k in range(PAIRS):
                    last = nc.tensor.transpose(back_ps[:, k // 4, (k % 4) * P:(k % 4 + 1) * P], o_sum[:, k * P:(k + 1) * P], c.ident[:, :])
                last.then_inc(s.back_full, 1)
                pe.wait_ge(s.oT_ready, w + 1)
                for k in range(PAIRS):
                    last = nc.tensor.matmul(back_ps[:, 2, 0:D], oT[:, k, :], w_out[:, k, :], start=(k == 0), stop=(k == PAIRS - 1))
                last.then_inc(s.back_full, 1)

            def tile(w, p):
                more = not (isinstance(w, int) and w == TILES - 1)
                back_a(w, p)
                if more:
                    front_a(w + 1)
                back_b(w, p)
                if more:
                    front_b(w + 1, 0)
                back_c(w, p, 0)
                if more:
                    front_b(w + 1, 1)
                back_c(w, p, 1)
                if more:
                    front_c(w + 1, 1 - p)
                back_d(w)
                if more:
                    front_d(w + 1, 1 - p)

            pe.wait_ge(s.set_up, 4)
            front_a(0)
            front_b(0, 0)
            front_b(0, 1)
            front_c(0, 0)
            front_d(0, 0)
            in_tile_pairs(pe, tile)

        @block.scalar
        def _(act):
            def elu_parts(f, k, b, source):
                wait(act, s.phi_ready, at(f, 3, -k))
                nc.scalar.activation(relu[b][:, :], source, ACT.Relu)
                nc.scalar.activation(expo[b][:, :], source, ACT.Exp).then_inc(s.elu_ready, 1)

            def front(f, p):
                act.wait_ge(s.ps_full, at(f, FILLS, 1))
                nc.scalar.activation(xnT[:, :], front_ps[0][:, 0:P], ACT.Identity, bias=ln_b[:, :], scale=ln_g[:, :]).then_inc(s.act_emptied, 1)
                for k, fills in ((0, ((1, 2), (3, 4))), (1, ((1, 6), (3, 7)))):
                    wait(act, s.cos_done, at(f, 2, k) - 1)
                    for half, (bank, number) in enumerate(fills):
                        act.wait_ge(s.ps_full, at(f, FILLS, number))
                        nc.scalar.copy(raw[k][:, 4 * half:4 * half + 4, :], front_ps[bank][:, :].rearrange("p (k t) -> p k t", t=P)).then_inc(s.act_emptied, 1)
                    act.wait_ge(s.act_emptied, at(f, EMPTIED, 3 + 2 * k))
                    elu_parts(f, k, k, raw[k][:, :, :].rearrange("p k t -> p (k t)"))
                wait(act, s.phi_ready, at(f, 3, 1))
                for half, bank in ((0, 1), (1, 2)):
                    act.wait_ge(s.ps_full, at(f, FILLS, 10 + half))
                    cols = slice(512 * half, 512 * half + 512)
                    nc.scalar.activation(relu[0][:, cols], front_ps[bank][:, :], ACT.Relu)
                    nc.scalar.activation(expo[0][:, cols], front_ps[bank][:, :], ACT.Exp).then_inc(s.act_emptied, 1)
                wait(act, s.back_full, at(f, BACKS, -10))
                for half, bank in ((0, 3), (1, 0)):
                    act.wait_ge(s.ps_full, at(f, FILLS, 12 + half))
                    nc.scalar.copy(v[p][:, 512 * half:512 * half + 512], front_ps[bank][:, :]).then_inc(s.act_emptied, 1)

            def front_exp(f):
                act.wait_ge(s.soft_shift, f + 1)
                nc.scalar.activation(e_sb[:, :, :], s_sb[:, :, :], ACT.Exp).then_inc(s.soft_exp, 1)

            def back(w):
                act.wait_ge(s.back_full, at(w, BACKS, 7))
                nc.scalar.copy(oT[:, :, :].rearrange("p k t -> p (k t)"), back_ps[:, 0:2, :].rearrange("p k t -> p (k t)")).then_inc(s.oT_ready, 1)

            def tile(w, p):
                more = not (isinstance(w, int) and w == TILES - 1)
                if more:
                    front(w + 1, 1 - p)
                back(w)
                if more:
                    front_exp(w + 1)

            act.wait_ge(s.loaded, 16 * (LOADS - 1))
            nc.scalar.activation(beta[:, :], beta_in[:, :], ACT.Sigmoid).then_inc(s.set_up, 1)
            front(0, 0)
            front_exp(0)
            in_tile_pairs(act, tile)

        @block.gpsimd
        def _(pool):
            def rstd_of(f, m):
                pool.wait_ge(s.ln_mv, at(f, 2, m + 1))
                nc.gpsimd.tensor_tensor(var[:, m:m + 1], mv[:, m, 1:2], c.eps[:, 0:1], ALU.add).then_inc(s.ln_var, 1)
                pool.wait_ge(s.ln_var, at(f, 2, m + 1))
                nc.gpsimd.tensor_tensor(rstd[:, m:m + 1], var[:, m:m + 1], c.minus_half[:, 0:1], ALU.pow).then_inc(s.ln_rstd, 1)

            def rope(f):
                for k in range(2):
                    pool.wait_ge(s.cos_done, at(f, 2, k + 1))
                    nc.gpsimd.tensor_tensor(roped[k][:, :, :], roped[k][:, :, :], turned[k][:, :, :], ALU.add).then_inc(s.rope_done, 1)

            def tile(w, p):
                more = not (isinstance(w, int) and w == TILES - 1)
                pool.wait_ge(s.o_ready, at(w, 2, 2))
                nc.gpsimd.tensor_tensor(o_sum[:, :], o[:, :], local[p][:, :], ALU.add).then_inc(s.o_sum_ready, 1)
                if more:
                    if not (isinstance(w, int) and w == TILES - 2):
                        rstd_of(w + 2, 0)
                    rope(w + 1)
                    if not (isinstance(w, int) and w == TILES - 2):
                        rstd_of(w + 2, 1)

            for f in range(2):
                rstd_of(f, 0)
                rstd_of(f, 1)
            rope(0)
            in_tile_pairs(pool, tile)

        @block.vector
        def _(dve):
            def stats_of(f, m, source):
                nc.vector.bn_stats(stats[:, m, :], source).then_inc(s.ln_stats, 1)
                wait_alone(dve, s.ln_stats, at(f, 2, m + 1), s.passed)
                nc.vector.bn_aggr(mv[:, m, :], stats[:, m, :]).then_inc(s.ln_mv, 1)

            def norm_1(f):
                stats_of(f, 0, X[:, f, :])

            def norm_2(f):
                dve.wait_ge(s.ln_rstd, at(f, 2, 1))
                nc.vector.tensor_scalar(xn1[:, :], X[:, f, :], mv[:, 0, 0:1], rstd[:, 0:1], ALU.subtract, ALU.mult).then_inc(s.xn1_ready, 1)
                wait_alone(dve, s.xn1_ready, f + 1, s.passed)
                stats_of(f, 1, xn1[:, :])

            def norm_3(f):
                dve.wait_ge(s.ln_rstd, at(f, 2, 2))
                wait(dve, s.ps_full, at(f, FILLS, 1 - FILLS))
                nc.vector.tensor_scalar(xn2[:, :], xn1[:, :], mv[:, 1, 0:1], rstd[:, 1:2], ALU.subtract, ALU.mult).then_inc(s.xn2_ready, 1)

            wide = lambda table: table[:, :].unsqueeze(1)

            def front_rope(f, k):
                wait(dve, s.rope_done, at(f, 2, k) - 1)
                for half, bank in ((0, 2), (1, 0)):
                    dve.wait_ge(s.ps_full, at(f, FILLS, (3, 5, 8, 9)[2 * k + half]))
                    nc.vector.tensor_tensor(turned[k][:, 4 * half:4 * half + 4, :], front_ps[bank][:, :].rearrange("p (k t) -> p k t", t=P),
                                            wide(sin).broadcast_to([P, 4, P]), ALU.mult).then_inc(s.rot_done, 1)
                dve.wait_ge(s.act_emptied, at(f, EMPTIED, 3 + 2 * k))
                wait(dve, s.ps_full, at(f, FILLS, 14 - FILLS))
                nc.vector.tensor_tensor(roped[k][:, :, :], raw[k][:, :, :], wide(cos).broadcast_to([P, PAIRS, P]), ALU.mult).then_inc(s.cos_done, 1)

            def front_phi(f, p, k):
                if k < 2:
                    dve.wait_ge(s.elu_ready, at(f, 2, k + 1))
                else:
                    dve.wait_ge(s.act_emptied, at(f, EMPTIED, 7))
                out = (phi_qT[p][:, :, :].rearrange("p k t -> p (k t)"), phi_kT[p][:, :, :].rearrange("p k t -> p (k t)"), phi_k[p][:, :])[k]
                nc.vector.scalar_tensor_tensor(out=out, in0=expo[k % 2][:, :], scalar=1.0, in1=relu[k % 2][:, :],
                                               op0=ALU.min, op1=ALU.add).then_inc(s.phi_ready, 1)

            def front_softmax_1(f):
                step = lambda k: at(f, SOFT_STEPS, k)
                by_half = halves(s_sb[:, :, :])
                dve.wait_ge(s.ps_full, at(f, FILLS, 14))
                wait(dve, s.soft_exp, f)
                for r in range(2):
                    last = nc.vector.scalar_tensor_tensor(out=by_half[:, r], in0=front_ps[1 + r][:, 0:PAIRS * SEG].rearrange("p (c m) -> p c m", m=SEG),
                                                          scalar=SCALE, in1=causal[:, :].unsqueeze(1).broadcast_to([P, PAIRS, SEG]),
                                                          op0=ALU.mult, op1=ALU.add)
                last.then_inc(s.scores_read, 1)
                dve.wait_ge(s.scores_read, f + 1)
                nc.vector.tensor_reduce(smax[:, :], s_sb[:, :, :], AX.X, ALU.max).then_inc(s.soft_step, 1)
                dve.wait_ge(s.soft_step, step(1))
                nc.vector.tensor_tensor(s_sb[:, :, :], s_sb[:, :, :], smax[:, :].unsqueeze(2).broadcast_to([P, HEADS, SEG]),
                                        ALU.subtract).then_inc(s.soft_shift, 1)

            def front_softmax_2(f):
                step = lambda k: at(f, SOFT_STEPS, k)
                dve.wait_ge(s.soft_exp, f + 1)
                wait(dve, s.ps_full, at(f, FILLS, 15 - FILLS))
                nc.vector.transpose(eT[:, :, :].rearrange("p h m -> p (h m)"), e_sb[:, :, :].rearrange("p h m -> p (h m)")).then_inc(s.pT_ready, 1)
                nc.vector.tensor_reduce(ssum[:, :], e_sb[:, :, :], AX.X, ALU.add).then_inc(s.soft_step, 1)
                dve.wait_ge(s.soft_step, step(2))
                nc.vector.reciprocal(srec[:, :], ssum[:, :]).then_inc(s.soft_step, 1)
                dve.wait_ge(s.soft_step, step(3))
                nc.vector.tensor_tensor(srec[:, :], srec[:, :], one_less_beta[:, :], ALU.mult).then_inc(s.soft_step, 1)
                dve.wait_ge(s.soft_step, step(4))

            def front_local(f, p):
                dve.wait_ge(s.ps_full, at(f, FILLS, 15))
                wait(dve, s.o_sum_ready, f - 1)
                for half, bank in ((0, 3), (1, 0)):
                    last = nc.vector.tensor_tensor(local[p][:, 512 * half:512 * half + 512].rearrange("p (h d) -> p h d", d=DH),
                                                   front_ps[bank][:, :].rearrange("p (h d) -> p h d", d=DH),
                                                   srec[:, 8 * half:8 * half + 8].unsqueeze(2).broadcast_to([P, 8, DH]), ALU.mult)
                last.then_inc(s.local_ready, 1)

            def answer(half):
                banks = back_ps[:, 2 * half:2 * half + 2, 0:4 * AUG].rearrange("p r (c e) -> p r c e", e=AUG)
                return banks[:, :, :, 0:DH], banks[:, :, :, DH]

            pairs_of = lambda ap, half: halves(ap)[:, :, 4 * half:4 * half + 4, :]
            spread = lambda ap: ap.unsqueeze(3).broadcast_to([P, 2, 4, DH])

            def back_u(w, p, half):
                step = lambda k: at(w, 10, 2 * half + k)
                values, norms = answer(half)
                dve.wait_ge(s.back_full, at(w, BACKS, 1 + half))
                nc.vector.reciprocal(rden[:, half], norms).then_inc(s.back_step, 1)
                dve.wait_ge(s.back_step, step(1))
                nc.vector.tensor_tensor(held[:, half], values, spread(rden[:, half]), ALU.mult).then_inc(s.back_step, 1)
                dve.wait_ge(s.back_step, step(2))
                nc.vector.tensor_tensor(pairs_of(u[:, :, 0:DH], half), pairs_of(v[p][:, :].rearrange("p (h d) -> p h d", d=DH), half),
                                        held[:, half], ALU.subtract).then_inc(s.u_ready, 1)

            def back_o(w, half):
                step = lambda k: at(w, 10, 4 + 3 * half + k)
                values, norms = answer(half)
                dve.wait_ge(s.back_full, at(w, BACKS, 3 + half))
                if half == 0:
                    wait(dve, s.o_sum_ready, w)
                nc.vector.tensor_scalar(rden[:, 2 + half], norms, 1e-6, None, ALU.add).then_inc(s.back_step, 1)
                dve.wait_ge(s.back_step, step(1))
                nc.vector.reciprocal(rden[:, 2 + half], rden[:, 2 + half]).then_inc(s.back_step, 1)
                dve.wait_ge(s.back_step, step(2))
                nc.vector.tensor_tensor(rden[:, 2 + half], rden[:, 2 + half], beta[:, :].rearrange("p (c r) -> p r c", r=2)[:, :, 4 * half:4 * half + 4],
                                        ALU.mult).then_inc(s.back_step, 1)
                dve.wait_ge(s.back_step, step(3))
                nc.vector.tensor_tensor(pairs_of(o[:, :].rearrange("p (h d) -> p h d", d=DH), half), values, spread(rden[:, 2 + half]),
                                        ALU.mult).then_inc(s.o_ready, 1)

            def back_mem(w, half):
                dve.wait_ge(s.back_full, at(w, BACKS, 5 + half))
                part = mem[:, :, 4 * half:4 * half + 4, :]
                nc.vector.tensor_tensor(part, part, back_ps[:, :, 0:4 * AUG].rearrange("p b (c e) -> p b c e", e=AUG), ALU.add).then_inc(s.mem_done, 1)

            def back_x(w):
                dve.wait_ge(s.back_full, at(w, BACKS, 8))
                nc.vector.tensor_tensor(X[:, w, :], X[:, w, :], back_ps[:, 2, 0:D], ALU.add).then_inc(s.x_done, 1)

            def tile(w, p):
                more = not (isinstance(w, int) and w == TILES - 1)
                norm = more and not (isinstance(w, int) and w == TILES - 2)
                for half in range(2):
                    back_u(w, p, half)
                for half in range(2):
                    back_o(w, half)
                for half in range(2):
                    back_mem(w, half)
                if norm:
                    norm_1(w + 2)
                if more:
                    front_rope(w + 1, 0)
                    front_phi(w + 1, 1 - p, 0)
                if norm:
                    norm_2(w + 2)
                if more:
                    front_rope(w + 1, 1)
                    for k in (1, 2):
                        front_phi(w + 1, 1 - p, k)
                if norm:
                    norm_3(w + 2)
                if more:
                    front_softmax_1(w + 1)
                    front_softmax_2(w + 1)
                    front_local(w + 1, 1 - p)
                back_x(w)

            nc.vector.memset(mem[:, :, :, 0:DH], 0.0)
            nc.vector.memset(mem[:, :, :, DH:AUG], 1e-6).then_inc(s.set_up, 1)
            nc.vector.memset(u[:, :, DH:AUG], 1.0)
            dve.wait_ge(s.loaded, 16 * (LOADS - 1))
            pairs = w_qkv[:, 0:2 * INNER].rearrange("p (i two) -> p i two", two=2)
            turned_w = w_rot[:, :].rearrange("p (i two) -> p i two", two=2)
            nc.vector.tensor_scalar(turned_w[:, :, 0], pairs[:, :, 1], -1.0, None, ALU.mult).then_inc(s.set_up, 1)
            nc.vector.tensor_copy(turned_w[:, :, 1], pairs[:, :, 0]).then_inc(s.set_up, 1)
            dve.wait_ge(s.set_up, 4)
            nc.vector.tensor_scalar(one_less_beta[:, :], beta[:, :], -1.0, 1.0, ALU.mult, ALU.add).then_inc(s.set_up, 1)
            for f in range(2):
                norm_1(f)
                norm_2(f)
                norm_3(f)
            front_rope(0, 0)
            front_phi(0, 0, 0)
            front_rope(0, 1)
            front_phi(0, 0, 1)
            front_phi(0, 0, 2)
            front_softmax_1(0)
            front_softmax_2(0)
            front_local(0, 0)
            in_tile_pairs(dve, tile)
B_HEADS, B_DH = 8, 16
PADDED = 32
QUAD = 4
WINDOW = 3
WEIGHTS = ("L1_attn_Wq", "L1_attn_Wk", "L1_attn_Wv", "L1_attn_Wproj", "L1_attn_Wo")


def band_attention_stage(nc, K, io):
    with ExitStack() as ctx:
        sb = lambda name, shape, dt=F32: ctx.enter_context(nc.sbuf_tensor(f"b_{name}", shape, dt))
        A = Named()
        A.wT = sb("wT", [P, len(WEIGHTS), P])
        A.w1T, A.w2T = sb("w1T", [P, 64]), sb("w2T", [64, 1])
        A.qk_bias, A.v_bias, A.o_bias = sb("qk_bias", [P, 2, P]), sb("v_bias", [P, P]), sb("o_bias", [P, P])
        A.proj_bias, A.b1, A.b2 = sb("proj_bias", [P, 1]), sb("b1", [64, 1]), sb("b2", [P, 1])
        A.ones, A.row_ones = sb("ones", [P, P]), sb("row_ones", [P, P])
        A.band = sb("band", [P, 3, WINDOW * SEG])
        A.row_of = sb("row_of", [P, BATCH])
        A.tiny = sb("tiny", [P, 1])
        A.v = sb("v", [P, TILES + 2, P])
        A.qn = K.w0.turned[:, 0:TILES, :]
        A.kn = sb("kn", [P, TILES + 2, P])
        A.soft = [sb(f"soft_{n}", [P, TILES, P]) for n in "qk"]
        A.norms = sb("norms", [P, TILES, 2])
        A.use_inv = sb("use_inv", [P, 2])
        A.plogp = sb("plogp", [P, 1])
        A.joint = sb("joint", [P, 2 * BATCH])
        A.gate = sb("gate", [P, 1])
        A.curv = sb("curv", [P, TILES])
        with ExitStack() as inner:
            A.xnT = inner.enter_context(nc.sbuf_tensor("b_xnT", [P, TILES * P], F32))
            A.invT = inner.enter_context(nc.sbuf_tensor("b_invT", [P, TILES * P], F32))
            band_projections(nc, K, A, io)
            band_queries(nc, K, A)
        band_entropies(nc, K, A)
        band_windows(nc, K, A)
        band_sum(nc, K, A)


def band_projections(nc, K, A, io):
    X, c = K.X, K.c
    with ExitStack() as ctx:
        sb = lambda name, shape, dt=F32: ctx.enter_context(nc.sbuf_tensor(f"bp_{name}", shape, dt))
        ps = lambda name: ctx.enter_context(nc.psum_tensor(f"bp_{name}", [P, 512], F32))
        natural, w1_natural = sb("natural", [P, len(WEIGHTS), P]), sb("w1_natural", [64, P])
        stats, mv, var, rstd = sb("stats", [P, GROUP, 6]), sb("mv", [P, GROUP, 2]), sb("var", [P, GROUP]), sb("rstd", [P, GROUP])
        xn, xs, inv, res = sb("xn", [P, GROUP, D]), sb("xs", [P, BLOCK]), sb("inv", [P, BLOCK]), sb("res", [P, BLOCK])
        squares = [sb(f"squares{m}", [P, BLOCK]) for m in range(2)]
        x_ps, inv_ps, v_ps, n_ps, w_ps, w_ps2 = (ps(n) for n in ("x_ps", "inv_ps", "v_ps", "n_ps", "w_ps", "w_ps2"))
        s = stage_sems(nc, ctx, "bp", "weights loaded passed turned kept ln_stats ln_mv ln_var ln_rstd xn_ready x_full xs_ready xs_kept inv_full inv_ready "
                                     "inv_kept v_full v_ready res_ready squares_ready n_full n_ready sqrt_ready gauge_step gauge_full")
        block = ctx.enter_context(nc.Block())
        SMALL = 12

        @block.sync
        def _(sp):
            for k, name in enumerate(WEIGHTS):
                sp.dma_start(natural[:, k, :], io[name]).then_inc(s.weights, 16)
            sp.dma_start(w1_natural[:, :], io["L1_attn_W1"]).then_inc(s.weights, 16)
            with nc.allow_non_contiguous_dma(reason="one element per partition"):
                for dst, src in ((A.proj_bias[:, :], io["L1_attn_bproj"].unsqueeze(1)), (A.v_bias[:, :], io["L1_attn_bv"].partition_broadcast(P)),
                                 (A.qk_bias[:, 0, :], io["L1_attn_bq"].partition_broadcast(P)), (A.qk_bias[:, 1, :], io["L1_attn_bk"].partition_broadcast(P)),
                                 (A.o_bias[:, :], io["L1_attn_bo"].partition_broadcast(P)), (A.b1[:, :], io["L1_attn_b1"].unsqueeze(1)),
                                 (A.b2[:, :], io["L1_attn_b2"].partition_broadcast(P)), (A.w2T[:, :], io["L1_attn_W2"].rearrange("a k -> k a")),
                                 (A.row_ones[:, :], io["c_row_ones"]), (A.band[:, :, :], io["c_band"]), (A.row_of[:, :], io["c_row_of"])):
                    sp.dma_start(dst, src).then_inc(s.loaded, 16)
            sp.wait_ge(s.loaded, 16 * (SMALL - 1))

        @block.tensor
        def _(pe):
            pe.wait_ge(s.weights, 16 * (len(WEIGHTS) + 1))
            for k in range(len(WEIGHTS)):
                bank = (w_ps, w_ps2)[k // 4]
                nc.tensor.transpose(bank[:, (k % 4) * P:(k % 4 + 1) * P], natural[:, k, :], c.ident[:, :])
            nc.tensor.transpose(w_ps2[:, P:P + 64], w1_natural[:, :], c.ident[0:64, 0:64]).then_inc(s.turned, 1)

            def trip(j, p):
                pe.wait_ge(s.xn_ready, j + 1)
                wait(pe, s.xs_ready, j)
                for t in range(GROUP):
                    last = nc.tensor.transpose(x_ps[:, t * P:(t + 1) * P], xn[:, t, :], c.ident[:, :])
                last.then_inc(s.x_full, 1)
                pe.wait_ge(s.xs_ready, j + 1)
                wait(pe, s.inv_ready, j)
                nc.tensor.matmul(inv_ps[:, :], A.wT[:, 3, :], xs[:, :], start=True, stop=True).then_inc(s.inv_full, 1)
                wait(pe, s.v_ready, j)
                for t in range(GROUP):
                    last = nc.tensor.matmul(v_ps[:, t * P:(t + 1) * P], xs[:, t * P:(t + 1) * P], A.wT[:, 2, :], start=(t == 0), stop=True,
                                            skip_group_check=True)
                last.then_inc(s.v_full, 1)
                pe.wait_ge(s.squares_ready, at(j, 2, 2))
                wait(pe, s.n_ready, j)
                for t in range(GROUP):
                    for m in range(2):
                        last = nc.tensor.matmul(n_ps[:, 2 * t + m:2 * t + m + 1], squares[m][:, t * P:(t + 1) * P], A.ones[:, 0:1],
                                                start=(t == 0 and m == 0), stop=True, skip_group_check=True)
                last.then_inc(s.n_full, 1)

            pe.wait_ge(s.kept, 3)
            in_trips(pe, trip)
            pe.wait_ge(s.gauge_step, 5)
            nc.tensor.matmul(n_ps[:, 0:1], A.ones[:, :], A.norms[:, 0, 0:1], start=True, stop=True).then_inc(s.gauge_full, 1)

        @block.scalar
        def _(act):
            def trip(j, p):
                act.wait_ge(s.x_full, j + 1)
                wait(act, s.n_full, j)
                wait(act, s.xs_kept, j)
                nc.scalar.copy(xs[:, :], x_ps[:, :]).then_inc(s.xs_ready, 1)
                act.wait_ge(s.xs_ready, j + 1)
                nc.scalar.activation(squares[1][:, :], xs[:, :], ACT.Square).then_inc(s.squares_ready, 1)
                act.wait_ge(s.inv_full, j + 1)
                wait(act, s.inv_kept, j)
                nc.scalar.activation(inv[:, :], inv_ps[:, :], ACT.Identity, bias=A.proj_bias[:, :]).then_inc(s.inv_ready, 1)
                act.wait_ge(s.res_ready, j + 1)
                nc.scalar.activation(squares[0][:, :], res[:, :], ACT.Square).then_inc(s.squares_ready, 1)

            act.wait_ge(s.loaded, 16 * (SMALL - 1))
            in_trips(act, trip)
            act.wait_ge(s.n_ready, TRIPS)
            nc.scalar.activation(A.norms[:, :, :], A.norms[:, :, :], ACT.Sqrt).then_inc(s.sqrt_ready, 1)

        @block.gpsimd
        def _(pool):
            def trip(j, p):
                pool.wait_ge(s.ln_mv, j + 1)
                nc.gpsimd.tensor_tensor(var[:, :], mv[:, :, 1], c.eps[:, 0:GROUP], ALU.add).then_inc(s.ln_var, 1)
                pool.wait_ge(s.ln_var, j + 1)
                nc.gpsimd.tensor_tensor(rstd[:, :], var[:, :], c.minus_half[:, 0:GROUP], ALU.pow).then_inc(s.ln_rstd, 1)
                wait_alone(pool, s.xs_ready, j + 1, s.passed)
                nc.gpsimd.tensor_copy(A.xnT[:, bass.ds(j * BLOCK, BLOCK)], xs[:, :]).then_inc(s.xs_kept, 1)
                wait_alone(pool, s.inv_ready, j + 1, s.passed)
                nc.gpsimd.tensor_copy(A.invT[:, bass.ds(j * BLOCK, BLOCK)], inv[:, :]).then_inc(s.inv_kept, 1)

            in_trips(pool, trip)

        @block.vector
        def _(dve):
            def trip(j, p):
                for t in range(GROUP):
                    last = nc.vector.bn_stats(stats[:, t, :], X[:, j * GROUP + t, :])
                last.then_inc(s.ln_stats, 1)
                wait_alone(dve, s.ln_stats, j + 1, s.passed)
                for t in range(GROUP):
                    last = nc.vector.bn_aggr(mv[:, t, :], stats[:, t, :])
                last.then_inc(s.ln_mv, 1)
                dve.wait_ge(s.ln_rstd, j + 1)
                wait(dve, s.x_full, j)
                for t in range(GROUP):
                    last = nc.vector.tensor_scalar(xn[:, t, :], X[:, j * GROUP + t, :], mv[:, t, 0:1], rstd[:, t:t + 1],
                                                   ALU.subtract, ALU.mult)
                last.then_inc(s.xn_ready, 1)
                dve.wait_ge(s.inv_ready, j + 1)
                nc.vector.tensor_tensor(res[:, :], xs[:, :], inv[:, :], ALU.subtract).then_inc(s.res_ready, 1)
                dve.wait_ge(s.v_full, j + 1)
                nc.vector.tensor_tensor(A.v[:, bass.ds(j * GROUP + 1, GROUP), :], v_ps[:, :].rearrange("p (t d) -> p t d", d=P),
                                        A.v_bias[:, :].unsqueeze(1).broadcast_to([P, GROUP, P]), ALU.add).then_inc(s.v_ready, 1)
                dve.wait_ge(s.n_full, j + 1)
                nc.vector.tensor_copy(A.norms[:, bass.ds(j * GROUP, GROUP), :], n_ps[:, 0:2 * GROUP].rearrange("p (t m) -> p t m", m=2)).then_inc(s.n_ready, 1)

            nc.vector.memset(A.ones[:, :], 1.0)
            nc.vector.memset(A.tiny[:, :], 1e-10)
            for kept in (A.v, A.kn):
                for end in (0, TILES + 1):
                    nc.vector.memset(kept[:, end, :], 0.0)
            dve.wait_ge(s.turned, 1)
            nc.vector.tensor_copy(A.wT[:, 0:4, :], w_ps[:, :].rearrange("p (k d) -> p k d", d=P)).then_inc(s.kept, 1)
            nc.vector.tensor_copy(A.wT[:, 4, :], w_ps2[:, 0:P]).then_inc(s.kept, 1)
            nc.vector.tensor_copy(A.w1T[:, :], w_ps2[:, P:P + 64]).then_inc(s.kept, 1)
            dve.wait_ge(s.loaded, 16 * (SMALL - 1))
            in_trips(dve, trip)
            dve.wait_ge(s.sqrt_ready, 1)
            nc.vector.tensor_scalar(A.norms[:, :, 1], A.norms[:, :, 1], 1e-8, None, ALU.add).then_inc(s.gauge_step, 1)
            dve.wait_ge(s.gauge_step, 1)
            nc.vector.reciprocal(A.curv[:, :], A.norms[:, :, 1]).then_inc(s.gauge_step, 1)
            dve.wait_ge(s.gauge_step, 2)
            nc.vector.tensor_tensor(A.curv[:, :], A.curv[:, :], A.norms[:, :, 0], ALU.mult).then_inc(s.gauge_step, 1)
            dve.wait_ge(s.gauge_step, 3)
            nc.vector.tensor_reduce(A.gate[:, :], A.curv[:, :], AX.X, ALU.add).then_inc(s.gauge_step, 1)
            dve.wait_ge(s.gauge_step, 4)
            nc.vector.tensor_copy(A.norms[:, 0, 0:1], A.gate[:, :]).then_inc(s.gauge_step, 1)
            dve.wait_ge(s.gauge_full, 1)
            nc.vector.tensor_scalar(A.use_inv[:, 0:1], n_ps[:, 0:1], 1.0 / (BATCH * SEQ), 0.3, ALU.mult, ALU.is_gt).then_inc(s.gauge_step, 1)
            dve.wait_ge(s.gauge_step, 6)
            nc.vector.tensor_scalar(A.use_inv[:, 1:2], A.use_inv[:, 0:1], -1.0, 1.0, ALU.mult, ALU.add).then_inc(s.gauge_step, 1)


def band_queries(nc, K, A):
    c = K.c
    VECS = GROUP * 2 * B_HEADS
    with ExitStack() as ctx:
        sb = lambda name, shape, dt=F32: ctx.enter_context(nc.sbuf_tensor(f"bq_{name}", shape, dt))
        tmp, xq = sb("tmp", [P, BLOCK]), sb("xq", [P, BLOCK])
        qk, square, shifted, expd = (sb(n, [P, GROUP, 2, P]) for n in ("qk", "square", "shifted", "expd"))
        sumsq, rnorm, vmax, vsum, vrec, half_power = (sb(n, [P, VECS]) for n in ("sumsq", "rnorm", "vmax", "vsum", "vrec", "half_power"))
        total, texp, tlog = (sb(n, [P, 2 * P]) for n in ("total", "texp", "tlog"))
        tmax, tsum = sb("tmax", [P, 16]), sb("tsum", [P, 16])
        qk_ps = ctx.enter_context(nc.psum_tensor("bq_qk_ps", [P, 2, 512], F32))
        total_ps = ctx.enter_context(nc.psum_tensor("bq_total_ps", [P, 512], F32))
        s = stage_sems(nc, ctx, "bq", "tmp_ready xq_ready qk_full qk_ready totals squared sum_step rnorm_ready unit_ready soft_step "
                                     "shift_ready exp_ready soft_ready marg_step marg_shift marg_exp marg_prob marg_log")
        block = ctx.enter_context(nc.Block())
        vecs = lambda ap: ap.rearrange("p t m (h d) -> p (t m h) d", d=B_DH)
        spread = lambda ap: ap[:, :].unsqueeze(2).broadcast_to([P, VECS, B_DH])

        @block.tensor
        def _(pe):
            def trip(j, p):
                first = isinstance(j, int) and j == 0
                pe.wait_ge(s.xq_ready, j + 1)
                wait(pe, s.qk_ready, j)
                for t in range(GROUP):
                    last = nc.tensor.matmul(qk_ps[:, t // 2, (t % 2) * 256:(t % 2 + 1) * 256], xq[:, t * P:(t + 1) * P],
                                            A.wT[:, 0:2, :].rearrange("p m d -> p (m d)"), start=(t % 2 == 0), stop=True, skip_group_check=True)
                last.then_inc(s.qk_full, 1)
                pe.wait_ge(s.qk_ready, j + 1)
                for t in range(GROUP):
                    last = nc.tensor.matmul(total_ps[:, 0:2 * P], A.row_ones[:, :], qk[:, t].rearrange("p m d -> p (m d)"),
                                            start=(first and t == 0), stop=(not first and not isinstance(j, int)) or t == GROUP - 1,
                                            skip_group_check=True)
                last.then_inc(s.totals, 1)

            in_trips(pe, trip)

        @block.scalar
        def _(act):
            def trip(j, p):
                act.wait_ge(s.qk_ready, j + 1)
                wait(act, s.sum_step, at(j, 2, -1))
                nc.scalar.activation(square[:, :, :, :], qk[:, :, :, :], ACT.Square).then_inc(s.squared, 1)
                act.wait_ge(s.shift_ready, j + 1)
                wait(act, s.soft_ready, j)
                nc.scalar.activation(expd[:, :, :, :], shifted[:, :, :, :], ACT.Exp).then_inc(s.exp_ready, 1)

            in_trips(act, trip)
            act.wait_ge(s.marg_shift, 1)
            nc.scalar.activation(texp[:, :], total[:, :], ACT.Exp).then_inc(s.marg_exp, 1)
            act.wait_ge(s.marg_prob, 1)
            nc.scalar.activation(tlog[:, :], texp[:, :], ACT.Ln, bias=A.tiny[:, :]).then_inc(s.marg_log, 1)

        @block.gpsimd
        def _(pool):
            def trip(j, p):
                pool.wait_ge(s.sum_step, at(j, 2, 2))
                nc.gpsimd.tensor_tensor(rnorm[:, :], sumsq[:, :], half_power[:, :], ALU.pow).then_inc(s.rnorm_ready, 1)

            in_trips(pool, trip)

        @block.vector
        def _(dve):
            def trip(j, p):
                block_of = bass.ds(j * BLOCK, BLOCK)
                nc.vector.tensor_scalar(tmp[:, :], A.xnT[:, block_of], A.use_inv[:, 1:2], None, ALU.mult).then_inc(s.tmp_ready, 1)
                dve.wait_ge(s.tmp_ready, j + 1)
                wait(dve, s.qk_full, j)
                nc.vector.scalar_tensor_tensor(out=xq[:, :], in0=A.invT[:, block_of], scalar=A.use_inv[:, 0:1], in1=tmp[:, :],
                                               op0=ALU.mult, op1=ALU.add).then_inc(s.xq_ready, 1)
                dve.wait_ge(s.qk_full, j + 1)
                wait(dve, s.totals, j)
                nc.vector.tensor_tensor(qk[:, :, :, :].rearrange("p t m d -> p t (m d)"), qk_ps[:, :, :].rearrange("p a (b d) -> p (a b) d", d=2 * P),
                                        A.qk_bias[:, :, :].rearrange("p m d -> p (m d)").unsqueeze(1).broadcast_to([P, GROUP, 2 * P]),
                                        ALU.add).then_inc(s.qk_ready, 1)
                dve.wait_ge(s.qk_ready, j + 1)
                nc.vector.tensor_reduce(vmax[:, :], vecs(qk[:, :, :, :]), AX.X, ALU.max).then_inc(s.soft_step, 1)
                dve.wait_ge(s.soft_step, at(j, 3, 1))
                nc.vector.tensor_tensor(vecs(shifted[:, :, :, :]), vecs(qk[:, :, :, :]), spread(vmax), ALU.subtract).then_inc(s.shift_ready, 1)
                dve.wait_ge(s.squared, j + 1)
                nc.vector.tensor_reduce(sumsq[:, :], vecs(square[:, :, :, :]), AX.X, ALU.add).then_inc(s.sum_step, 1)
                dve.wait_ge(s.sum_step, at(j, 2, 1))
                nc.vector.tensor_scalar(sumsq[:, :], sumsq[:, :], 1e-24, None, ALU.max).then_inc(s.sum_step, 1)
                dve.wait_ge(s.exp_ready, j + 1)
                nc.vector.tensor_reduce(vsum[:, :], vecs(expd[:, :, :, :]), AX.X, ALU.add).then_inc(s.soft_step, 1)
                dve.wait_ge(s.soft_step, at(j, 3, 2))
                nc.vector.reciprocal(vrec[:, :], vsum[:, :]).then_inc(s.soft_step, 1)
                dve.wait_ge(s.soft_step, at(j, 3, 3))
                by_vec = lambda ap, m: ap.rearrange("p (t m h) -> p t m h", t=GROUP, m=2)[:, :, m, :].unsqueeze(3).broadcast_to([P, GROUP, B_HEADS, B_DH])
                heads = lambda ap: ap.rearrange("p t (h d) -> p t h d", d=B_DH)
                for m in range(2):
                    last = nc.vector.tensor_tensor(heads(A.soft[m][:, bass.ds(j * GROUP, GROUP), :]), heads(expd[:, :, m, :]), by_vec(vrec[:, :], m), ALU.mult)
                last.then_inc(s.soft_ready, 1)
                dve.wait_ge(s.rnorm_ready, j + 1)
                for m, unit in enumerate((A.qn[:, bass.ds(j * GROUP, GROUP), :], A.kn[:, bass.ds(j * GROUP + 1, GROUP), :])):
                    last = nc.vector.tensor_tensor(heads(unit), heads(qk[:, :, m, :]), by_vec(rnorm[:, :], m), ALU.mult)
                last.then_inc(s.unit_ready, 1)

            nc.vector.memset(half_power[:, :], -0.5)
            in_trips(dve, trip)
            by16 = lambda ap: ap[:, :].rearrange("p (v d) -> p v d", d=B_DH)
            spread16 = lambda ap: ap[:, :].unsqueeze(2).broadcast_to([P, 16, B_DH])
            dve.wait_ge(s.totals, TRIPS)
            nc.vector.tensor_reduce(tmax[:, :], total_ps[:, 0:2 * P].rearrange("p (v d) -> p v d", d=B_DH), AX.X, ALU.max).then_inc(s.marg_step, 1)
            dve.wait_ge(s.marg_step, 1)
            nc.vector.tensor_tensor(by16(total), total_ps[:, 0:2 * P].rearrange("p (v d) -> p v d", d=B_DH), spread16(tmax), ALU.subtract).then_inc(s.marg_shift, 1)
            dve.wait_ge(s.marg_exp, 1)
            nc.vector.tensor_reduce(tsum[:, :], by16(texp), AX.X, ALU.add).then_inc(s.marg_step, 1)
            dve.wait_ge(s.marg_step, 2)
            nc.vector.reciprocal(tsum[:, :], tsum[:, :]).then_inc(s.marg_step, 1)
            dve.wait_ge(s.marg_step, 3)
            nc.vector.tensor_tensor(by16(texp), by16(texp), spread16(tsum), ALU.mult).then_inc(s.marg_prob, 1)
            dve.wait_ge(s.marg_log, 1)
            nc.vector.tensor_tensor(total[:, :], texp[:, :], tlog[:, :], ALU.mult).then_inc(s.marg_step, 1)
            dve.wait_ge(s.marg_step, 4)
            nc.vector.tensor_reduce(A.plogp[:, :], total[:, :], AX.X, ALU.add).then_inc(s.marg_step, 1)


def band_entropies(nc, K, A):
    c = K.c
    ROWS, COLS = SEQ // P, SEQ // 512
    STEPS = ROWS * COLS
    with ExitStack() as ctx:
        sb = lambda name, shape, dt=F32: ctx.enter_context(nc.sbuf_tensor(f"be_{name}", shape, dt))
        padded = [K.w0.turned[:, TILES + GROUP * m:TILES + GROUP * (m + 1), :].rearrange("p t (a d) -> p t a d", d=PADDED) for m in range(2)]
        softT = [sb(f"softT_{n}", [P, TILES * P]) for n in "qk"]
        row = [sb(f"row_{n}", [P, SEQ]) for n in "qk"]
        logs = [sb(f"logs{i}", [P, QUAD, 512]) for i in range(2)]
        sums = sb("sums", [P, STEPS])
        entropy = sb("entropy", [P, 4])
        joint_all = sb("joint_all", [P, 2 * BATCH])
        joint_ps = [ctx.enter_context(nc.psum_tensor(f"be_joint{i}", [P, QUAD, 512], F32)) for i in range(2)]
        s = stage_sems(nc, ctx, "be", "cleared passed padded_ready turned_full turned_kept row_ready joint_full log_ready summed row_summed entropy_step all_full")
        block = ctx.enter_context(nc.Block())

        def each_row(eng, group, one_row):
            if group == 0:
                one_row(0, 0)
                with eng.Fori(1, BATCH) as b:
                    one_row(b, b)
            else:
                with eng.Fori(BATCH, 2 * BATCH) as r:
                    one_row(r, r - BATCH)

        @block.tensor
        def _(pe):
            def one_row(r, b):
                pe.wait_ge(s.row_ready, at(r, 2, 2))
                for k in range(STEPS):
                    i, half = k // COLS, k % COLS
                    if k >= 2:
                        wait_alone(pe, s.summed, at(r, STEPS, k - 1), s.passed)
                    else:
                        wait(pe, s.summed, at(r, STEPS, k - 1))
                        wait_alone(pe, s.row_ready, at(r, 2, 2), s.passed)
                    for a in range(QUAD):
                        rows = slice(PADDED * a, PADDED * (a + 1))
                        last = nc.tensor.matmul(joint_ps[k % 2][:, a, :], row[0][rows, i * P:(i + 1) * P], row[1][rows, half * 512:(half + 1) * 512],
                                                start=True, stop=True)
                    last.then_inc(s.joint_full, 1)

            for group in range(2):
                def turn(j, p):
                    n = group * TRIPS + j
                    pe.wait_ge(s.padded_ready, at(n, 2, 2))
                    wait(pe, s.turned_kept, at(n, 2, 0))
                    if group == 1 and isinstance(j, int) and j == 0:
                        pe.wait_ge(s.summed, BATCH * STEPS)
                    for m in range(2):
                        for t in range(GROUP):
                            last = nc.tensor.transpose(joint_ps[0][:, m, t * P:(t + 1) * P], padded[m][:, t].rearrange("p a d -> p (a d)"), c.ident[:, :])
                    last.then_inc(s.turned_full, 1)

                in_trips(pe, turn)
                pe.wait_ge(s.turned_kept, at(group, 2 * TRIPS, 2 * TRIPS))
                each_row(pe, group, one_row)
            pe.wait_ge(s.row_summed, 2 * BATCH)
            pe.wait_ge(s.summed, 2 * BATCH * STEPS)
            nc.tensor.matmul(joint_ps[0][:, 0, 0:2 * BATCH], A.ones[:, :], A.joint[:, :], start=True, stop=True).then_inc(s.all_full, 1)

        @block.scalar
        def _(act):
            act.wait_ge(s.cleared, 2)

            def one_row(r, b):
                wait(act, s.joint_full, at(r, STEPS, 0))
                nc.scalar.copy(row[0][:, :].rearrange("p (w n) -> p w n", n=SEG),
                               softT[0][:, :].rearrange("p (w b n) -> p w b n", b=BATCH, n=SEG)[:, :, b, :]).then_inc(s.row_ready, 1)
                for k in range(STEPS):
                    act.wait_ge(s.joint_full, at(r, STEPS, k + 1))
                    wait(act, s.summed, at(r, STEPS, k - 1))
                    nc.scalar.activation(logs[k % 2][:, :, :], joint_ps[k % 2][:, :, :], ACT.Ln, bias=A.tiny[:, :]).then_inc(s.log_ready, 1)

            for group in range(2):
                def turn(j, p):
                    n = group * TRIPS + j
                    wait(act, s.turned_full, n)
                    nc.scalar.copy(padded[0][:, :, :, 0:B_DH], A.soft[0][:, bass.ds(j * GROUP, GROUP), group * 64:group * 64 + 64]
                                   .rearrange("p t (a d) -> p t a d", d=B_DH)).then_inc(s.padded_ready, 1)
                    act.wait_ge(s.turned_full, n + 1)
                    nc.scalar.copy(softT[0][:, bass.ds(j * BLOCK, BLOCK)], joint_ps[0][:, 0, :]).then_inc(s.turned_kept, 1)

                in_trips(act, turn)
                act.wait_ge(s.turned_kept, at(group, 2 * TRIPS, 2 * TRIPS))
                each_row(act, group, one_row)

        @block.vector
        def _(dve):
            for m in range(2):
                nc.vector.memset(padded[m][:, :, :, :], 0.0).then_inc(s.cleared, 1)
            dve.wait_ge(s.cleared, 2)

            def one_row(r, b):
                wait(dve, s.joint_full, at(r, STEPS, 0))
                nc.vector.tensor_copy(row[1][:, :].rearrange("p (w n) -> p w n", n=SEG),
                                      softT[1][:, :].rearrange("p (w b n) -> p w b n", b=BATCH, n=SEG)[:, :, b, :]).then_inc(s.row_ready, 1)
                for k in range(STEPS):
                    dve.wait_ge(s.log_ready, at(r, STEPS, k + 1))
                    flat = logs[k % 2][:, :, :].rearrange("p a j -> p (a j)")
                    nc.vector.tensor_tensor_reduce(out=flat, in0=joint_ps[k % 2][:, :, :].rearrange("p a j -> p (a j)"), in1=flat,
                                                   scale=1.0, scalar=0.0, op0=ALU.mult, op1=ALU.add,
                                                   accum_out=sums[:, k:k + 1]).then_inc(s.summed, 1)
                dve.wait_ge(s.summed, at(r, STEPS, STEPS))
                nc.vector.tensor_reduce(A.joint[:, bass.ds(r, 1)], sums[:, :], AX.X, ALU.add).then_inc(s.row_summed, 1)

            for group in range(2):
                def turn(j, p):
                    n = group * TRIPS + j
                    wait(dve, s.turned_full, n)
                    nc.vector.tensor_copy(padded[1][:, :, :, 0:B_DH], A.soft[1][:, bass.ds(j * GROUP, GROUP), group * 64:group * 64 + 64]
                                          .rearrange("p t (a d) -> p t a d", d=B_DH)).then_inc(s.padded_ready, 1)
                    dve.wait_ge(s.turned_full, n + 1)
                    nc.vector.tensor_copy(softT[1][:, bass.ds(j * BLOCK, BLOCK)], joint_ps[0][:, 1, :]).then_inc(s.turned_kept, 1)

                in_trips(dve, turn)
                dve.wait_ge(s.turned_kept, at(group, 2 * TRIPS, 2 * TRIPS))
                each_row(dve, group, one_row)
            dve.wait_ge(s.all_full, 1)
            nc.vector.tensor_copy(joint_all[:, :], joint_ps[0][:, 0, 0:2 * BATCH]).then_inc(s.entropy_step, 1)
            dve.wait_ge(s.entropy_step, 1)
            nc.vector.tensor_tensor(joint_all[:, 0:BATCH], joint_all[:, 0:BATCH], joint_all[:, BATCH:2 * BATCH], ALU.add).then_inc(s.entropy_step, 1)
            dve.wait_ge(s.entropy_step, 2)
            nc.vector.tensor_tensor(joint_all[:, BATCH:2 * BATCH], joint_all[:, 0:BATCH], A.row_of[:, :], ALU.mult).then_inc(s.entropy_step, 1)
            dve.wait_ge(s.entropy_step, 3)
            nc.vector.tensor_reduce(entropy[:, 0:1], joint_all[:, BATCH:2 * BATCH], AX.X, ALU.add).then_inc(s.entropy_step, 1)
            dve.wait_ge(s.entropy_step, 4)
            nc.vector.tensor_tensor(entropy[:, 1:2], A.plogp[:, :], entropy[:, 0:1], ALU.subtract).then_inc(s.entropy_step, 1)
            dve.wait_ge(s.entropy_step, 5)
            nc.vector.tensor_scalar(A.gate[:, :], entropy[:, 1:2], 1.0 / B_HEADS, 0.15, ALU.mult, ALU.is_gt).then_inc(s.entropy_step, 1)


def band_windows(nc, K, A):
    c = K.c
    KEYS = GROUP + 2
    WIDE = WINDOW * SEG
    ROWS_T = GROUP * B_HEADS
    with ExitStack() as ctx:
        sb = lambda name, shape, dt=F32: ctx.enter_context(nc.sbuf_tensor(f"bw_{name}", shape, dt))
        pad_q, pad_k = sb("pad_q", [P, GROUP, 2, P]), sb("pad_k", [P, KEYS, 2, P])
        qT, kT = sb("qT", [P, GROUP, 2, P]), sb("kT", [P, KEYS, 2, P])
        v = sb("v", [P, KEYS, P])
        dist, expd = (sb(n, [P, GROUP, B_HEADS, WIDE]) for n in ("dist", "expd"))
        expT = A.soft[1][:, :, :].rearrange("p w d -> p (w d)")[:, 0:ROWS_T * WIDE].rearrange("p (t h m) -> p t h m", t=GROUP, h=B_HEADS)
        esum, erec, grec, eden = (sb(n, [P, ROWS_T]) for n in ("esum", "erec", "grec", "eden"))
        factor = sb("factor", [P, ROWS_T])
        out, outT, hid = sb("out", [P, GROUP, P]), sb("outT", [P, BLOCK]), sb("hid", [64, BLOCK])
        sim_ps = ctx.enter_context(nc.psum_tensor("bw_sim", [P, QUAD, 512], F32))
        turn_ps = [ctx.enter_context(nc.psum_tensor(f"bw_turn{i}", [P, 512], F32)) for i in range(2)]
        o_ps, h_ps = (ctx.enter_context(nc.psum_tensor(f"bw_{n}", [P, 512], F32)) for n in ("o", "h"))
        s = stage_sems(nc, ctx, "bw", "cleared passed pad_ready v_ready turn_full turn_kept sim_full dist_read clipped roots exps masked esum_step recip_ready factor_ready expT_ready "
                                     "o_full out_ready outT_full outT_ready h_full h_ready curv_full curv_ready z_full z_ready")
        block = ctx.enter_context(nc.Block())
        TURNS = 5

        @block.tensor
        def _(pe):
            def trip(j, p):
                pe.wait_ge(s.pad_ready, at(j, 2, 2))
                for q in range(TURNS):
                    if q >= 2:
                        pe.wait_ge(s.turn_kept, at(j, TURNS, q - 1))
                    else:
                        wait(pe, s.z_ready, j)
                    for m in range(4):
                        i = 4 * q + m
                        source = pad_q[:, i // 2, i % 2, :] if q < 2 else pad_k[:, (i - 8) // 2, i % 2, :]
                        last = nc.tensor.transpose(turn_ps[q % 2][:, m * P:(m + 1) * P], source, c.ident[:, :])
                    last.then_inc(s.turn_full, 1)
                pe.wait_ge(s.turn_kept, at(j, TURNS, TURNS))
                for t in range(GROUP):
                    wait_alone(pe, s.dist_read, at(j, GROUP, t), s.passed)
                    for g in range(2):
                        for a in range(QUAD):
                            rows = slice(PADDED * a, PADDED * (a + 1))
                            for b in range(BATCH):
                                seg = slice(SEG * b, SEG * (b + 1))
                                last = nc.tensor.matmul(sim_ps[seg, a, g * WIDE:(g + 1) * WIDE], qT[rows, t, g, seg], kT[rows, t:t + WINDOW, g, seg],
                                                        start=True, stop=True, skip_group_check=True)
                    last.then_inc(s.sim_full, 1)
                pe.wait_ge(s.v_ready, j + 1)
                wait(pe, s.out_ready, j)
                wait_alone(pe, s.expT_ready, j + 1, s.passed)
                for t in range(GROUP):
                    for h in range(B_HEADS):
                        for b in range(BATCH):
                            seg = slice(SEG * b, SEG * (b + 1))
                            for k in range(WINDOW):
                                last = nc.tensor.matmul(o_ps[seg, t * P + h * B_DH:t * P + (h + 1) * B_DH],
                                                        expT[seg, t, 2 * (h % QUAD) + h // QUAD, k * SEG:(k + 1) * SEG],
                                                        v[seg, t + k, h * B_DH:(h + 1) * B_DH], start=(k == 0), stop=(k == WINDOW - 1),
                                                        skip_group_check=True)
                last.then_inc(s.o_full, 1)
                pe.wait_ge(s.out_ready, j + 1)
                for t in range(GROUP):
                    last = nc.tensor.transpose(turn_ps[0][:, t * P:(t + 1) * P], out[:, t, :], c.ident[:, :])
                last.then_inc(s.outT_full, 1)
                pe.wait_ge(s.outT_ready, j + 1)
                wait(pe, s.curv_ready, j)
                nc.tensor.matmul(h_ps[0:64, :], A.w1T[:, :], outT[:, :], start=True, stop=True).then_inc(s.h_full, 1)
                for t in range(GROUP):
                    last = nc.tensor.matmul(turn_ps[1][:, t * P:(t + 1) * P], outT[:, t * P:(t + 1) * P], A.wT[:, 4, :], start=(t == 0), stop=True,
                                            skip_group_check=True)
                last.then_inc(s.z_full, 1)
                pe.wait_ge(s.h_ready, j + 1)
                for t in range(GROUP):
                    last = nc.tensor.matmul(h_ps[:, t:t + 1], hid[:, t * P:(t + 1) * P], A.w2T[:, :], start=(t == 0), stop=True, skip_group_check=True)
                last.then_inc(s.curv_full, 1)

            in_trips(pe, trip)

        @block.scalar
        def _(act):
            act.wait_ge(s.cleared, 2)

            def trip(j, p):
                pads = lambda ap: ap.rearrange("p t g (a d) -> p (t g a) d", d=PADDED)[:, :, 0:B_DH]
                heads = lambda ap: ap.rearrange("p t (h d) -> p (t h) d", d=B_DH)
                wait(act, s.turn_full, at(j, TURNS, 0))
                nc.scalar.copy(pads(pad_q[:, :, :, :]), heads(A.qn[:, bass.ds(j * GROUP, GROUP), :])).then_inc(s.pad_ready, 1)
                nc.scalar.copy(pads(pad_k[:, :, :, :]), heads(A.kn[:, bass.ds(j * GROUP, KEYS), :])).then_inc(s.pad_ready, 1)
                wait(act, s.sim_full, at(j, GROUP, 0))
                for q in range(TURNS):
                    act.wait_ge(s.turn_full, at(j, TURNS, q + 1))
                    half = slice(2 * q, 2 * q + 2) if q < 2 else slice(2 * q - 4, 2 * q - 2)
                    nc.scalar.copy((qT if q < 2 else kT)[:, half, :, :], turn_ps[q % 2][:, :].rearrange("p (t g d) -> p t g d", g=2, d=P)).then_inc(s.turn_kept, 1)
                act.wait_ge(s.clipped, j + 1)
                nc.scalar.activation(dist[:, :, :, :], dist[:, :, :, :], ACT.Sqrt).then_inc(s.roots, 1)
                act.wait_ge(s.roots, j + 1)
                wait(act, s.expT_ready, j)
                nc.scalar.activation(expd[:, :, :, :], dist[:, :, :, :], ACT.Exp, scale=-1.0).then_inc(s.exps, 1)
                act.wait_ge(s.outT_full, j + 1)
                nc.scalar.copy(outT[:, :], turn_ps[0][:, :]).then_inc(s.outT_ready, 1)
                act.wait_ge(s.h_full, j + 1)
                nc.scalar.activation(hid[:, :], h_ps[0:64, :], ACT.Relu, bias=A.b1[:, :]).then_inc(s.h_ready, 1)
                act.wait_ge(s.z_full, j + 1)
                nc.scalar.copy(A.soft[0][:, bass.ds(j * GROUP, GROUP), :], turn_ps[1][:, :].rearrange("p (t d) -> p t d", d=P)).then_inc(s.z_ready, 1)

            in_trips(act, trip)

        @block.gpsimd
        def _(pool):
            def trip(j, p):
                wait_alone(pool, s.o_full, j, s.passed)
                nc.gpsimd.tensor_copy(v[:, :, :], A.v[:, bass.ds(j * GROUP, KEYS), :]).then_inc(s.v_ready, 1)

            in_trips(pool, trip)

        @block.vector
        def _(dve):
            nc.vector.memset(pad_q[:, :, :, :], 0.0).then_inc(s.cleared, 1)
            nc.vector.memset(pad_k[:, :, :, :], 0.0).then_inc(s.cleared, 1)

            def trip(j, p):
                step = lambda k: at(j, 5, k)
                for t in range(GROUP):
                    dve.wait_ge(s.sim_full, at(j, GROUP, t + 1))
                    if t == 0:
                        wait(dve, s.exps, j)
                    nc.vector.tensor_scalar(dist[:, t].rearrange("p (a g) m -> p a (g m)", g=2), sim_ps[:, :, 0:2 * WIDE], -2.0, 2.0,
                                            ALU.mult, ALU.add).then_inc(s.dist_read, 1)
                dve.wait_ge(s.dist_read, at(j, GROUP, GROUP))
                nc.vector.tensor_scalar(dist[:, :, :, :], dist[:, :, :, :], 1e-30, 4.0, ALU.max, ALU.min).then_inc(s.clipped, 1)
                dve.wait_ge(s.exps, j + 1)
                for t in range(GROUP):
                    edge = 0 if isinstance(j, int) and (j, t) == (0, 0) else 2 if isinstance(j, int) and (j, t) == (TRIPS - 1, GROUP - 1) else 1
                    last = nc.vector.tensor_tensor(expd[:, t], expd[:, t], A.band[:, edge, :].unsqueeze(1).broadcast_to([P, B_HEADS, WIDE]), ALU.mult)
                last.then_inc(s.masked, 1)
                dve.wait_ge(s.masked, j + 1)
                wait(dve, s.o_full, j)
                nc.vector.transpose(expT[:, :, :, :].rearrange("p t h m -> p (t h m)"), expd[:, :, :, :].rearrange("p t h m -> p (t h m)")).then_inc(s.expT_ready, 1)
                nc.vector.tensor_reduce(esum[:, :], expd[:, :, :, :].rearrange("p t h m -> p (t h) m"), AX.X, ALU.add).then_inc(s.esum_step, 1)
                dve.wait_ge(s.esum_step, step(1))
                nc.vector.reciprocal(erec[:, :], esum[:, :]).then_inc(s.esum_step, 1)
                dve.wait_ge(s.esum_step, step(2))
                nc.vector.tensor_scalar(grec[:, :], erec[:, :], A.gate[:, :], None, ALU.mult).then_inc(s.esum_step, 1)
                dve.wait_ge(s.esum_step, step(3))
                nc.vector.tensor_tensor(eden[:, :], grec[:, :], esum[:, :], ALU.mult).then_inc(s.esum_step, 1)
                dve.wait_ge(s.esum_step, step(4))
                nc.vector.tensor_scalar(eden[:, :], eden[:, :], 1e-10, None, ALU.add).then_inc(s.esum_step, 1)
                dve.wait_ge(s.esum_step, step(5))
                nc.vector.reciprocal(eden[:, :], eden[:, :]).then_inc(s.recip_ready, 1)
                dve.wait_ge(s.recip_ready, j + 1)
                by_place = lambda ap: ap[:, :].rearrange("p (t a g) -> p t a g", a=QUAD, g=2)
                nc.vector.tensor_tensor(factor[:, :].rearrange("p (t g a) -> p t a g", a=QUAD, g=2), by_place(eden), by_place(grec),
                                        ALU.mult).then_inc(s.factor_ready, 1)
                dve.wait_ge(s.factor_ready, j + 1)
                dve.wait_ge(s.o_full, j + 1)
                wait(dve, s.outT_full, j)
                nc.vector.tensor_tensor(out[:, :, :].rearrange("p t (h d) -> p (t h) d", d=B_DH), o_ps[:, :].rearrange("p (r d) -> p r d", d=B_DH),
                                        factor[:, :].unsqueeze(2).broadcast_to([P, ROWS_T, B_DH]), ALU.mult).then_inc(s.out_ready, 1)
                dve.wait_ge(s.curv_full, j + 1)
                nc.vector.tensor_copy(A.curv[:, bass.ds(j * GROUP, GROUP)], h_ps[:, 0:GROUP]).then_inc(s.curv_ready, 1)

            in_trips(dve, trip)


def band_sum(nc, K, A):
    X = K.X
    with ExitStack() as ctx:
        sb = lambda name, shape, dt=F32: ctx.enter_context(nc.sbuf_tensor(f"bs_{name}", shape, dt))
        curved, social, penalty = sb("curved", [P, TILES]), sb("social", [P, 1]), sb("penalty", [P, 4])
        sum_ps = ctx.enter_context(nc.psum_tensor("bs_sum", [P, 512], F32))
        s = stage_sems(nc, ctx, "bs", "curved_ready social_full exp_ready step")
        block = ctx.enter_context(nc.Block())

        @block.scalar
        def _(act):
            nc.scalar.activation(curved[:, :], A.curv[:, :], ACT.Sigmoid, bias=A.b2[:, :]).then_inc(s.curved_ready, 1)
            act.wait_ge(s.social_full, 1)
            nc.scalar.activation(penalty[:, 0:1], sum_ps[:, 0:1], ACT.Exp, scale=-1.0 / 0.5 / (BATCH * SEQ)).then_inc(s.exp_ready, 1)

        @block.tensor
        def _(pe):
            pe.wait_ge(s.step, 1)
            nc.tensor.matmul(sum_ps[:, 0:1], A.ones[:, :], social[:, :], start=True, stop=True).then_inc(s.social_full, 1)

        @block.vector
        def _(dve):
            dve.wait_ge(s.curved_ready, 1)
            nc.vector.tensor_reduce(social[:, :], curved[:, :], AX.X, ALU.add).then_inc(s.step, 1)
            dve.wait_ge(s.exp_ready, 1)
            nc.vector.tensor_scalar(penalty[:, 1:2], penalty[:, 0:1], 0.5, 1.5, ALU.max, ALU.min).then_inc(s.step, 1)
            dve.wait_ge(s.step, 2)
            nc.vector.tensor_scalar(penalty[:, 2:3], penalty[:, 1:2], -1.0, 1.0, ALU.mult, ALU.add).then_inc(s.step, 1)
            dve.wait_ge(s.step, 3)
            nc.vector.tensor_scalar(penalty[:, 3:4], penalty[:, 2:3], -0.3, 1.0, ALU.mult, ALU.add).then_inc(s.step, 1)
            dve.wait_ge(s.step, 4)
            nc.vector.scalar_tensor_tensor(out=X[:, :, :], in0=A.soft[0][:, :, :], scalar=penalty[:, 3:4], in1=X[:, :, :],
                                           op0=ALU.mult, op1=ALU.add).then_inc(s.step, 1)
            dve.wait_ge(s.step, 5)
            nc.vector.tensor_tensor(X[:, :, :], X[:, :, :], A.o_bias[:, :].unsqueeze(1).broadcast_to([P, TILES, P]), ALU.add).then_inc(s.step, 1)
def load_stage(nc, K, io):
    X, c, w0 = K.X, K.c, K.w0
    with ExitStack() as ctx:
        sb = lambda name, shape, dt=F32: ctx.enter_context(nc.sbuf_tensor(f"ld_{name}", shape, dt))
        BLOCKS = 5 * NE
        natural = sb("natural", [P, BLOCKS, D])
        gate_natural = sb("gate_natural", [E, D])
        banks = [ctx.enter_context(nc.psum_tensor(f"ld_ps{i}", [P, 512], F32)) for i in range(2)]
        s = stage_sems(nc, ctx, "ld", "const x natural small turned kept")
        block = ctx.enter_context(nc.Block())
        up = [natural[:, m * 2 * NE:(m + 1) * 2 * NE, :].rearrange("p (e two) d -> p e two d", two=2) for m in range(2)]
        down = natural[:, 4 * NE:5 * NE, :]
        quads = [(i, min(4, BLOCKS - i)) for i in range(0, BLOCKS, 4)]
        turned = w0.turned[:, :, :].rearrange("p k f -> p (k f)")

        @block.sync
        def _(sp):
            for dst, name in ((c.ident, "c_ident"), (c.iota, "c_iota"), (c.minus_half, "c_minus_half"), (c.eps, "c_eps")):
                sp.dma_start(dst[:, :], io[name]).then_inc(s.const, 16)
            for m, (routed, shared) in enumerate((("L0_ffn_w1", "L0_ffn_sw1"), ("L0_ffn_w3", "L0_ffn_sw3"))):
                sp.dma_start(up[m][:, 0:E], io[routed].rearrange("e (p two) d -> p e two d", two=2)).then_inc(s.natural, 16)
                sp.dma_start(up[m][:, E], io[shared].rearrange("(p two) d -> p two d", two=2)).then_inc(s.natural, 16)
            sp.dma_start(down[:, 0:E, :], io["L0_ffn_w2"].rearrange("e d f -> d e f")).then_inc(s.natural, 16)
            sp.dma_start(down[:, E, :], io["L0_ffn_sw2"]).then_inc(s.natural, 16)
            sp.dma_start(gate_natural[:, :], io["L0_ffn_gate_w"]).then_inc(s.natural, 16)
            for b in range(BATCH):
                sp.dma_start(X[SEG * b:SEG * (b + 1), :, :], io["L0_attn_x"][b].rearrange("(w n) d -> n w d", n=SEG)).then_inc(s.x, 16)
            sp.wait_ge(s.x, 16 * BATCH)

        @block.scalar
        def _(act):
            n = 0
            with nc.allow_non_contiguous_dma(reason="biases, one element per partition"):
                for dst, src in ((w0.b1[:, 0:E, :], io["L0_ffn_b1"].rearrange("e (p two) -> p e two", two=2)),
                                 (w0.b1[:, E, :], io["L0_ffn_sb1"].rearrange("(p two) -> p two", two=2)),
                                 (w0.b3[:, 0:E, :], io["L0_ffn_b3"].rearrange("e (p two) -> p e two", two=2)),
                                 (w0.b3[:, E, :], io["L0_ffn_sb3"].rearrange("(p two) -> p two", two=2)),
                                 (w0.b2[0:E, :], io["L0_ffn_b2"]), (w0.b2[E:NE, :], io["L0_ffn_sb2"].unsqueeze(0)),
                                 (w0.router_bias[:, :], io["L0_ffn_gate_b"].partition_broadcast(P))):
                    act.dma_start(dst, src).then_inc(s.small, 16)
                    n += 16
            act.wait_ge(s.small, n)

        @block.tensor
        def _(pe):
            pe.wait_ge(s.const, 64)
            pe.wait_ge(s.natural, 16 * 7)
            for q, (first, count) in enumerate(quads):
                if q >= 2:
                    pe.wait_ge(s.kept, q - 1)
                for k in range(count):
                    last = nc.tensor.transpose(banks[q % 2][:, k * P:(k + 1) * P], natural[:, first + k, :], c.ident[:, :])
                last.then_inc(s.turned, 1)
            pe.wait_ge(s.kept, len(quads) - 1)
            nc.tensor.transpose(banks[len(quads) % 2][:, 0:E], gate_natural[:, :], c.ident[0:E, 0:E]).then_inc(s.turned, 1)

        @block.vector
        def _(dve):
            for q, (first, count) in enumerate(quads):
                dve.wait_ge(s.turned, q + 1)
                nc.vector.tensor_copy(turned[:, first * P:(first + count) * P], banks[q % 2][:, 0:count * P]).then_inc(s.kept, 1)
            dve.wait_ge(s.turned, len(quads) + 1)
            nc.vector.tensor_copy(w0.router[:, :], banks[len(quads) % 2][:, 0:E]).then_inc(s.kept, 1)


def load_silu_weights(nc, eng, io, w, loaded):
    n = 0
    with nc.allow_non_contiguous_dma(reason="biases, one element per partition"):
        for dst, src in ((w.router1[:, :], io["L1_ffn_Wr1"]), (w.router1_bias[:, :], io["L1_ffn_br1"].unsqueeze(1)),
                         (w.router2[:, :], io["L1_ffn_Wr2"]), (w.router2_bias[:, :], io["L1_ffn_br2"].partition_broadcast(P)),
                         (w.be1[:, 0:E, :], io["L1_ffn_be1"].rearrange("e (k p) -> p e k", p=P)),
                         (w.be1[:, E, :], io["L1_ffn_bs1"].rearrange("(k p) -> p k", p=P)),
                         (w.be2[0:E, :], io["L1_ffn_be2"]), (w.be2[E:NE, :], io["L1_ffn_bs2"].unsqueeze(0)),
                         (w.we1[:, 0:E, :], io["L1_ffn_We1"].rearrange("e c i -> c e i")), (w.we1[:, E, :], io["L1_ffn_Ws1"]),
                         (w.we2[:, E, :, :], io["L1_ffn_Ws2"].rearrange("(k p) c -> p k c", p=P)),
                         *((w.we2[:, e, :, :], io["L1_ffn_We2"][e].rearrange("(k p) c -> p k c", p=P)) for e in range(E))):
            eng.dma_start(dst, src).then_inc(loaded, 16)
            n += 16
    eng.wait_ge(loaded, n)


def store_stage(nc, K, out):
    with ExitStack() as ctx:
        stored = ctx.enter_context(nc.semaphore("stored"))
        block = ctx.enter_context(nc.Block())

        @block.sync
        def _(sp):
            for b in range(BATCH):
                sp.dma_start(out[b].rearrange("(w n) d -> n w d", n=SEG), K.X[SEG * b:SEG * (b + 1), :, :]).then_inc(stored, 16)
            sp.wait_ge(stored, 16 * BATCH)


def allocate_silu_weights(sb, K):
    K.w1 = w1 = Named()
    w1.we1 = sb("w1_we1", [P, NE, 512])
    w1.we2 = sb("w1_we2", [P, NE, 4, D])
    w1.be1 = sb("w1_be1", [P, NE, 4])
    w1.be2 = sb("w1_be2", [NE, D])
    w1.router1 = sb("w1_router1", [P, 32])
    w1.router1_bias = sb("w1_router1_bias", [32, 1])
    w1.router2 = sb("w1_router2", [32, E])
    w1.router2_bias = sb("w1_router2_bias", [P, E])


def allocate_gated_weights(sb, K):
    K.w0 = w0 = Named()
    w0.turned = sb("w0_turned", [P, 5 * NE, P])
    w0.w13T = w0.turned[:, 0:4 * NE, :].rearrange("p (m e two) f -> p m e two f", m=2, two=2)
    w0.w2T = w0.turned[:, 4 * NE:5 * NE, :]
    w0.router = sb("w0_router", [P, E])
    w0.router_bias = sb("w0_router_bias", [P, E])
    w0.b1 = sb("w0_b1", [P, NE, 2])
    w0.b3 = sb("w0_b3", [P, NE, 2])
    w0.b2 = sb("w0_b2", [NE, D])


def build_program(nc, io, out):
    with ExitStack() as ctx:
        sb = lambda name, shape, dt=F32: ctx.enter_context(nc.sbuf_tensor(name, shape, dt))
        K = Named()
        K.X = sb("X", [P, TILES, D])
        K.c = c = Named()
        c.ident = sb("ident", [P, P])
        c.iota = sb("iota", [P, E])
        c.minus_half = sb("minus_half", [P, 8])
        c.eps = sb("eps", [P, 8])
        allocate_gated_weights(sb, K)
        K.s0 = make_sems(nc, ctx, "f0", ROUTE_SEMS + " t3g_ready t3l_ready pg_ready pl_ready g_ready l_ready gl_ready sig_ready "
                                                     "full_g1 full_g3 full_l1 full_l3 a_ready y_full y_done x_done")
        K.s1 = make_sems(nc, ctx, "f1", ROUTE_SEMS + " pair_mult loaded y_full y_done x_done", "h_full a_ready")
        load_stage(nc, K, io)
        gated_stage(nc, K, 0, io)
        memory_attention_stage(nc, K, io)
        allocate_silu_weights(sb, K)
        gated_stage(nc, K, 1, io)
        silu_stage(nc, K, 0)
        band_attention_stage(nc, K, io)
        silu_stage(nc, K, 1)
        store_stage(nc, K, out)


def constants():
    place = np.arange(P) % SEG
    angle = np.outer(10000.0 ** (-np.arange(0, DH, 2) / DH), place)
    rows = np.arange(P) % DH // 2
    key = np.arange(WINDOW * SEG) - SEG
    near = np.abs(place[:, None] - key[None, :]) <= 32
    band = np.stack([near & (key >= 0), near, near & (key < SEG)], axis=1)
    return {"c_ident": np.eye(P, dtype=np.float32),
            "c_iota": np.tile(np.arange(E, dtype=np.float32), (P, 1)),
            "c_minus_half": np.full((P, 8), -0.5, np.float32),
            "c_eps": np.full((P, 8), LN_EPS, np.float32),
            "c_cos": np.cos(angle)[rows].astype(np.float32), "c_sin": np.sin(angle)[rows].astype(np.float32),
            "c_causal": np.where(np.arange(SEG)[None, :] <= place[:, None], 0.0, -1e30).astype(np.float32),
            "c_row_ones": (np.arange(P)[:, None] // SEG == np.arange(P)[None, :] // SEG).astype(np.float32),
            "c_row_of": (np.arange(P)[:, None] // SEG == np.arange(BATCH)[None, :]).astype(np.float32),
            "c_band": band.astype(np.float32)}


def kernel(**inputs):
    import concourse.bacc as bacc
    from concourse.bass_utils import run_bass_kernel_spmd

    nc = bacc.Bacc("TRN2", target_bir_lowering=False, num_devices=1)
    arrays = {name: np.ascontiguousarray(a) for name, a in inputs.items()} | constants()
    io = {name: nc.dram_tensor(name, a.shape, F32, kind="ExternalInput").ap() for name, a in arrays.items()}
    out = nc.dram_tensor("out", (BATCH, SEQ, D), F32, kind="ExternalOutput").ap()
    build_program(nc, io, out)
    return run_bass_kernel_spmd(nc, [arrays], core_ids=[0]).results[0]["out"]
```

```python
from collections import namedtuple
from contextlib import ExitStack

import numpy as np
import concourse.bass as bass
from concourse import mybir

F32 = mybir.dt.float32
F32R = mybir.dt.float32r
U32 = mybir.dt.uint32
ALU = mybir.AluOpType
ACT = mybir.ActivationFunctionType
AX = mybir.AxisListType

P = 128
BATCH, SEQ, D = 4, 1024, 128
SEG = 32
TILES = SEQ // SEG
GROUP = 4
TRIPS = TILES // GROUP
BLOCK = GROUP * P
HEADS, DH = 16, 64
PAIRS = HEADS // 2
INNER = HEADS * DH
E = 8
NE = E + 1
LN_EPS = 1e-5


def at(trip, per_trip, n):
    return trip * per_trip + n


def wait(eng, sem, value):
    if not isinstance(value, int) or value > 0:
        eng.wait_ge(sem, value)


def wait_alone(eng, sem, value, passed):
    if not isinstance(value, int) or value > 0:
        eng.wait_ge(sem, value)
        eng.sem_inc(passed, 1)


class Named:
    pass


def make_sems(nc, ctx, prefix, names, lists=""):
    make = lambda n: ctx.enter_context(nc.semaphore(f"{prefix}_{n}"))
    return namedtuple(prefix, (names + " " + lists).split())(*(make(n) for n in names.split()),
                                                             *([make(f"{n}{k}") for k in range(4)] for n in lists.split()))


def stage_sems(nc, ctx, prefix, names):
    s = namedtuple(prefix, names)(*(nc.alloc_semaphore(name=f"{prefix}_{n}") for n in names.split()))

    def give_back():
        nc.clear_and_free_semaphores(list(s))
        nc.all_engine_barrier()

    ctx.callback(give_back)
    return s


def in_trips(eng, one_trip):
    one_trip(0, 0)
    with eng.Fori(0, TRIPS // 2 - 1) as i:
        one_trip(2 * i + 1, 1)
        one_trip(2 * i + 2, 0)
    one_trip(TRIPS - 1, 1)
ORDER = [E] + list(range(E))

ROUTE_SEMS = ("ln_stats ln_mv ln_var ln_rstd xn_ready xnT_ps xnT_ready hid_ps hid_ready logits_ps "
              "passed gate_step shift_ready exp_ready pair_ready pair_exp cw_ready cwT_ps cwT_ready")


def route_buffers(sb, ps, kind):
    r = Named()
    r.stats = sb("ln_stats", [P, GROUP, 6])
    r.mv = sb("ln_mv", [P, GROUP, 2])
    r.var = sb("ln_var", [P, GROUP])
    r.rstd = sb("ln_rstd", [P, GROUP])
    r.xn = sb("xn", [P, GROUP, D])
    r.xnT = [sb(f"xnT{i}", [P, BLOCK]) for i in range(2)]
    r.logits = sb("logits", [P, GROUP, E])
    r.shift = sb("shift", [P, GROUP, E])
    r.expd = sb("expd", [P, GROUP, E])
    r.score = sb("score", [P, GROUP, E])
    r.biased = sb("biased", [P, GROUP, E])
    r.top = sb("top", [P, GROUP, 8])
    r.index = sb("index", [P, GROUP, 8], U32)
    r.indexf = sb("indexf", [P, GROUP, 8])
    r.hot = sb("hot", [P, 2, GROUP, E])
    r.small = sb("small", [P, 8, GROUP])
    r.cw = [sb(f"cw{i}", [P, GROUP, NE]) for i in range(2)]
    r.cwT = [sb(f"cwT{i}", [NE, BLOCK]) for i in range(2)]
    r.hidden = sb("router_hidden", [32, BLOCK]) if kind == 1 else None
    r.ps_x = ps("route_ps_x")
    r.ps_l = ps("route_ps_l")
    return r


GATE_STEPS = {0: 9, 1: 12}


class Route:

    def __init__(self, nc, kind, X, r, s, c, w):
        self.nc, self.kind, self.X, self.r, self.s, self.c, self.w = nc, kind, X, r, s, c, w

    def dve_stats(self, dve, j, n, p):
        nc, X, r, s = self.nc, self.X, self.r, self.s
        for t in range(GROUP):
            last = nc.vector.bn_stats(r.stats[:, t, :], X[:, j * GROUP + t, :])
        last.then_inc(s.ln_stats, 1)
        wait_alone(dve, s.ln_stats, n + 1, s.passed)
        for t in range(GROUP):
            last = nc.vector.bn_aggr(r.mv[:, t, :], r.stats[:, t, :])
        last.then_inc(s.ln_mv, 1)

    def pool_rstd(self, pool, j, n, p):
        nc, r, s = self.nc, self.r, self.s
        pool.wait_ge(s.ln_mv, n + 1)
        nc.gpsimd.tensor_tensor(r.var[:, :], r.mv[:, :, 1], self.c.eps[:, 0:GROUP], ALU.add).then_inc(s.ln_var, 1)
        pool.wait_ge(s.ln_var, n + 1)
        nc.gpsimd.tensor_tensor(r.rstd[:, :], r.var[:, :], self.c.minus_half[:, 0:GROUP], ALU.pow).then_inc(s.ln_rstd, 1)

    def dve_normalise(self, dve, j, n, p):
        nc, X, r, s = self.nc, self.X, self.r, self.s
        dve.wait_ge(s.ln_rstd, n + 1)
        wait(dve, s.xnT_ps, n)
        for t in range(GROUP):
            last = nc.vector.tensor_scalar(r.xn[:, t, :], X[:, j * GROUP + t, :], r.mv[:, t, 0:1], r.rstd[:, t:t + 1],
                                           ALU.subtract, ALU.mult)
        last.then_inc(s.xn_ready, 1)

    def pe_transpose(self, pe, j, n, p):
        nc, r, s = self.nc, self.r, self.s
        pe.wait_ge(s.xn_ready, n + 1)
        wait(pe, s.hid_ready if self.kind else s.xnT_ready, n)
        for t in range(GROUP):
            last = nc.tensor.transpose(r.ps_x[:, t * P:(t + 1) * P], r.xn[:, t, :], self.c.ident[:, :])
        last.then_inc(s.xnT_ps, 1)

    def act_xnT(self, act, j, n, p):
        nc, r, s = self.nc, self.r, self.s
        act.wait_ge(s.xnT_ps, n + 1)
        nc.scalar.copy(r.xnT[p][:, :], r.ps_x[:, :]).then_inc(s.xnT_ready, 1)

    def pe_hidden(self, pe, j, n, p):
        nc, r, s = self.nc, self.r, self.s
        pe.wait_ge(s.x_high, n + 1)
        nc.tensor.matmul(r.ps_x[0:32, :], self.w.router1[:, :], r.xnT[p][:, :], start=True, stop=True).then_inc(s.hid_ps, 1)

    def act_hidden(self, act, j, n, p):
        nc, r, s = self.nc, self.r, self.s
        act.wait_ge(s.hid_ps, n + 1)
        nc.scalar.activation(r.hidden[:, :], r.ps_x[0:32, :], ACT.Relu, bias=self.w.router1_bias[:, :]).then_inc(s.hid_ready, 1)

    def pe_logits(self, pe, j, n, p):
        nc, r, s = self.nc, self.r, self.s
        wait(pe, s.cwT_ready, n)
        if self.kind == 0:
            pe.wait_ge(s.xnT_ready, n + 1)
            lhs, rhs = r.xnT[p], self.w.router
        else:
            pe.wait_ge(s.hid_ready, n + 1)
            lhs, rhs = r.hidden, self.w.router2
        for t in range(GROUP):
            last = nc.tensor.matmul(r.ps_l[:, t * E:(t + 1) * E], lhs[:, t * P:(t + 1) * P], rhs[:, :], start=(t == 0), stop=True,
                                    skip_group_check=True)
        last.then_inc(s.logits_ps, 1)

    def dve_shift(self, dve, j, n, p):
        nc, r, s = self.nc, self.r, self.s
        k = lambda m: at(n, GATE_STEPS[self.kind], m)
        dve.wait_ge(s.logits_ps, n + 1)
        ps = r.ps_l[:, 0:GROUP * E].rearrange("p (t e) -> p t e", e=E)
        if self.kind == 0:
            nc.vector.tensor_copy(r.logits[:, :, :], ps).then_inc(s.gate_step, 1)
        else:
            nc.vector.tensor_tensor(r.logits[:, :, :], ps, self.w.router2_bias[:, :].unsqueeze(1).broadcast_to([P, GROUP, E]),
                                    ALU.add).then_inc(s.gate_step, 1)
        dve.wait_ge(s.gate_step, k(1))
        nc.vector.tensor_reduce(r.small[:, 0, :], r.logits[:, :, :], AX.X, ALU.max).then_inc(s.gate_step, 1)
        dve.wait_ge(s.gate_step, k(2))
        nc.vector.tensor_tensor(r.shift[:, :, :], r.logits[:, :, :], r.small[:, 0, :].unsqueeze(2).broadcast_to([P, GROUP, E]),
                                ALU.subtract).then_inc(s.shift_ready, 1)

    def act_exp(self, act, j, n, p):
        nc, r, s = self.nc, self.r, self.s
        act.wait_ge(s.shift_ready, n + 1)
        nc.scalar.activation(r.expd[:, :, :], r.shift[:, :, :], ACT.Exp).then_inc(s.exp_ready, 1)

    def dve_top2(self, dve, j, n, p):
        nc, r, s = self.nc, self.r, self.s
        k = lambda m: at(n, GATE_STEPS[self.kind], m)
        dve.wait_ge(s.exp_ready, n + 1)
        nc.vector.tensor_reduce(r.small[:, 1, :], r.expd[:, :, :], AX.X, ALU.add).then_inc(s.gate_step, 1)
        dve.wait_ge(s.gate_step, k(3))
        nc.vector.reciprocal(r.small[:, 2, :], r.small[:, 1, :]).then_inc(s.gate_step, 1)
        dve.wait_ge(s.gate_step, k(4))
        nc.vector.tensor_tensor(r.score[:, :, :], r.expd[:, :, :], r.small[:, 2, :].unsqueeze(2).broadcast_to([P, GROUP, E]),
                                ALU.mult).then_inc(s.gate_step, 1)
        ranked = r.score
        if self.kind == 0:
            dve.wait_ge(s.gate_step, k(5))
            ranked = r.biased
            nc.vector.tensor_tensor(r.biased[:, :, :], r.score[:, :, :], self.w.router_bias[:, :].unsqueeze(1).broadcast_to([P, GROUP, E]),
                                    ALU.add).then_inc(s.gate_step, 1)
        done = 6 if self.kind == 0 else 5
        wait_alone(dve, s.gate_step, k(done), s.passed)
        for t in range(GROUP):
            last = nc.vector.max(r.top[:, t, :], ranked[:, t, :])
        last.then_inc(s.gate_step, 1)
        wait_alone(dve, s.gate_step, k(done + 1), s.passed)
        for t in range(GROUP):
            last = nc.vector.max_index(r.index[:, t, :], r.top[:, t, :], ranked[:, t, :])
        last.then_inc(s.gate_step, 1)
        if self.kind == 1:
            nc.vector.tensor_tensor(r.small[:, 3, :], r.top[:, :, 1], r.top[:, :, 0], ALU.subtract).then_inc(s.pair_ready, 1)
        dve.wait_ge(s.gate_step, k(done + 2))
        nc.vector.tensor_copy(r.indexf[:, :, :], r.index[:, :, :]).then_inc(s.gate_step, 1)
        dve.wait_ge(s.gate_step, k(done + 3))
        for m in range(2):
            last = nc.vector.tensor_tensor(r.hot[:, m, :, :], self.c.iota[:, :].unsqueeze(1).broadcast_to([P, GROUP, E]),
                                           r.indexf[:, :, m].unsqueeze(2).broadcast_to([P, GROUP, E]), ALU.is_equal)
        if self.kind == 1:
            last.then_inc(s.gate_step, 1)
            return
        last.then_inc(s.pair_ready, 1)
        dve.wait_ge(s.pair_ready, n + 1)
        nc.vector.tensor_tensor(r.hot[:, 0, :, :], r.hot[:, 0, :, :], r.hot[:, 1, :, :], ALU.add).then_inc(s.pair_exp, 1)
        dve.wait_ge(s.pair_exp, n + 1)
        nc.vector.tensor_tensor(r.cw[p][:, :, 0:E], r.score[:, :, :], r.hot[:, 0, :, :], ALU.mult).then_inc(s.cw_ready, 1)

    def act_pair(self, act, j, n, p):
        nc, r, s = self.nc, self.r, self.s
        act.wait_ge(s.pair_ready, n + 1)
        nc.scalar.activation(r.small[:, 4, :], r.small[:, 3, :], ACT.Exp, scale=0.5).then_inc(s.pair_exp, 1)

    def dve_pair(self, dve, j, n, p):
        nc, r, s = self.nc, self.r, self.s
        k = lambda m: at(n, GATE_STEPS[1], m)
        dve.wait_ge(s.pair_exp, n + 1)
        nc.vector.tensor_scalar(r.small[:, 5, :], r.small[:, 4, :], 1.0, None, ALU.add).then_inc(s.gate_step, 1)
        dve.wait_ge(s.gate_step, k(10))
        nc.vector.reciprocal(r.small[:, 6, :], r.small[:, 5, :]).then_inc(s.gate_step, 1)
        dve.wait_ge(s.gate_step, k(11))
        nc.vector.tensor_tensor(r.small[:, 7, :], r.small[:, 6, :], r.small[:, 4, :], ALU.mult).then_inc(s.gate_step, 1)
        nc.vector.tensor_tensor(r.biased[:, :, :], r.hot[:, 0, :, :], r.small[:, 6, :].unsqueeze(2).broadcast_to([P, GROUP, E]),
                                ALU.mult)
        dve.wait_ge(s.gate_step, k(12))
        nc.vector.tensor_tensor(r.shift[:, :, :], r.hot[:, 1, :, :], r.small[:, 7, :].unsqueeze(2).broadcast_to([P, GROUP, E]),
                                ALU.mult).then_inc(s.pair_mult, 1)
        dve.wait_ge(s.pair_mult, n + 1)
        nc.vector.tensor_tensor(r.cw[p][:, :, 0:E], r.biased[:, :, :], r.shift[:, :, :], ALU.add).then_inc(s.cw_ready, 1)

    def pe_cwT(self, pe, j, n, p):
        nc, r, s = self.nc, self.r, self.s
        pe.wait_ge(s.cw_ready, n + 1)
        for t in range(GROUP):
            last = nc.tensor.transpose(r.ps_l[0:NE, t * P:(t + 1) * P], r.cw[p][:, t, :], self.c.ident[:, :])
        last.then_inc(s.cwT_ps, 1)

    def act_cwT(self, act, j, n, p):
        nc, r, s = self.nc, self.r, self.s
        act.wait_ge(s.cwT_ps, n + 1)
        nc.scalar.copy(r.cwT[p][:, :], r.ps_l[0:NE, :]).then_inc(s.cwT_ready, 1)


def expert_sum(nc, dve, s, r, buf, X, j, n, p, e):
    step = at(n, NE, e)
    b = (p + e) % 2
    dve.wait_ge(s.y_full, step + 1)
    wait(dve, s.y_done, step)
    if e == 0:
        wait(dve, s.x_done, n)
        last = nc.vector.tensor_copy(buf.acc[:, :, :], buf.ps_y[b][:, :].rearrange("p (t d) -> p t d", d=D))
    else:
        for t in range(GROUP):
            last = nc.vector.scalar_tensor_tensor(out=buf.acc[:, t, :], in0=buf.ps_y[b][:, t * D:(t + 1) * D],
                                                  scalar=r.cw[p][:, t, ORDER[e]:ORDER[e] + 1], in1=buf.acc[:, t, :],
                                                  op0=ALU.mult, op1=ALU.add)
    last.then_inc(s.y_done, 1)
    if e == NE - 1:
        dve.wait_ge(s.y_done, step + 1)
        x = X[:, bass.ds(j * GROUP, GROUP), :]
        nc.vector.scalar_tensor_tensor(out=x, in0=buf.acc[:, :, :], scalar=0.5, in1=x,
                                       op0=ALU.mult, op1=ALU.add).then_inc(s.x_done, 1)


def gated_stage(nc, K, call, io):
    F = 128
    X, c, w, s, base = K.X, K.c, K.w0, K.s0, call * TRIPS
    with ExitStack() as ctx:
        sb = lambda name, shape, dt=F32: ctx.enter_context(nc.sbuf_tensor(f"g{call}_{name}", shape, dt))
        ps = lambda name: ctx.enter_context(nc.psum_tensor(f"g{call}_{name}", [P, 512], F32))
        r = route_buffers(sb, ps, 0)
        buf = Named()
        h_full = {"g1": s.full_g1, "g3": s.full_g3, "l1": s.full_l1, "l3": s.full_l3}
        buf.ps_h = {h: ps(f"ps_{h}") for h in ("g1", "g3", "l1", "l3")}
        buf.ps_y = [ps(f"ps_y{i}") for i in range(2)]
        buf.t3 = {h: sb(f"t3{h}", [P, BLOCK]) for h in "gl"}
        buf.prod_g = sb("prod_g", [P, BLOCK])
        buf.prod_l = [sb(f"prod_l{i}", [P, BLOCK]) for i in range(2)]
        buf.g = [sb(f"g{i}", [P, BLOCK]) for i in range(2)]
        buf.l = [sb(f"l{i}", [P, BLOCK]) for i in range(2)]
        buf.sig = [sb(f"sig{i}", [P, BLOCK]) for i in range(2)]
        buf.gl = sb("gl", [P, BLOCK])
        buf.a = [sb(f"a{i}", [P, BLOCK]) for i in range(2)]
        buf.acc = sb("acc", [P, GROUP, D])
        route = Route(nc, 0, X, r, s, c, w)
        block = ctx.enter_context(nc.Block())

        def before(j, p, e):
            return (j, p, e - 1) if e else (j - 1, 1 - p, NE - 1)

        @block.tensor
        def _(pe):
            def outputs(j, p, e):
                n = base + j
                step = at(n, NE, e)
                b = (p + e) % 2
                pe.wait_ge(s.a_ready, step + 1)
                wait(pe, s.y_done, step - 1)
                for t in range(GROUP):
                    last = nc.tensor.matmul(buf.ps_y[b][:, t * D:(t + 1) * D], buf.a[b][:, t * P:(t + 1) * P], w.w2T[:, ORDER[e], :],
                                            start=(t == 0), stop=(e > 0), skip_group_check=True)
                if e == 0:
                    pe.wait_ge(s.cwT_ready, n + 1)
                    for t in range(GROUP):
                        last = nc.tensor.matmul(buf.ps_y[b][:, t * D:(t + 1) * D], r.cwT[p][:, t * P:(t + 1) * P], w.b2[:, :],
                                                start=False, stop=True, skip_group_check=True)
                last.then_inc(s.y_full, 1)

            def trip(j, p):
                n = base + j
                more = not (isinstance(j, int) and j == TRIPS - 1)
                pe.wait_ge(s.xnT_ready, n + 1)
                for e in range(NE):
                    step = at(n, NE, e)
                    for h, mat, part, freed in (("g3", 1, 0, s.t3g_ready), ("g1", 0, 0, s.pg_ready),
                                                ("l3", 1, 1, s.t3l_ready), ("l1", 0, 1, s.pl_ready)):
                        wait(pe, freed, step)
                        nc.tensor.matmul(buf.ps_h[h][:, :], w.w13T[:, mat, ORDER[e], part, :], r.xnT[p][:, :],
                                         start=True, stop=True).then_inc(h_full[h], 1)
                    if not (isinstance(j, int) and j == 0 and e < 2):
                        outputs(*before(*before(j, p, e)))
                    if more and e == 3:
                        route.pe_transpose(pe, j + 1, n + 1, 1 - p)
                    if more and e == 4:
                        route.pe_logits(pe, j + 1, n + 1, 1 - p)
                    if more and e == 7:
                        route.pe_cwT(pe, j + 1, n + 1, 1 - p)

            route.pe_transpose(pe, 0, base, 0)
            route.pe_logits(pe, 0, base, 0)
            route.pe_cwT(pe, 0, base, 0)
            in_trips(pe, trip)
            outputs(TRIPS - 1, 1, NE - 2)
            outputs(TRIPS - 1, 1, NE - 1)

        if call == 1:
            @block.sync
            def _(sp):
                load_silu_weights(nc, sp, io, K.w1, K.s1.loaded)

        @block.scalar
        def _(act):
            def trip(j, p):
                n = base + j
                more = not (isinstance(j, int) and j == TRIPS - 1)
                for e in range(NE):
                    step = at(n, NE, e)
                    b = (p + e) % 2
                    x = ORDER[e]
                    act.wait_ge(s.full_g3, step + 1)
                    wait(act, s.pg_ready, step)
                    nc.scalar.activation(buf.t3["g"][:, :], buf.ps_h["g3"][:, :], ACT.Identity, bias=w.b3[:, x, 0:1]).then_inc(s.t3g_ready, 1)
                    act.wait_ge(s.full_l3, step + 1)
                    wait(act, s.pl_ready, step)
                    nc.scalar.activation(buf.t3["l"][:, :], buf.ps_h["l3"][:, :], ACT.Identity, bias=w.b3[:, x, 1:2]).then_inc(s.t3l_ready, 1)
                    act.wait_ge(s.g_ready, step + 1)
                    wait(act, s.a_ready, step - 1)
                    nc.scalar.activation(buf.sig[b][:, :], buf.g[b][:, :], ACT.Sigmoid, scale=1.702).then_inc(s.sig_ready, 1)
                    if more and e == 3:
                        route.act_xnT(act, j + 1, n + 1, 1 - p)
                    if more and e == 5:
                        route.act_exp(act, j + 1, n + 1, 1 - p)
                    if more and e == 7:
                        route.act_cwT(act, j + 1, n + 1, 1 - p)

            route.act_xnT(act, 0, base, 0)
            route.act_exp(act, 0, base, 0)
            route.act_cwT(act, 0, base, 0)
            in_trips(act, trip)

        @block.gpsimd
        def _(pool):
            def trip(j, p):
                n = base + j
                more = not (isinstance(j, int) and j == TRIPS - 1)
                for e in range(NE):
                    step = at(n, NE, e)
                    b = (p + e) % 2
                    wait(pool, s.gl_ready, step - 1)
                    wait_alone(pool, s.pl_ready, step + 1, s.passed)
                    nc.gpsimd.tensor_scalar(buf.l[b][:, :], buf.prod_l[b][:, :], 7.0, -7.0, ALU.min, ALU.max).then_inc(s.l_ready, 1)
                    if more and e == 1:
                        route.pool_rstd(pool, j + 1, n + 1, 1 - p)

            route.pool_rstd(pool, 0, base, 0)
            in_trips(pool, trip)

        @block.vector
        def _(dve):
            def activate(j, p, e):
                step = at(base + j, NE, e)
                b = (p + e) % 2
                dve.wait_ge(s.l_ready, step + 1)
                dve.wait_ge(s.g_ready, step + 1)
                wait(dve, s.a_ready, step)
                nc.vector.scalar_tensor_tensor(out=buf.gl[:, :], in0=buf.l[b][:, :], scalar=1.0, in1=buf.g[b][:, :],
                                               op0=ALU.add, op1=ALU.mult).then_inc(s.gl_ready, 1)
                dve.wait_ge(s.sig_ready, step + 1)
                dve.wait_ge(s.gl_ready, step + 1)
                wait(dve, s.y_full, step - 1)
                nc.vector.tensor_tensor(buf.a[b][:, :], buf.gl[:, :], buf.sig[b][:, :], ALU.mult).then_inc(s.a_ready, 1)

            def trip(j, p):
                n = base + j
                more = not (isinstance(j, int) and j == TRIPS - 1)
                first = isinstance(j, int) and j == 0
                for e in range(NE):
                    step = at(n, NE, e)
                    b = (p + e) % 2
                    x = ORDER[e]
                    dve.wait_ge(s.t3g_ready, step + 1)
                    dve.wait_ge(s.full_g1, step + 1)
                    nc.vector.scalar_tensor_tensor(out=buf.prod_g[:, :], in0=buf.ps_h["g1"][:, :], scalar=w.b1[:, x, 0:1],
                                                   in1=buf.t3["g"][:, :], op0=ALU.add, op1=ALU.mult).then_inc(s.pg_ready, 1)
                    dve.wait_ge(s.t3l_ready, step + 1)
                    dve.wait_ge(s.full_l1, step + 1)
                    nc.vector.scalar_tensor_tensor(out=buf.prod_l[b][:, :], in0=buf.ps_h["l1"][:, :], scalar=w.b1[:, x, 1:2],
                                                   in1=buf.t3["l"][:, :], op0=ALU.add, op1=ALU.mult).then_inc(s.pl_ready, 1)
                    dve.wait_ge(s.pg_ready, step + 1)
                    wait(dve, s.sig_ready, step - 1)
                    nc.vector.tensor_scalar(buf.g[b][:, :], buf.prod_g[:, :], 7.0, None, ALU.min).then_inc(s.g_ready, 1)
                    if not (first and e == 0):
                        activate(*before(j, p, e))
                    if not (first and e <= 2):
                        jj, pp, ee = before(*before(*before(j, p, e)))
                        expert_sum(nc, dve, s, r, buf, X, jj, base + jj, pp, ee)
                    if more and e == 1:
                        route.dve_stats(dve, j + 1, n + 1, 1 - p)
                    if more and e == 2:
                        route.dve_normalise(dve, j + 1, n + 1, 1 - p)
                    if more and e == 5:
                        route.dve_shift(dve, j + 1, n + 1, 1 - p)
                    if more and e == 6:
                        route.dve_top2(dve, j + 1, n + 1, 1 - p)

            nc.vector.memset(r.cw[0][:, :, E:NE], 1.0)
            nc.vector.memset(r.cw[1][:, :, E:NE], 1.0)
            route.dve_stats(dve, 0, base, 0)
            route.dve_normalise(dve, 0, base, 0)
            route.dve_shift(dve, 0, base, 0)
            route.dve_top2(dve, 0, base, 0)
            in_trips(dve, trip)
            last = (TRIPS - 1, 1, NE - 1)
            activate(*last)
            for jj, pp, ee in (before(*before(*last)), before(*last), last):
                expert_sum(nc, dve, s, r, buf, X, jj, base + jj, pp, ee)


def silu_stage(nc, K, call):
    CH = 4
    X, c, w, s, base = K.X, K.c, K.w1, K.s1, call * TRIPS
    with ExitStack() as ctx:
        sb = lambda name, shape, dt=F32: ctx.enter_context(nc.sbuf_tensor(f"s{call}_{name}", shape, dt))
        ps = lambda name: ctx.enter_context(nc.psum_tensor(f"s{call}_{name}", [P, 512], F32))
        r = route_buffers(sb, ps, 1)
        buf = Named()
        buf.ps_h = [ps(f"ps_h{k}") for k in range(CH)]
        buf.ps_y = [ps(f"ps_y{i}") for i in range(2)]
        buf.a = [sb(f"a{i}", [P, CH, BLOCK]) for i in range(2)]
        buf.acc = sb("acc", [P, GROUP, D])
        w_hi, w_lo = (sb(f"w_{n}", [P, NE, 512], F32R) for n in ("hi", "lo"))
        x_hi, x_lo = ([sb(f"x_{n}{i}", [P, BLOCK], F32R) for i in range(2)] for n in ("hi", "lo"))
        route = Route(nc, 1, X, r, s, c, w)
        block = ctx.enter_context(nc.Block())

        def before(j, p, e):
            return (j, p, e - 1) if e else (j - 1, 1 - p, NE - 1)

        @block.tensor
        def _(pe):
            def outputs(j, p, e):
                n = base + j
                step = at(n, NE, e)
                b = (p + e) % 2
                wait(pe, s.y_done, step - 1)
                for k in range(CH):
                    pe.wait_ge(s.a_ready[k], step + 1)
                    for t in range(GROUP):
                        last = nc.tensor.matmul(buf.ps_y[b][:, t * D:(t + 1) * D], buf.a[b][:, k, t * P:(t + 1) * P],
                                                w.we2[:, ORDER[e], k, :], start=(k == 0 and t == 0),
                                                stop=(e > 0 and k == CH - 1), skip_group_check=True)
                if e == 0:
                    pe.wait_ge(s.cwT_ready, n + 1)
                    for t in range(GROUP):
                        last = nc.tensor.matmul(buf.ps_y[b][:, t * D:(t + 1) * D], r.cwT[p][:, t * P:(t + 1) * P], w.be2[:, :],
                                                start=False, stop=True, skip_group_check=True)
                last.then_inc(s.y_full, 1)

            def trip(j, p):
                n = base + j
                more = not (isinstance(j, int) and j == TRIPS - 1)
                pe.wait_ge(s.x_parts, n + 1)
                for e in range(NE):
                    step = at(n, NE, e)
                    if isinstance(j, int) and j == 0:
                        pe.wait_ge(s.w_parts, at(call, NE, e + 1))
                    for k in range(CH):
                        wait(pe, s.a_ready[k], step)
                        chunk = slice(k * P, (k + 1) * P)
                        nc.tensor.matmul(buf.ps_h[k][:, :], w_hi[:, ORDER[e], chunk], x_hi[p][:, :], start=True, stop=False)
                        nc.tensor.matmul(buf.ps_h[k][:, :], w_hi[:, ORDER[e], chunk], x_lo[p][:, :], start=False, stop=False)
                        nc.tensor.matmul(buf.ps_h[k][:, :], w_lo[:, ORDER[e], chunk], x_hi[p][:, :], start=False, stop=True).then_inc(s.h_full[k], 1)
                    if not (isinstance(j, int) and j == 0 and e == 0):
                        outputs(*before(j, p, e))
                    if more and e == 2:
                        route.pe_transpose(pe, j + 1, n + 1, 1 - p)
                    if more and e == 3:
                        route.pe_hidden(pe, j + 1, n + 1, 1 - p)
                    if more and e == 4:
                        route.pe_logits(pe, j + 1, n + 1, 1 - p)
                    if more and e == 8:
                        route.pe_cwT(pe, j + 1, n + 1, 1 - p)

            route.pe_transpose(pe, 0, base, 0)
            route.pe_hidden(pe, 0, base, 0)
            route.pe_logits(pe, 0, base, 0)
            route.pe_cwT(pe, 0, base, 0)
            in_trips(pe, trip)
            outputs(TRIPS - 1, 1, NE - 1)

        @block.scalar
        def _(act):
            def x_high(n, p):
                wait(act, s.y_full, at(n - 1, NE, -1))
                nc.scalar.copy(x_hi[p][:, :], r.ps_x[:, :]).then_inc(s.x_high, 1)

            for e in range(NE):
                nc.scalar.copy(w_hi[:, ORDER[e], :], w.we1[:, ORDER[e], :]).then_inc(s.w_high, 1)

            def trip(j, p):
                n = base + j
                more = not (isinstance(j, int) and j == TRIPS - 1)
                for e in range(NE):
                    step = at(n, NE, e)
                    b = (p + e) % 2
                    wait(act, s.y_full, step - 1)
                    for k in range(CH):
                        act.wait_ge(s.h_full[k], step + 1)
                        nc.scalar.activation(buf.a[b][:, k, :], buf.ps_h[k][:, :], ACT.Silu,
                                             bias=w.be1[:, ORDER[e], k:k + 1]).then_inc(s.a_ready[k], 1)
                    if more and e == 2:
                        route.act_xnT(act, j + 1, n + 1, 1 - p)
                        x_high(n + 1, 1 - p)
                    if more and e == 3:
                        route.act_hidden(act, j + 1, n + 1, 1 - p)
                    if more and e == 5:
                        route.act_exp(act, j + 1, n + 1, 1 - p)
                        route.act_pair(act, j + 1, n + 1, 1 - p)
                    if more and e == 8:
                        route.act_cwT(act, j + 1, n + 1, 1 - p)

            route.act_xnT(act, 0, base, 0)
            x_high(base, 0)
            route.act_hidden(act, 0, base, 0)
            route.act_exp(act, 0, base, 0)
            route.act_pair(act, 0, base, 0)
            route.act_cwT(act, 0, base, 0)
            in_trips(act, trip)

        @block.gpsimd
        def _(pool):
            def trip(j, p):
                n = base + j
                route.pool_rstd(pool, j, n, p)
                pool.wait_ge(s.x_high, n + 1)
                nc.gpsimd.tensor_tensor(x_lo[p][:, :], r.xnT[p][:, :], x_hi[p][:, :].bitcast(F32), ALU.subtract).then_inc(s.x_parts, 1)

            in_trips(pool, trip)

        @block.vector
        def _(dve):
            def trip(j, p):
                n = base + j
                more = not (isinstance(j, int) and j == TRIPS - 1)
                for e in range(NE):
                    if not (isinstance(j, int) and j == 0 and e == 0):
                        jj, pp, ee = before(j, p, e)
                        expert_sum(nc, dve, s, r, buf, X, jj, base + jj, pp, ee)
                    if more and e == 0:
                        route.dve_stats(dve, j + 1, n + 1, 1 - p)
                    if more and e == 1:
                        route.dve_normalise(dve, j + 1, n + 1, 1 - p)
                    if more and e == 4:
                        route.dve_shift(dve, j + 1, n + 1, 1 - p)
                        route.dve_top2(dve, j + 1, n + 1, 1 - p)
                        route.dve_pair(dve, j + 1, n + 1, 1 - p)

            nc.vector.memset(r.cw[0][:, :, E:NE], 1.0)
            nc.vector.memset(r.cw[1][:, :, E:NE], 1.0)
            route.dve_stats(dve, 0, base, 0)
            route.dve_normalise(dve, 0, base, 0)
            route.dve_shift(dve, 0, base, 0)
            route.dve_top2(dve, 0, base, 0)
            route.dve_pair(dve, 0, base, 0)
            for e in range(NE):
                dve.wait_ge(s.w_high, at(call, NE, e + 1))
                nc.vector.tensor_tensor(w_lo[:, ORDER[e], :], w.we1[:, ORDER[e], :], w_hi[:, ORDER[e], :].bitcast(F32), ALU.subtract).then_inc(s.w_parts, 1)
            in_trips(dve, trip)
            expert_sum(nc, dve, s, r, buf, X, TRIPS - 1, base + TRIPS - 1, 1, NE - 1)
BACKS = 8
SOFT_STEPS = 4


def in_tile_pairs(eng, one_tile):
    one_tile(0, 0)
    one_tile(1, 1)
    with eng.Fori(1, TILES // 2 - 1) as i:
        one_tile(2 * i, 0)
        one_tile(2 * i + 1, 1)
    one_tile(TILES - 2, 0)
    one_tile(TILES - 1, 1)


def memory_attention_stage(nc, K, io):
    X, c = K.X, K.c
    SCALE = DH ** -0.5
    AUG = DH + 1
    with ExitStack() as ctx:
        sb = lambda name, shape, dt=F32: ctx.enter_context(nc.sbuf_tensor(f"m_{name}", shape, dt))
        w_qkv = sb("w_qkv", [P, 3 * INNER])
        w_rot = sb("w_rot", [P, 2 * INNER])
        w_out = sb("w_out", [P, PAIRS, D])
        ln_g, ln_b = sb("ln_g", [P, 1]), sb("ln_b", [P, 1])
        beta_in, beta, one_less_beta = (sb(n, [P, HEADS]) for n in ("beta_in", "beta", "one_less_beta"))
        cos, sin = sb("cos", [P, P]), sb("sin", [P, P])
        causal = sb("causal", [P, SEG])
        mem = sb("mem", [P, BATCH, PAIRS, 2 * AUG])
        stats, mv = sb("stats", [P, 2, 6]), sb("mv", [P, 2, 2])
        var, rstd = sb("var", [P, 2]), sb("rstd", [P, 2])
        xn1, xn2 = sb("xn1", [P, D]), sb("xn2", [P, D])
        xnT = sb("xnT", [P, P])
        raw = [sb(f"raw_{n}", [P, PAIRS, P]) for n in "qk"]
        turned = [sb(f"turned_{n}", [P, PAIRS, P]) for n in "qk"]
        roped = [sb(f"roped_{n}", [P, PAIRS, P]) for n in "qk"]
        relu = [sb(f"relu{i}", [P, INNER]) for i in range(2)]
        expo = [sb(f"expo{i}", [P, INNER]) for i in range(2)]
        phi_qT = [sb(f"phi_qT{i}", [P, PAIRS, P]) for i in range(2)]
        phi_kT = [sb(f"phi_kT{i}", [P, PAIRS, P]) for i in range(2)]
        phi_k = [sb(f"phi_k{i}", [P, INNER]) for i in range(2)]
        v = [sb(f"v{i}", [P, INNER]) for i in range(2)]
        local = [sb(f"local{i}", [P, INNER]) for i in range(2)]
        s_sb, e_sb, eT = (sb(n, [P, HEADS, SEG]) for n in ("scores", "exps", "expsT"))
        smax, ssum, srec = (sb(n, [P, HEADS]) for n in ("smax", "ssum", "srec"))
        u = sb("u", [P, HEADS, AUG])
        rden = sb("rden", [P, 4, 2, 4])
        held = sb("held", [P, 2, 2, 4, DH])
        o, o_sum = sb("o", [P, INNER]), sb("o_sum", [P, INNER])
        oT = sb("oT", [P, PAIRS, P])
        front_ps = [ctx.enter_context(nc.psum_tensor(f"m_front{i}", [P, 512], F32)) for i in range(4)]
        back_ps = ctx.enter_context(nc.psum_tensor("m_back", [P, 4, 512], F32))
        s = stage_sems(nc, ctx, "m", "loaded emptied set_up passed ln_stats ln_mv ln_var ln_rstd xn1_ready xn2_ready xnT_full xnT_ready "
                                    "q_full k_full tok_full v_full scores_full local_full q_copied k_copied tok_read v_copied rot_done cos_done "
                                    "rope_done elu_ready phi_ready scores_read soft_step soft_shift soft_exp pT_ready local_ready "
                                    "back_full back_step u_ready o_ready o_sum_ready mem_done oT_ready x_done")
        block = ctx.enter_context(nc.Block())
        wide = lambda table: table[:, :].unsqueeze(1)
        halves = lambda ap: ap.rearrange("p (c r) d -> p r c d", r=2)
        LOADS = 9

        @block.sync
        def _(sp):
            with nc.allow_non_contiguous_dma(reason="one element per partition"):
                for dst, src in ((w_qkv[:, :], io["L0_attn_w_qkv"]), (w_out[:, :, :], io["L0_attn_w_out"].rearrange("(c p) d -> p c d", p=P)),
                                 (ln_g[:, :], io["L0_attn_ln_g"].unsqueeze(1)), (ln_b[:, :], io["L0_attn_ln_b"].unsqueeze(1)),
                                 (beta_in[:, :], io["L0_attn_mem_beta"].rearrange("a h b c -> (a h b c)").partition_broadcast(P)),
                                 (cos[:, :], io["c_cos"]), (sin[:, :], io["c_sin"]), (causal[:, :], io["c_causal"])):
                    sp.dma_start(dst, src).then_inc(s.loaded, 16)
            sp.wait_ge(s.loaded, 16 * (LOADS - 1))

        @block.tensor
        def _(pe):
            def fill(bank, weights, column, full):
                for k in range(4):
                    last = nc.tensor.matmul(front_ps[bank][:, k * P:(k + 1) * P], weights[:, column + k * P:column + (k + 1) * P], xnT[:, :],
                                            start=(k == 0), stop=True, skip_group_check=True)
                last.then_inc(full, 1)

            def fill_tokens(bank, column, full):
                nc.tensor.matmul(front_ps[bank][:, :], xnT[:, :], w_qkv[:, column:column + 512], start=True, stop=True).then_inc(full, 1)

            def turn_x(f):
                pe.wait_ge(s.xn2_ready, f + 1)
                wait(pe, s.v_copied, at(f, 2, -1))
                nc.tensor.transpose(front_ps[0][:, 0:P], xn2[:, :], c.ident[:, :]).then_inc(s.xnT_full, 1)

            def fill_q(f):
                pe.wait_ge(s.xnT_ready, f + 1)
                fill(0, w_qkv, 0, s.q_full)
                wait(pe, s.scores_read, f)
                fill(1, w_rot, 0, s.q_full)
                wait(pe, s.v_copied, at(f, 2, 0))
                fill(2, w_qkv, 512, s.q_full)
                fill(3, w_rot, 512, s.q_full)

            def fill_k(f, halves=(0, 1)):
                for half in halves:
                    pe.wait_ge(s.q_copied, at(f, 2, half + 1))
                    fill(2 * half, w_qkv, INNER + 512 * half, s.k_full)
                    pe.wait_ge(s.rot_done, at(f, 4, half + 1))
                    fill(2 * half + 1, w_rot, INNER + 512 * half, s.k_full)

            def fill_k_tokens(f, halves=(0, 1)):
                for half in halves:
                    pe.wait_ge(s.k_copied, at(f, 2, half + 1))
                    fill_tokens(2 * half, INNER + 512 * half, s.tok_full)

            def fill_v(f, halves=(0, 1)):
                for half in halves:
                    pe.wait_ge(s.tok_read, at(f, 2, half + 1))
                    fill_tokens(2 * half, 2 * INNER + 512 * half, s.v_full)

            def scores(f):
                if isinstance(f, int) and f == 0:
                    pe.wait_ge(s.rot_done, 4)
                else:
                    wait_alone(pe, s.local_ready, f, s.passed)
                wait_alone(pe, s.rope_done, at(f, 2, 2), s.passed)
                for h in range(HEADS):
                    rows = slice(DH * (h % 2), DH * (h % 2 + 1))
                    for b in range(BATCH):
                        seg = slice(SEG * b, SEG * (b + 1))
                        last = nc.tensor.matmul(front_ps[1 + 2 * (h % 2)][seg, (h // 2) * SEG:(h // 2 + 1) * SEG], roped[0][rows, h // 2, seg],
                                                roped[1][rows, h // 2, seg], start=True, stop=True, skip_group_check=True)
                last.then_inc(s.scores_full, 1)

            def softmax_values(w, p, more):
                if more:
                    wait_alone(pe, s.rot_done, at(w + 1, 4, 4), s.passed)
                wait_alone(pe, s.v_copied, at(w, 2, 2), s.passed)
                wait_alone(pe, s.pT_ready, w + 1, s.passed)
                for h in range(HEADS):
                    for b in range(BATCH):
                        seg = slice(SEG * b, SEG * (b + 1))
                        last = nc.tensor.matmul(front_ps[1 + 2 * (h // 8)][seg, (h % 8) * DH:(h % 8 + 1) * DH], eT[seg, h, :],
                                                v[p][seg, h * DH:(h + 1) * DH], start=True, stop=True, skip_group_check=True)
                last.then_inc(s.local_full, 1)

            def recall(phiT, half):
                for k in range(4):
                    for b in range(BATCH):
                        seg = slice(SEG * b, SEG * (b + 1))
                        last = nc.tensor.matmul(back_ps[seg, 2 * half + k // 2, k % 2 * 2 * AUG:(k % 2 + 1) * 2 * AUG], phiT[:, 4 * half + k, seg],
                                                mem[:, b, 4 * half + k, :], start=True, stop=True, skip_group_check=True)
                last.then_inc(s.back_full, 1)

            def back_a(w, p):
                wait(pe, s.mem_done, 2 * w)
                wait(pe, s.x_done, w)
                wait_alone(pe, s.phi_ready, at(w, 3, 3), s.passed)
                recall(phi_kT[p], 0)
                recall(phi_kT[p], 1)

            def back_b(w, p):
                for half in range(2):
                    wait_alone(pe, s.u_ready, at(w, 2, half + 1), s.passed)
                    recall(phi_qT[p], half)

            def back_c(w, p, half):
                if half == 0:
                    wait_alone(pe, s.o_ready, at(w, 2, 2), s.passed)
                else:
                    wait_alone(pe, s.mem_done, at(w, 2, 1), s.passed)
                for k in range(4):
                    for r in range(2):
                        h = 2 * (4 * half + k) + r
                        for b in range(BATCH):
                            seg = slice(SEG * b, SEG * (b + 1))
                            last = nc.tensor.matmul(back_ps[DH * r:DH * (r + 1), b, k * AUG:(k + 1) * AUG], phi_k[p][seg, h * DH:(h + 1) * DH],
                                                    u[seg, h, :], start=True, stop=True, skip_group_check=True)
                last.then_inc(s.back_full, 1)

            def turn_o(w):
                wait(pe, s.mem_done, at(w, 2, 2))
                pe.wait_ge(s.o_sum_ready, w + 1)
                for k in range(PAIRS):
                    last = nc.tensor.transpose(back_ps[:, k // 4, (k % 4) * P:(k % 4 + 1) * P], o_sum[:, k * P:(k + 1) * P], c.ident[:, :])
                last.then_inc(s.back_full, 1)

            def project(w):
                pe.wait_ge(s.oT_ready, w + 1)
                for k in range(PAIRS):
                    last = nc.tensor.matmul(back_ps[:, 2, 0:D], oT[:, k, :], w_out[:, k, :], start=(k == 0), stop=(k == PAIRS - 1))
                last.then_inc(s.back_full, 1)

            def tile(w, p):
                more = not (isinstance(w, int) and w == TILES - 1)
                back_a(w, p)
                if more:
                    fill_q(w + 1)
                back_b(w, p)
                if more:
                    fill_k(w + 1)
                back_c(w, p, 0)
                if more:
                    fill_k_tokens(w + 1)
                softmax_values(w, p, more)
                back_c(w, p, 1)
                if more:
                    fill_v(w + 1)
                turn_o(w)
                if more:
                    scores(w + 1)
                project(w)
                if more and not (isinstance(w, int) and w == TILES - 2):
                    turn_x(w + 2)

            pe.wait_ge(s.set_up, 4)
            turn_x(0)
            fill_q(0)
            fill_k(0)
            fill_k_tokens(0)
            fill_v(0)
            scores(0)
            turn_x(1)
            in_tile_pairs(pe, tile)

        @block.scalar
        def _(act):
            def elu_parts(f, k, b, source):
                wait(act, s.phi_ready, at(f, 3, -k))
                nc.scalar.activation(relu[b][:, :], source, ACT.Relu)
                nc.scalar.activation(expo[b][:, :], source, ACT.Exp).then_inc(s.elu_ready, 1)

            def copy_x(f):
                act.wait_ge(s.xnT_full, f + 1)
                nc.scalar.activation(xnT[:, :], front_ps[0][:, 0:P], ACT.Identity, bias=ln_b[:, :], scale=ln_g[:, :]).then_inc(s.xnT_ready, 1)

            def front(f, p):
                for k, full, copied in ((0, s.q_full, s.q_copied), (1, s.k_full, s.k_copied)):
                    wait(act, s.cos_done, at(f, 2, k) - 1)
                    for half in range(2):
                        act.wait_ge(full, at(f, 4, 2 * half + 1))
                        nc.scalar.copy(raw[k][:, 4 * half:4 * half + 4, :], front_ps[2 * half][:, :].rearrange("p (k t) -> p k t", t=P)).then_inc(copied, 1)
                    act.wait_ge(copied, at(f, 2, 2))
                    elu_parts(f, k, k, raw[k][:, :, :].rearrange("p k t -> p (k t)"))
                wait(act, s.phi_ready, at(f, 3, 1))
                for half in range(2):
                    act.wait_ge(s.tok_full, at(f, 2, half + 1))
                    cols = slice(512 * half, 512 * half + 512)
                    nc.scalar.activation(relu[0][:, cols], front_ps[2 * half][:, :], ACT.Relu)
                    nc.scalar.activation(expo[0][:, cols], front_ps[2 * half][:, :], ACT.Exp).then_inc(s.tok_read, 1)
                wait(act, s.local_full, f - 1)
                wait(act, s.u_ready, at(f, 2, -2))
                for half in range(2):
                    act.wait_ge(s.v_full, at(f, 2, half + 1))
                    nc.scalar.copy(v[p][:, 512 * half:512 * half + 512], front_ps[2 * half][:, :]).then_inc(s.v_copied, 1)

            def soft_exp(w):
                act.wait_ge(s.soft_shift, w + 1)
                nc.scalar.activation(e_sb[:, :, :], s_sb[:, :, :], ACT.Exp).then_inc(s.soft_exp, 1)

            def back(w):
                act.wait_ge(s.back_full, at(w, BACKS, 7))
                nc.scalar.copy(oT[:, :, :].rearrange("p k t -> p (k t)"), back_ps[:, 0:2, :].rearrange("p k t -> p (k t)")).then_inc(s.oT_ready, 1)

            def tile(w, p):
                more = not (isinstance(w, int) and w == TILES - 1)
                soft_exp(w)
                if more:
                    front(w + 1, 1 - p)
                back(w)
                if more and not (isinstance(w, int) and w == TILES - 2):
                    copy_x(w + 2)

            act.wait_ge(s.loaded, 16 * (LOADS - 1))
            nc.scalar.activation(beta[:, :], beta_in[:, :], ACT.Sigmoid).then_inc(s.set_up, 1)
            copy_x(0)
            front(0, 0)
            copy_x(1)
            in_tile_pairs(act, tile)

        @block.gpsimd
        def _(pool):
            def rstd_of(f, m):
                pool.wait_ge(s.ln_mv, at(f, 2, m + 1))
                nc.gpsimd.tensor_tensor(var[:, m:m + 1], mv[:, m, 1:2], c.eps[:, 0:1], ALU.add).then_inc(s.ln_var, 1)
                pool.wait_ge(s.ln_var, at(f, 2, m + 1))
                nc.gpsimd.tensor_tensor(rstd[:, m:m + 1], var[:, m:m + 1], c.minus_half[:, 0:1], ALU.pow).then_inc(s.ln_rstd, 1)

            def rope(f, k):
                copied = (s.q_copied, s.k_copied)[k]
                pool.wait_ge(copied, at(f, 2, 2))
                wait(pool, s.scores_full, f)
                nc.gpsimd.tensor_tensor(roped[k][:, :, :], raw[k][:, :, :], wide(cos).broadcast_to([P, PAIRS, P]), ALU.mult).then_inc(s.cos_done, 1)
                pool.wait_ge(s.cos_done, at(f, 2, k + 1))
                pool.wait_ge(s.rot_done, at(f, 4, 2 * k + 2))
                nc.gpsimd.tensor_tensor(roped[k][:, :, :], roped[k][:, :, :], turned[k][:, :, :], ALU.add).then_inc(s.rope_done, 1)

            def tile(w, p):
                more = not (isinstance(w, int) and w == TILES - 1)
                norm = more and not (isinstance(w, int) and w == TILES - 2)
                if norm:
                    rstd_of(w + 2, 0)
                if more:
                    rope(w + 1, 0)
                if norm:
                    rstd_of(w + 2, 1)
                if more:
                    rope(w + 1, 1)
                pool.wait_ge(s.local_ready, w + 1)
                nc.gpsimd.tensor_tensor(o_sum[:, :], o[:, :], local[p][:, :], ALU.add).then_inc(s.o_sum_ready, 1)

            for f in range(2):
                rstd_of(f, 0)
                rstd_of(f, 1)
            rope(0, 0)
            rope(0, 1)
            in_tile_pairs(pool, tile)

        @block.vector
        def _(dve):
            def stats_of(f, m, source):
                nc.vector.bn_stats(stats[:, m, :], source).then_inc(s.ln_stats, 1)
                wait_alone(dve, s.ln_stats, at(f, 2, m + 1), s.passed)
                nc.vector.bn_aggr(mv[:, m, :], stats[:, m, :]).then_inc(s.ln_mv, 1)

            def norm_1(f):
                stats_of(f, 0, X[:, f, :])

            def norm_2(f):
                dve.wait_ge(s.ln_rstd, at(f, 2, 1))
                nc.vector.tensor_scalar(xn1[:, :], X[:, f, :], mv[:, 0, 0:1], rstd[:, 0:1], ALU.subtract, ALU.mult).then_inc(s.xn1_ready, 1)
                wait_alone(dve, s.xn1_ready, f + 1, s.passed)
                stats_of(f, 1, xn1[:, :])

            def norm_3(f):
                dve.wait_ge(s.ln_rstd, at(f, 2, 2))
                wait(dve, s.xnT_full, f)
                nc.vector.tensor_scalar(xn2[:, :], xn1[:, :], mv[:, 1, 0:1], rstd[:, 1:2], ALU.subtract, ALU.mult).then_inc(s.xn2_ready, 1)

            def front_rope(f, k):
                wait(dve, s.rope_done, at(f, 2, k) - 1)
                for half in range(2):
                    dve.wait_ge((s.q_full, s.k_full)[k], at(f, 4, 2 * half + 2))
                    nc.vector.tensor_tensor(turned[k][:, 4 * half:4 * half + 4, :], front_ps[2 * half + 1][:, :].rearrange("p (k t) -> p k t", t=P),
                                            wide(sin).broadcast_to([P, 4, P]), ALU.mult).then_inc(s.rot_done, 1)

            def front_phi(f, p, k):
                if k < 2:
                    dve.wait_ge(s.elu_ready, at(f, 2, k + 1))
                else:
                    dve.wait_ge(s.tok_read, at(f, 2, 2))
                out = (phi_qT[p][:, :, :].rearrange("p k t -> p (k t)"), phi_kT[p][:, :, :].rearrange("p k t -> p (k t)"), phi_k[p][:, :])[k]
                nc.vector.scalar_tensor_tensor(out=out, in0=expo[k % 2][:, :], scalar=1.0, in1=relu[k % 2][:, :],
                                               op0=ALU.min, op1=ALU.add).then_inc(s.phi_ready, 1)

            def front_softmax_1(f):
                step = lambda k: at(f, SOFT_STEPS, k)
                by_half = halves(s_sb[:, :, :])
                dve.wait_ge(s.scores_full, f + 1)
                wait(dve, s.soft_exp, f)
                for r in range(2):
                    last = nc.vector.scalar_tensor_tensor(out=by_half[:, r], in0=front_ps[1 + 2 * r][:, 0:PAIRS * SEG].rearrange("p (c m) -> p c m", m=SEG),
                                                          scalar=SCALE, in1=causal[:, :].unsqueeze(1).broadcast_to([P, PAIRS, SEG]),
                                                          op0=ALU.mult, op1=ALU.add)
                last.then_inc(s.scores_read, 1)
                dve.wait_ge(s.scores_read, f + 1)
                nc.vector.tensor_reduce(smax[:, :], s_sb[:, :, :], AX.X, ALU.max).then_inc(s.soft_step, 1)
                dve.wait_ge(s.soft_step, step(1))
                nc.vector.tensor_tensor(s_sb[:, :, :], s_sb[:, :, :], smax[:, :].unsqueeze(2).broadcast_to([P, HEADS, SEG]),
                                        ALU.subtract).then_inc(s.soft_shift, 1)

            def front_softmax_2(f):
                step = lambda k: at(f, SOFT_STEPS, k)
                dve.wait_ge(s.soft_exp, f + 1)
                wait(dve, s.local_full, f)
                nc.vector.transpose(eT[:, :, :].rearrange("p h m -> p (h m)"), e_sb[:, :, :].rearrange("p h m -> p (h m)")).then_inc(s.pT_ready, 1)
                nc.vector.tensor_reduce(ssum[:, :], e_sb[:, :, :], AX.X, ALU.add).then_inc(s.soft_step, 1)
                dve.wait_ge(s.soft_step, step(2))
                nc.vector.reciprocal(srec[:, :], ssum[:, :]).then_inc(s.soft_step, 1)
                dve.wait_ge(s.soft_step, step(3))
                nc.vector.tensor_tensor(srec[:, :], srec[:, :], one_less_beta[:, :], ALU.mult).then_inc(s.soft_step, 1)
                dve.wait_ge(s.soft_step, step(4))

            def front_local(f, p):
                dve.wait_ge(s.local_full, f + 1)
                wait(dve, s.o_sum_ready, f - 1)
                for half, bank in ((0, 1), (1, 3)):
                    last = nc.vector.tensor_tensor(local[p][:, 512 * half:512 * half + 512].rearrange("p (h d) -> p h d", d=DH),
                                                   front_ps[bank][:, :].rearrange("p (h d) -> p h d", d=DH),
                                                   srec[:, 8 * half:8 * half + 8].unsqueeze(2).broadcast_to([P, 8, DH]), ALU.mult)
                last.then_inc(s.local_ready, 1)

            def answer(half):
                banks = back_ps[:, 2 * half:2 * half + 2, 0:4 * AUG].rearrange("p k (h e) -> p k h e", e=AUG)
                return banks[:, :, :, 0:DH], banks[:, :, :, DH]

            eight = lambda ap, half: ap[:, 8 * half:8 * half + 8].rearrange("p (k h) d -> p k h d", k=2)
            spread = lambda ap: ap.unsqueeze(3).broadcast_to([P, 2, 4, DH])

            def back_u(w, p, half):
                step = lambda k: at(w, 10, 2 * half + k)
                values, norms = answer(half)
                dve.wait_ge(s.back_full, at(w, BACKS, 1 + half))
                nc.vector.reciprocal(rden[:, half], norms).then_inc(s.back_step, 1)
                dve.wait_ge(s.back_step, step(1))
                nc.vector.tensor_tensor(held[:, half], values, spread(rden[:, half]), ALU.mult).then_inc(s.back_step, 1)
                dve.wait_ge(s.back_step, step(2))
                dve.wait_ge(s.v_copied, at(w, 2, 2))
                nc.vector.tensor_tensor(eight(u[:, :, 0:DH], half), eight(v[p][:, :].rearrange("p (h d) -> p h d", d=DH), half),
                                        held[:, half], ALU.subtract).then_inc(s.u_ready, 1)

            def back_o(w, half):
                step = lambda k: at(w, 10, 4 + 3 * half + k)
                values, norms = answer(half)
                dve.wait_ge(s.back_full, at(w, BACKS, 3 + half))
                if half == 0:
                    wait(dve, s.o_sum_ready, w)
                nc.vector.tensor_scalar(rden[:, 2 + half], norms, 1e-6, None, ALU.add).then_inc(s.back_step, 1)
                dve.wait_ge(s.back_step, step(1))
                nc.vector.reciprocal(rden[:, 2 + half], rden[:, 2 + half]).then_inc(s.back_step, 1)
                dve.wait_ge(s.back_step, step(2))
                nc.vector.tensor_tensor(rden[:, 2 + half], rden[:, 2 + half], beta[:, 8 * half:8 * half + 8].rearrange("p (k h) -> p k h", k=2),
                                        ALU.mult).then_inc(s.back_step, 1)
                dve.wait_ge(s.back_step, step(3))
                nc.vector.tensor_tensor(eight(o[:, :].rearrange("p (h d) -> p h d", d=DH), half), values, spread(rden[:, 2 + half]),
                                        ALU.mult).then_inc(s.o_ready, 1)

            def back_mem(w, half):
                dve.wait_ge(s.back_full, at(w, BACKS, 5 + half))
                for r in range(2):
                    part = mem[DH * r:DH * (r + 1), :, 4 * half:4 * half + 4, AUG * r:AUG * (r + 1)]
                    last = nc.vector.tensor_tensor(part, part, back_ps[DH * r:DH * (r + 1), :, 0:4 * AUG].rearrange("p b (c e) -> p b c e", e=AUG), ALU.add)
                last.then_inc(s.mem_done, 1)

            def back_x(w):
                dve.wait_ge(s.back_full, at(w, BACKS, 8))
                nc.vector.tensor_tensor(X[:, w, :], X[:, w, :], back_ps[:, 2, 0:D], ALU.add).then_inc(s.x_done, 1)

            def tile(w, p):
                more = not (isinstance(w, int) and w == TILES - 1)
                norm = more and not (isinstance(w, int) and w == TILES - 2)
                if norm:
                    norm_1(w + 2)
                front_softmax_1(w)
                for half in range(2):
                    back_u(w, p, half)
                front_softmax_2(w)
                if more:
                    front_rope(w + 1, 0)
                for half in range(2):
                    back_o(w, half)
                if norm:
                    norm_2(w + 2)
                if more:
                    front_phi(w + 1, 1 - p, 0)
                    front_rope(w + 1, 1)
                back_mem(w, 0)
                if norm:
                    norm_3(w + 2)
                front_local(w, p)
                if more:
                    front_phi(w + 1, 1 - p, 1)
                back_mem(w, 1)
                if more:
                    front_phi(w + 1, 1 - p, 2)
                back_x(w)

            nc.vector.memset(mem[:, :, :, :], 0.0).then_inc(s.emptied, 1)
            dve.wait_ge(s.emptied, 1)
            for r in range(2):
                last = nc.vector.memset(mem[DH * r:DH * (r + 1), :, :, AUG * r + DH:AUG * (r + 1)], 1e-6)
            last.then_inc(s.set_up, 1)
            nc.vector.memset(u[:, :, DH:AUG], 1.0)
            dve.wait_ge(s.loaded, 16 * (LOADS - 1))
            pairs = w_qkv[:, 0:2 * INNER].rearrange("p (i two) -> p i two", two=2)
            turned_w = w_rot[:, :].rearrange("p (i two) -> p i two", two=2)
            nc.vector.tensor_scalar(turned_w[:, :, 0], pairs[:, :, 1], -1.0, None, ALU.mult).then_inc(s.set_up, 1)
            nc.vector.tensor_copy(turned_w[:, :, 1], pairs[:, :, 0]).then_inc(s.set_up, 1)
            dve.wait_ge(s.set_up, 4)
            nc.vector.tensor_scalar(one_less_beta[:, :], beta[:, :], -1.0, 1.0, ALU.mult, ALU.add).then_inc(s.set_up, 1)
            for f in range(2):
                norm_1(f)
                norm_2(f)
                norm_3(f)
            front_rope(0, 0)
            front_phi(0, 0, 0)
            front_rope(0, 1)
            front_phi(0, 0, 1)
            front_phi(0, 0, 2)
            in_tile_pairs(dve, tile)
B_HEADS, B_DH = 8, 16
WINDOW = 3
WEIGHTS = ("L1_attn_Wq", "L1_attn_Wk", "L1_attn_Wv", "L1_attn_Wproj", "L1_attn_Wo")


def band_attention_stage(nc, K, io):
    with ExitStack() as ctx:
        sb = lambda name, shape, dt=F32: ctx.enter_context(nc.sbuf_tensor(f"b_{name}", shape, dt))
        A = Named()
        A.wT = sb("wT", [P, len(WEIGHTS), P])
        A.w1T, A.w2T = sb("w1T", [P, 64]), sb("w2T", [64, 1])
        A.qk_bias, A.v_bias, A.o_bias = sb("qk_bias", [P, 2, P]), sb("v_bias", [P, P]), sb("o_bias", [P, P])
        A.proj_bias, A.b1, A.b2 = sb("proj_bias", [P, 1]), sb("b1", [64, 1]), sb("b2", [P, 1])
        A.ones, A.row_ones = sb("ones", [P, P]), sb("row_ones", [P, P])
        A.band = sb("band", [P, 3, WINDOW * SEG])
        A.row_of = sb("row_of", [P, BATCH])
        A.tiny = sb("tiny", [P, 1])
        A.v = sb("v", [P, TILES + 2, P])
        A.qnT = K.w0.turned[:, 0:TILES, :]
        A.knT = sb("knT", [P, TILES + 2, P])
        A.head_of = sb("head_of", [P, B_HEADS])
        A.soft = [sb(f"soft_{n}", [P, TILES, P]) for n in "qk"]
        A.norms = sb("norms", [P, TILES, 2])
        A.use_inv = sb("use_inv", [P, 2])
        A.plogp = sb("plogp", [P, 1])
        A.joint = sb("joint", [P, B_HEADS // 2 * BATCH])
        A.gate = sb("gate", [P, 1])
        A.curv = sb("curv", [P, TILES])
        with ExitStack() as inner:
            A.xnT = inner.enter_context(nc.sbuf_tensor("b_xnT", [P, TILES * P], F32))
            A.invT = inner.enter_context(nc.sbuf_tensor("b_invT", [P, TILES * P], F32))
            band_projections(nc, K, A, io)
            band_queries(nc, K, A)
        band_entropies(nc, K, A)
        band_windows(nc, K, A)
        band_sum(nc, K, A)


def band_projections(nc, K, A, io):
    X, c = K.X, K.c
    with ExitStack() as ctx:
        sb = lambda name, shape, dt=F32: ctx.enter_context(nc.sbuf_tensor(f"bp_{name}", shape, dt))
        ps = lambda name: ctx.enter_context(nc.psum_tensor(f"bp_{name}", [P, 512], F32))
        natural, w1_natural = sb("natural", [P, len(WEIGHTS), P]), sb("w1_natural", [64, P])
        stats, mv, var, rstd = sb("stats", [P, GROUP, 6]), sb("mv", [P, GROUP, 2]), sb("var", [P, GROUP]), sb("rstd", [P, GROUP])
        xn, res = sb("xn", [P, GROUP, D]), sb("res", [P, BLOCK])
        xs = [sb(f"xs{i}", [P, BLOCK]) for i in range(2)]
        squares = [sb(f"squares{m}", [P, BLOCK]) for m in range(2)]
        x_ps, inv_ps, v_ps, n_ps, w_ps, w_ps2 = (ps(n) for n in ("x_ps", "inv_ps", "v_ps", "n_ps", "w_ps", "w_ps2"))
        s = stage_sems(nc, ctx, "bp", "weights loaded passed turned kept ln_stats ln_mv ln_var ln_rstd xn_ready x_full xs_ready inv_full inv_ready "
                                     "v_full v_ready res_ready squares_ready n_full n_ready sqrt_ready gauge_step gauge_full")
        block = ctx.enter_context(nc.Block())
        SMALL = 13

        @block.sync
        def _(sp):
            for k, name in enumerate(WEIGHTS):
                sp.dma_start(natural[:, k, :], io[name]).then_inc(s.weights, 16)
            sp.dma_start(w1_natural[:, :], io["L1_attn_W1"]).then_inc(s.weights, 16)
            with nc.allow_non_contiguous_dma(reason="one element per partition"):
                for dst, src in ((A.proj_bias[:, :], io["L1_attn_bproj"].unsqueeze(1)), (A.v_bias[:, :], io["L1_attn_bv"].partition_broadcast(P)),
                                 (A.qk_bias[:, 0, :], io["L1_attn_bq"].partition_broadcast(P)), (A.qk_bias[:, 1, :], io["L1_attn_bk"].partition_broadcast(P)),
                                 (A.o_bias[:, :], io["L1_attn_bo"].partition_broadcast(P)), (A.b1[:, :], io["L1_attn_b1"].unsqueeze(1)),
                                 (A.b2[:, :], io["L1_attn_b2"].partition_broadcast(P)), (A.w2T[:, :], io["L1_attn_W2"].rearrange("a k -> k a")),
                                 (A.row_ones[:, :], io["c_row_ones"]), (A.band[:, :, :], io["c_band"]), (A.row_of[:, :], io["c_row_of"]),
                                 (A.head_of[:, :], io["c_head_of"])):
                    sp.dma_start(dst, src).then_inc(s.loaded, 16)
            sp.wait_ge(s.loaded, 16 * (SMALL - 1))

        @block.tensor
        def _(pe):
            pe.wait_ge(s.weights, 16 * (len(WEIGHTS) + 1))
            for k in range(len(WEIGHTS)):
                bank = (w_ps, w_ps2)[k // 4]
                nc.tensor.transpose(bank[:, (k % 4) * P:(k % 4 + 1) * P], natural[:, k, :], c.ident[:, :])
            nc.tensor.transpose(w_ps2[:, P:P + 64], w1_natural[:, :], c.ident[0:64, 0:64]).then_inc(s.turned, 1)

            def turn_x(j):
                pe.wait_ge(s.xn_ready, j + 1)
                wait(pe, s.xs_ready, j)
                for t in range(GROUP):
                    last = nc.tensor.transpose(x_ps[:, t * P:(t + 1) * P], xn[:, t, :], c.ident[:, :])
                last.then_inc(s.x_full, 1)

            def trip(j, p):
                pe.wait_ge(s.xs_ready, j + 1)
                wait(pe, s.inv_ready, j)
                nc.tensor.matmul(inv_ps[:, :], A.wT[:, 3, :], xs[p][:, :], start=True, stop=True).then_inc(s.inv_full, 1)
                wait(pe, s.v_ready, j)
                for t in range(GROUP):
                    last = nc.tensor.matmul(v_ps[:, t * P:(t + 1) * P], xs[p][:, t * P:(t + 1) * P], A.wT[:, 2, :], start=(t == 0), stop=True,
                                            skip_group_check=True)
                last.then_inc(s.v_full, 1)
                if not (isinstance(j, int) and j == TRIPS - 1):
                    turn_x(j + 1)
                pe.wait_ge(s.squares_ready, at(j, 2, 2))
                wait(pe, s.n_ready, j)
                for t in range(GROUP):
                    for m in range(2):
                        last = nc.tensor.matmul(n_ps[:, 2 * t + m:2 * t + m + 1], squares[m][:, t * P:(t + 1) * P], A.ones[:, 0:1],
                                                start=(t == 0 and m == 0), stop=True, skip_group_check=True)
                last.then_inc(s.n_full, 1)

            pe.wait_ge(s.kept, 3)
            turn_x(0)
            in_trips(pe, trip)
            pe.wait_ge(s.gauge_step, 5)
            nc.tensor.matmul(n_ps[:, 0:1], A.ones[:, :], A.norms[:, 0, 0:1], start=True, stop=True).then_inc(s.gauge_full, 1)

        @block.scalar
        def _(act):
            def copy_x(j, p):
                act.wait_ge(s.x_full, j + 1)
                wait(act, s.v_full, j - 1)
                wait(act, s.res_ready, j - 1)
                nc.scalar.copy(xs[p][:, :], x_ps[:, :]).then_inc(s.xs_ready, 1)

            def trip(j, p):
                act.wait_ge(s.xs_ready, j + 1)
                wait(act, s.n_full, j)
                nc.scalar.activation(squares[1][:, :], xs[p][:, :], ACT.Square).then_inc(s.squares_ready, 1)
                act.wait_ge(s.inv_full, j + 1)
                nc.scalar.activation(A.invT[:, bass.ds(j * BLOCK, BLOCK)], inv_ps[:, :], ACT.Identity, bias=A.proj_bias[:, :]).then_inc(s.inv_ready, 1)
                if not (isinstance(j, int) and j == TRIPS - 1):
                    copy_x(j + 1, 1 - p)
                act.wait_ge(s.res_ready, j + 1)
                nc.scalar.activation(squares[0][:, :], res[:, :], ACT.Square).then_inc(s.squares_ready, 1)

            act.wait_ge(s.loaded, 16 * (SMALL - 1))
            copy_x(0, 0)
            in_trips(act, trip)
            act.wait_ge(s.n_ready, TRIPS)
            nc.scalar.activation(A.norms[:, :, :], A.norms[:, :, :], ACT.Sqrt).then_inc(s.sqrt_ready, 1)

        @block.gpsimd
        def _(pool):
            def trip(j, p):
                pool.wait_ge(s.ln_mv, j + 1)
                nc.gpsimd.tensor_tensor(var[:, :], mv[:, :, 1], c.eps[:, 0:GROUP], ALU.add).then_inc(s.ln_var, 1)
                pool.wait_ge(s.ln_var, j + 1)
                nc.gpsimd.tensor_tensor(rstd[:, :], var[:, :], c.minus_half[:, 0:GROUP], ALU.pow).then_inc(s.ln_rstd, 1)

            in_trips(pool, trip)

        @block.vector
        def _(dve):
            def statistics(j):
                for t in range(GROUP):
                    last = nc.vector.bn_stats(stats[:, t, :], X[:, j * GROUP + t, :])
                last.then_inc(s.ln_stats, 1)
                wait_alone(dve, s.ln_stats, j + 1, s.passed)
                for t in range(GROUP):
                    last = nc.vector.bn_aggr(mv[:, t, :], stats[:, t, :])
                last.then_inc(s.ln_mv, 1)

            def normalise(j):
                dve.wait_ge(s.ln_rstd, j + 1)
                wait(dve, s.x_full, j)
                for t in range(GROUP):
                    last = nc.vector.tensor_scalar(xn[:, t, :], X[:, j * GROUP + t, :], mv[:, t, 0:1], rstd[:, t:t + 1],
                                                   ALU.subtract, ALU.mult)
                last.then_inc(s.xn_ready, 1)

            def trip(j, p):
                more = not (isinstance(j, int) and j == TRIPS - 1)
                if more:
                    statistics(j + 1)
                dve.wait_ge(s.xs_ready, j + 1)
                nc.vector.tensor_copy(A.xnT[:, bass.ds(j * BLOCK, BLOCK)], xs[p][:, :])
                if more:
                    normalise(j + 1)
                dve.wait_ge(s.inv_ready, j + 1)
                wait(dve, s.squares_ready, at(j, 2, 0))
                nc.vector.tensor_tensor(res[:, :], xs[p][:, :], A.invT[:, bass.ds(j * BLOCK, BLOCK)], ALU.subtract).then_inc(s.res_ready, 1)
                dve.wait_ge(s.v_full, j + 1)
                nc.vector.tensor_tensor(A.v[:, bass.ds(j * GROUP + 1, GROUP), :], v_ps[:, :].rearrange("p (t d) -> p t d", d=P),
                                        A.v_bias[:, :].unsqueeze(1).broadcast_to([P, GROUP, P]), ALU.add).then_inc(s.v_ready, 1)
                dve.wait_ge(s.n_full, j + 1)
                nc.vector.tensor_copy(A.norms[:, bass.ds(j * GROUP, GROUP), :], n_ps[:, 0:2 * GROUP].rearrange("p (t m) -> p t m", m=2)).then_inc(s.n_ready, 1)

            nc.vector.memset(A.ones[:, :], 1.0)
            nc.vector.memset(A.tiny[:, :], 1e-10)
            for kept in (A.v, A.knT):
                for end in (0, TILES + 1):
                    nc.vector.memset(kept[:, end, :], 0.0)
            dve.wait_ge(s.turned, 1)
            nc.vector.tensor_copy(A.wT[:, 0:4, :], w_ps[:, :].rearrange("p (k d) -> p k d", d=P)).then_inc(s.kept, 1)
            nc.vector.tensor_copy(A.wT[:, 4, :], w_ps2[:, 0:P]).then_inc(s.kept, 1)
            nc.vector.tensor_copy(A.w1T[:, :], w_ps2[:, P:P + 64]).then_inc(s.kept, 1)
            dve.wait_ge(s.loaded, 16 * (SMALL - 1))
            statistics(0)
            normalise(0)
            in_trips(dve, trip)
            dve.wait_ge(s.sqrt_ready, 1)
            nc.vector.tensor_scalar(A.norms[:, :, 1], A.norms[:, :, 1], 1e-8, None, ALU.add).then_inc(s.gauge_step, 1)
            dve.wait_ge(s.gauge_step, 1)
            nc.vector.reciprocal(A.curv[:, :], A.norms[:, :, 1]).then_inc(s.gauge_step, 1)
            dve.wait_ge(s.gauge_step, 2)
            nc.vector.tensor_tensor(A.curv[:, :], A.curv[:, :], A.norms[:, :, 0], ALU.mult).then_inc(s.gauge_step, 1)
            dve.wait_ge(s.gauge_step, 3)
            nc.vector.tensor_reduce(A.gate[:, :], A.curv[:, :], AX.X, ALU.add).then_inc(s.gauge_step, 1)
            dve.wait_ge(s.gauge_step, 4)
            nc.vector.tensor_copy(A.norms[:, 0, 0:1], A.gate[:, :]).then_inc(s.gauge_step, 1)
            dve.wait_ge(s.gauge_full, 1)
            nc.vector.tensor_scalar(A.use_inv[:, 0:1], n_ps[:, 0:1], 1.0 / (BATCH * SEQ), 0.3, ALU.mult, ALU.is_gt).then_inc(s.gauge_step, 1)
            dve.wait_ge(s.gauge_step, 6)
            nc.vector.tensor_scalar(A.use_inv[:, 1:2], A.use_inv[:, 0:1], -1.0, 1.0, ALU.mult, ALU.add).then_inc(s.gauge_step, 1)


def band_queries(nc, K, A):
    c = K.c
    VECS = GROUP * 2 * B_HEADS
    with ExitStack() as ctx:
        sb = lambda name, shape, dt=F32: ctx.enter_context(nc.sbuf_tensor(f"bq_{name}", shape, dt))
        tmp, xq = sb("tmp", [P, BLOCK]), sb("xq", [P, BLOCK])
        qks = [sb(f"qk{i}", [P, GROUP, 2, P]) for i in range(2)]
        shifted, unit = (sb(n, [P, GROUP, 2, P]) for n in ("shifted", "unit"))
        expd = shifted
        square = K.w0.turned[:, TILES:TILES + 2 * GROUP, :].rearrange("p (t m) d -> p t m d", m=2)
        sumsq, rnorm, vmax, vsum, vrec, half_power = (sb(n, [P, VECS]) for n in ("sumsq", "rnorm", "vmax", "vsum", "vrec", "half_power"))
        total, texp, tlog = (sb(n, [P, 2 * P]) for n in ("total", "texp", "tlog"))
        tmax, tsum = sb("tmax", [P, 16]), sb("tsum", [P, 16])
        qk_ps = ctx.enter_context(nc.psum_tensor("bq_qk_ps", [P, 2, 512], F32))
        total_ps = ctx.enter_context(nc.psum_tensor("bq_total_ps", [P, 512], F32))
        unit_ps = [ctx.enter_context(nc.psum_tensor(f"bq_unit_ps{m}", [P, 512], F32)) for m in range(2)]
        s = stage_sems(nc, ctx, "bq", "tmp_ready xq_ready qk_full qk_ready totals squared sum_step rnorm_ready unit_ready soft_step unit_full unit_kept "
                                     "shift_ready exp_ready soft_ready marg_step marg_shift marg_exp marg_prob marg_log")
        block = ctx.enter_context(nc.Block())
        vecs = lambda ap: ap.rearrange("p t m (h d) -> p (t m h) d", d=B_DH)
        spread = lambda ap: ap[:, :].unsqueeze(2).broadcast_to([P, VECS, B_DH])

        @block.tensor
        def _(pe):
            def products(j, p):
                first = isinstance(j, int) and j == 0
                pe.wait_ge(s.xq_ready, j + 1)
                wait(pe, s.qk_ready, j)
                for t in range(GROUP):
                    last = nc.tensor.matmul(qk_ps[:, t // 2, (t % 2) * 256:(t % 2 + 1) * 256], xq[:, t * P:(t + 1) * P],
                                            A.wT[:, 0:2, :].rearrange("p m d -> p (m d)"), start=(t % 2 == 0), stop=True, skip_group_check=True)
                last.then_inc(s.qk_full, 1)
                pe.wait_ge(s.qk_ready, j + 1)
                for t in range(GROUP):
                    last = nc.tensor.matmul(total_ps[:, 0:2 * P], A.row_ones[:, :], qks[p][:, t].rearrange("p m d -> p (m d)"),
                                            start=(first and t == 0), stop=(not first and not isinstance(j, int)) or t == GROUP - 1,
                                            skip_group_check=True)
                last.then_inc(s.totals, 1)

            def turn_units(j):
                pe.wait_ge(s.unit_ready, j + 1)
                wait(pe, s.unit_kept, at(j, 2, 0))
                for m in range(2):
                    for t in range(GROUP):
                        last = nc.tensor.transpose(unit_ps[m][:, t * P:(t + 1) * P], unit[:, t, m, :], c.ident[:, :])
                    last.then_inc(s.unit_full, 1)

            def trip(j, p):
                if not (isinstance(j, int) and j == TRIPS - 1):
                    products(j + 1, 1 - p)
                turn_units(j)

            products(0, 0)
            in_trips(pe, trip)

        @block.scalar
        def _(act):
            def squares(j, p):
                act.wait_ge(s.qk_ready, j + 1)
                wait(act, s.sum_step, at(j, 2, -1))
                nc.scalar.activation(square[:, :, :, :], qks[p][:, :, :, :], ACT.Square).then_inc(s.squared, 1)
                act.wait_ge(s.shift_ready, j + 1)
                nc.scalar.activation(expd[:, :, :, :], shifted[:, :, :, :], ACT.Exp).then_inc(s.exp_ready, 1)

            def trip(j, p):
                if not (isinstance(j, int) and j == TRIPS - 1):
                    squares(j + 1, 1 - p)
                for m, keep in enumerate((A.qnT[:, bass.ds(j * GROUP, GROUP), :], A.knT[:, bass.ds(j * GROUP + 1, GROUP), :])):
                    act.wait_ge(s.unit_full, at(j, 2, m + 1))
                    nc.scalar.copy(keep, unit_ps[m][:, :].rearrange("p (t d) -> p t d", d=P)).then_inc(s.unit_kept, 1)

            squares(0, 0)
            in_trips(act, trip)
            act.wait_ge(s.marg_shift, 1)
            nc.scalar.activation(texp[:, :], total[:, :], ACT.Exp).then_inc(s.marg_exp, 1)
            act.wait_ge(s.marg_prob, 1)
            nc.scalar.activation(tlog[:, :], texp[:, :], ACT.Ln, bias=A.tiny[:, :]).then_inc(s.marg_log, 1)

        @block.gpsimd
        def _(pool):
            def trip(j, p):
                pool.wait_ge(s.sum_step, at(j, 2, 2))
                nc.gpsimd.tensor_tensor(rnorm[:, :], sumsq[:, :], half_power[:, :], ALU.pow).then_inc(s.rnorm_ready, 1)

            in_trips(pool, trip)

        @block.vector
        def _(dve):
            by_vec = lambda ap, m: ap.rearrange("p (t m h) -> p t m h", t=GROUP, m=2)[:, :, m, :].unsqueeze(3).broadcast_to([P, GROUP, B_HEADS, B_DH])
            heads = lambda ap: ap.rearrange("p t (h d) -> p t h d", d=B_DH)

            def choose(j):
                block_of = bass.ds(j * BLOCK, BLOCK)
                nc.vector.tensor_scalar(tmp[:, :], A.xnT[:, block_of], A.use_inv[:, 1:2], None, ALU.mult).then_inc(s.tmp_ready, 1)
                dve.wait_ge(s.tmp_ready, j + 1)
                wait(dve, s.qk_full, j)
                nc.vector.scalar_tensor_tensor(out=xq[:, :], in0=A.invT[:, block_of], scalar=A.use_inv[:, 0:1], in1=tmp[:, :],
                                               op0=ALU.mult, op1=ALU.add).then_inc(s.xq_ready, 1)

            def shift(j, p):
                dve.wait_ge(s.qk_full, j + 1)
                wait(dve, s.totals, j - 1)
                nc.vector.tensor_tensor(qks[p][:, :, :, :].rearrange("p t m d -> p t (m d)"), qk_ps[:, :, :].rearrange("p a (b d) -> p (a b) d", d=2 * P),
                                        A.qk_bias[:, :, :].rearrange("p m d -> p (m d)").unsqueeze(1).broadcast_to([P, GROUP, 2 * P]),
                                        ALU.add).then_inc(s.qk_ready, 1)
                dve.wait_ge(s.qk_ready, j + 1)
                nc.vector.tensor_reduce(vmax[:, :], vecs(qks[p][:, :, :, :]), AX.X, ALU.max).then_inc(s.soft_step, 1)
                dve.wait_ge(s.soft_step, at(j, 3, 1))
                nc.vector.tensor_tensor(vecs(shifted[:, :, :, :]), vecs(qks[p][:, :, :, :]), spread(vmax), ALU.subtract).then_inc(s.shift_ready, 1)

            def norms(j):
                dve.wait_ge(s.squared, j + 1)
                nc.vector.tensor_reduce(sumsq[:, :], vecs(square[:, :, :, :]), AX.X, ALU.add).then_inc(s.sum_step, 1)
                dve.wait_ge(s.sum_step, at(j, 2, 1))
                nc.vector.tensor_scalar(sumsq[:, :], sumsq[:, :], 1e-24, None, ALU.max).then_inc(s.sum_step, 1)

            def softmaxes(j, p):
                dve.wait_ge(s.exp_ready, j + 1)
                nc.vector.tensor_reduce(vsum[:, :], vecs(expd[:, :, :, :]), AX.X, ALU.add).then_inc(s.soft_step, 1)
                dve.wait_ge(s.soft_step, at(j, 3, 2))
                nc.vector.reciprocal(vrec[:, :], vsum[:, :]).then_inc(s.soft_step, 1)
                dve.wait_ge(s.soft_step, at(j, 3, 3))
                for m in range(2):
                    last = nc.vector.tensor_tensor(heads(A.soft[m][:, bass.ds(j * GROUP, GROUP), :]), heads(expd[:, :, m, :]), by_vec(vrec[:, :], m), ALU.mult)
                last.then_inc(s.soft_ready, 1)
                dve.wait_ge(s.soft_ready, j + 1)

            def units(j, p):
                dve.wait_ge(s.rnorm_ready, j + 1)
                wait(dve, s.unit_full, at(j, 2, 0))
                for m in range(2):
                    last = nc.vector.tensor_tensor(heads(unit[:, :, m, :]), heads(qks[p][:, :, m, :]), by_vec(rnorm[:, :], m), ALU.mult)
                last.then_inc(s.unit_ready, 1)

            def trip(j, p):
                more = not (isinstance(j, int) and j == TRIPS - 1)
                if more:
                    choose(j + 1)
                norms(j)
                softmaxes(j, p)
                if more:
                    shift(j + 1, 1 - p)
                units(j, p)

            nc.vector.memset(half_power[:, :], -0.5)
            choose(0)
            shift(0, 0)
            in_trips(dve, trip)
            by16 = lambda ap: ap[:, :].rearrange("p (v d) -> p v d", d=B_DH)
            spread16 = lambda ap: ap[:, :].unsqueeze(2).broadcast_to([P, 16, B_DH])
            dve.wait_ge(s.totals, TRIPS)
            nc.vector.tensor_reduce(tmax[:, :], total_ps[:, 0:2 * P].rearrange("p (v d) -> p v d", d=B_DH), AX.X, ALU.max).then_inc(s.marg_step, 1)
            dve.wait_ge(s.marg_step, 1)
            nc.vector.tensor_tensor(by16(total), total_ps[:, 0:2 * P].rearrange("p (v d) -> p v d", d=B_DH), spread16(tmax), ALU.subtract).then_inc(s.marg_shift, 1)
            dve.wait_ge(s.marg_exp, 1)
            nc.vector.tensor_reduce(tsum[:, :], by16(texp), AX.X, ALU.add).then_inc(s.marg_step, 1)
            dve.wait_ge(s.marg_step, 2)
            nc.vector.reciprocal(tsum[:, :], tsum[:, :]).then_inc(s.marg_step, 1)
            dve.wait_ge(s.marg_step, 3)
            nc.vector.tensor_tensor(by16(texp), by16(texp), spread16(tsum), ALU.mult).then_inc(s.marg_prob, 1)
            dve.wait_ge(s.marg_log, 1)
            nc.vector.tensor_tensor(total[:, :], texp[:, :], tlog[:, :], ALU.mult).then_inc(s.marg_step, 1)
            dve.wait_ge(s.marg_step, 4)
            nc.vector.tensor_reduce(A.plogp[:, :], total[:, :], AX.X, ALU.add).then_inc(s.marg_step, 1)


def band_entropies(nc, K, A):
    c = K.c
    GROUPS, PARTS = B_HEADS // 2, 4
    TURN = 4
    TURNS = TILES // TURN
    ROWS = SEQ // P
    STEPS = BATCH * ROWS * 2
    DEPTH = 4
    HI, LO = ((0, 1), (0, 2)), ((2, 3), (1, 3))
    with ExitStack() as ctx:
        sb = lambda name, shape, dt=F32: ctx.enter_context(nc.sbuf_tensor(f"be_{name}", shape, dt))
        parts = [[sb(f"parts_{n}{i}", [P, TURN, 2, PARTS, B_DH], F32R) for n in "qk"] for i in range(2)]
        partsT = [sb(f"partsT_{n}", [P, BATCH, SEQ], F32R) for n in "qk"]
        logs = [sb(f"logs{i}", [P, 2, 512]) for i in range(DEPTH)]
        sums = sb("sums", [P, BATCH, 2 * ROWS])
        entropy = sb("entropy", [P, 4])
        joint_all = sb("joint_all", [P, GROUPS, BATCH])
        joint_ps = [ctx.enter_context(nc.psum_tensor(f"be_joint{i}", [P, 2, 512], F32)) for i in range(DEPTH)]
        s = stage_sems(nc, ctx, "be", "hi_ready parts_ready turned kept_q kept_k joint_full log_ready summed row_summed entropy_step all_full")
        block = ctx.enter_context(nc.Block())

        def each_group(eng, one_group):
            one_group(0)
            with eng.Fori(1, GROUPS) as g:
                one_group(g)

        def source(m, g, j):
            return A.soft[m][:, j * TURN:(j + 1) * TURN, bass.ds(g * 2 * B_DH, 2 * B_DH)].rearrange("p t (a d) -> p t a d", d=B_DH)

        def kept(m, j, bank):
            return (partsT[m][:, :, j * TURN * SEG:(j + 1) * TURN * SEG].rearrange("p b (t n) -> p t b n", n=SEG),
                    joint_ps[bank][:, m, :].rearrange("p (t b n) -> p t b n", b=BATCH, n=SEG))

        @block.tensor
        def _(pe):
            def one_group(g):
                for j in range(TURNS):
                    pe.wait_ge(s.parts_ready, at(g, TURNS, j + 1))
                    if j >= DEPTH:
                        pe.wait_ge(s.kept_q, at(g, TURNS, j - DEPTH + 1))
                        pe.wait_ge(s.kept_k, at(g, TURNS, j - DEPTH + 1))
                    else:
                        wait(pe, s.summed, at(g, STEPS, j + 1 - DEPTH))
                    for m in range(2):
                        for t in range(TURN):
                            last = nc.tensor.transpose(joint_ps[j % DEPTH][:, m, t * P:(t + 1) * P],
                                                       parts[j % 2][m][:, t].rearrange("p a s d -> p (a s d)").bitcast(F32), c.ident[:, :])
                    last.then_inc(s.turned, 1)
                pe.wait_ge(s.kept_q, at(g, TURNS, TURNS))
                pe.wait_ge(s.kept_k, at(g, TURNS, TURNS))
                for k in range(STEPS):
                    b, i, half = k // (2 * ROWS), k // 2 % ROWS, k % 2
                    if k >= DEPTH:
                        pe.wait_ge(s.summed, at(g, STEPS, k - DEPTH + 1))
                    for a in range(2):
                        rows = slice(64 * a, 64 * (a + 1))
                        last = nc.tensor.matmul(joint_ps[k % DEPTH][:, a, :], partsT[0][rows, b, i * P:(i + 1) * P],
                                                partsT[1][rows, b, half * 512:(half + 1) * 512], start=True, stop=True)
                    last.then_inc(s.joint_full, 1)

            each_group(pe, one_group)
            pe.wait_ge(s.row_summed, GROUPS)
            pe.wait_ge(s.summed, GROUPS * STEPS)
            nc.tensor.matmul(joint_ps[0][:, 0, 0:GROUPS * BATCH], A.ones[:, :], A.joint[:, :], start=True, stop=True).then_inc(s.all_full, 1)

        @block.scalar
        def _(act):
            def one_group(g):
                def high(j):
                    wait(act, s.turned, at(g, TURNS, j - 1))
                    for m in range(2):
                        for place in HI[m]:
                            last = nc.scalar.copy(parts[j % 2][m][:, :, :, place, :], source(m, g, j))
                    last.then_inc(s.hi_ready, 1)

                high(0)
                for j in range(TURNS):
                    if j + 1 < TURNS:
                        high(j + 1)
                    act.wait_ge(s.turned, at(g, TURNS, j + 1))
                    if j == 0:
                        wait(act, s.joint_full, at(g, STEPS, 0))
                    nc.scalar.copy(*kept(0, j, j % DEPTH)).then_inc(s.kept_q, 1)
                for k in range(STEPS):
                    act.wait_ge(s.joint_full, at(g, STEPS, k + 1))
                    wait(act, s.summed, at(g, STEPS, k - DEPTH + 1))
                    nc.scalar.activation(logs[k % DEPTH][:, :, :], joint_ps[k % DEPTH][:, :, :], ACT.Ln, bias=A.tiny[:, :]).then_inc(s.log_ready, 1)

            each_group(act, one_group)

        @block.vector
        def _(dve):
            def one_group(g):
                def low(j):
                    dve.wait_ge(s.hi_ready, at(g, TURNS, j + 1))
                    for m in range(2):
                        for place in LO[m]:
                            last = nc.vector.tensor_tensor(parts[j % 2][m][:, :, :, place, :], source(m, g, j),
                                                           parts[j % 2][m][:, :, :, 0, :].bitcast(F32), ALU.subtract)
                    last.then_inc(s.parts_ready, 1)

                low(0)
                for j in range(TURNS):
                    if j + 1 < TURNS:
                        low(j + 1)
                    dve.wait_ge(s.turned, at(g, TURNS, j + 1))
                    if j == 0:
                        wait(dve, s.joint_full, at(g, STEPS, 0))
                    nc.vector.tensor_copy(*kept(1, j, j % DEPTH)).then_inc(s.kept_k, 1)
                wait(dve, s.row_summed, g)
                for k in range(STEPS):
                    dve.wait_ge(s.log_ready, at(g, STEPS, k + 1))
                    flat = logs[k % DEPTH][:, :, :].rearrange("p a j -> p (a j)")
                    nc.vector.tensor_tensor_reduce(out=flat, in0=joint_ps[k % DEPTH][:, :, :].rearrange("p a j -> p (a j)"), in1=flat,
                                                   scale=1.0, scalar=0.0, op0=ALU.mult, op1=ALU.add,
                                                   accum_out=sums[:, k // (2 * ROWS), k % (2 * ROWS):k % (2 * ROWS) + 1]).then_inc(s.summed, 1)
                dve.wait_ge(s.summed, at(g, STEPS, STEPS))
                nc.vector.tensor_reduce(A.joint[:, bass.ds(g * BATCH, BATCH)], sums[:, :, :], AX.X, ALU.add).then_inc(s.row_summed, 1)

            each_group(dve, one_group)
            dve.wait_ge(s.all_full, 1)
            nc.vector.tensor_tensor(joint_all[:, :, :], joint_ps[0][:, 0, 0:GROUPS * BATCH].rearrange("p (g b) -> p g b", b=BATCH),
                                    A.row_of[:, :].unsqueeze(1).broadcast_to([P, GROUPS, BATCH]), ALU.mult).then_inc(s.entropy_step, 1)
            dve.wait_ge(s.entropy_step, 1)
            nc.vector.tensor_reduce(entropy[:, 0:1], joint_all[:, :, :].rearrange("p g b -> p (g b)"), AX.X, ALU.add).then_inc(s.entropy_step, 1)
            dve.wait_ge(s.entropy_step, 2)
            nc.vector.tensor_tensor(entropy[:, 1:2], A.plogp[:, :], entropy[:, 0:1], ALU.subtract).then_inc(s.entropy_step, 1)
            dve.wait_ge(s.entropy_step, 3)
            nc.vector.tensor_scalar(A.gate[:, :], entropy[:, 1:2], 1.0 / B_HEADS, 0.15, ALU.mult, ALU.is_gt).then_inc(s.entropy_step, 1)


def band_windows(nc, K, A):
    c = K.c
    KEYS = GROUP + 2
    WIDE = WINDOW * SEG
    ROWS_T = GROUP * B_HEADS
    with ExitStack() as ctx:
        sb = lambda name, shape, dt=F32: ctx.enter_context(nc.sbuf_tensor(f"bw_{name}", shape, dt))
        qT = sb("qT", [P, BLOCK])
        kT = sb("kT", [P, B_HEADS, KEYS, P])
        spare = K.w0.turned[:, TILES:TILES + 3 * GROUP, :].rearrange("p (i t) d -> p i t d", t=GROUP)
        out = spare[:, 0, :, :]
        dist, expd = (sb(n, [P, GROUP, B_HEADS, WIDE]) for n in ("dist", "expd"))
        free = A.soft[1][:, :, :].rearrange("p w d -> p (w d)")
        expT = [free[0:WIDE, i * B_HEADS * P:(i + 1) * B_HEADS * P] for i in range(2)]
        rest = free[:, 2 * B_HEADS * P:2 * B_HEADS * P + 4 * BLOCK].rearrange("p (i n) -> p i n", n=BLOCK)
        outT, hid = rest[:, 0, :], out[0:64].rearrange("p t d -> p (t d)")
        v = [[rest[:, i, :].rearrange("p (t d) -> p t d", d=P) for i in (1, 2, 3)] + [spare[:, 1]],
             [spare[:, 2]] + [sb(f"v{b}", [WIDE, GROUP, P]) for b in range(1, BATCH)]]
        esum, erec, grec, eden = (sb(n, [P, ROWS_T]) for n in ("esum", "erec", "grec", "eden"))
        factor = sb("factor", [P, ROWS_T])
        OF_ACT, OF_DVE, OF_POOL = range(0, 2), range(2, 3), range(3, 8)
        sim_ps = [ctx.enter_context(nc.psum_tensor(f"bw_sim{i}", [P, 2, 512], F32)) for i in range(2)]
        exp_ps = ctx.enter_context(nc.psum_tensor("bw_exp", [P, 2, 512], F32))
        o_ps, tail_ps = (ctx.enter_context(nc.psum_tensor(f"bw_{n}", [P, 512], F32)) for n in ("o", "tail"))
        s = stage_sems(nc, ctx, "bw", "passed keys_ready v_ready sim_full clipped roots exps masked expT_full expT_ready summed esum_step recip_ready factor_ready "
                                     "o_full out_ready outT_full outT_ready h_full h_ready curv_full curv_ready z_full z_ready")
        block = ctx.enter_context(nc.Block())
        first_of = lambda j: isinstance(j, int) and j == 0
        last_of = lambda j: isinstance(j, int) and j == TRIPS - 1

        @block.tensor
        def _(pe):
            def scores(j, t):
                if t == 0:
                    pe.wait_ge(s.keys_ready, at(j, 3, 3))
                wait_alone(pe, s.clipped, at(j, GROUP, t - 1), s.passed)
                for b in range(BATCH):
                    seg = slice(SEG * b, SEG * (b + 1))
                    for g in range(2):
                        last = nc.tensor.matmul(sim_ps[t % 2][seg, g, 0:4 * WIDE].rearrange("p (h k m) -> p h k m", h=4, k=WINDOW),
                                                qT[:, t * P + SEG * b:t * P + SEG * (b + 1)], kT[:, 4 * g:4 * g + 4, t:t + WINDOW, seg],
                                                start=True, stop=True, skip_group_check=True)
                last.then_inc(s.sim_full, 1)

            def turn_exps(j, t):
                wait_alone(pe, s.expT_ready, at(j, GROUP, t), s.passed)
                wait_alone(pe, s.masked, at(j, GROUP, t + 1), s.passed)
                for h in range(B_HEADS):
                    last = nc.tensor.transpose(exp_ps[0:WIDE, h // 4, h % 4 * P:(h % 4 + 1) * P], expd[:, t, h, :], c.ident[:, :])
                last.then_inc(s.expT_full, 1)

            def values(j, p, t):
                if t == 0:
                    pe.wait_ge(s.v_ready, j + 1)
                    wait(pe, s.out_ready, j)
                wait_alone(pe, s.expT_ready, at(j, GROUP, t + 1), s.passed)
                for h in range(B_HEADS):
                    for b in range(BATCH):
                        last = nc.tensor.matmul(o_ps[SEG * b:SEG * (b + 1), t * P + h * B_DH:t * P + (h + 1) * B_DH],
                                                expT[t % 2][:, h * P + SEG * b:h * P + SEG * (b + 1)], v[p][b][0:WIDE, t, h * B_DH:(h + 1) * B_DH],
                                                start=True, stop=True, skip_group_check=True)
                last.then_inc(s.o_full, 1)

            def turn(j):
                pe.wait_ge(s.out_ready, j + 1)
                wait(pe, s.z_ready, j)
                for t in range(GROUP):
                    last = nc.tensor.transpose(tail_ps[:, t * P:(t + 1) * P], out[:, t, :], c.ident[:, :])
                last.then_inc(s.outT_full, 1)

            def hidden(j):
                pe.wait_ge(s.outT_ready, j + 1)
                nc.tensor.matmul(tail_ps[0:64, :], A.w1T[:, :], outT[:, :], start=True, stop=True).then_inc(s.h_full, 1)

            def curvature(j):
                pe.wait_ge(s.h_ready, j + 1)
                for t in range(GROUP):
                    last = nc.tensor.matmul(tail_ps[:, t:t + 1], hid[:, t * P:(t + 1) * P], A.w2T[:, :], start=(t == 0), stop=True, skip_group_check=True)
                last.then_inc(s.curv_full, 1)

            def project(j):
                pe.wait_ge(s.curv_ready, j + 1)
                for t in range(GROUP):
                    last = nc.tensor.matmul(tail_ps[:, t * P:(t + 1) * P], outT[:, t * P:(t + 1) * P], A.wT[:, 4, :], start=(t == 0), stop=True,
                                            skip_group_check=True)
                last.then_inc(s.z_full, 1)

            def trip(j, p):
                for t in range(GROUP):
                    turn_exps(j, t)
                    if not last_of(j):
                        scores(j + 1, t)
                    if not first_of(j):
                        if t == 0:
                            turn(j - 1)
                        if t == 1:
                            hidden(j - 1)
                        if t == 2:
                            curvature(j - 1)
                        if t == 3:
                            project(j - 1)
                    values(j, p, t)

            for t in range(GROUP):
                scores(0, t)
            in_trips(pe, trip)
            turn(TRIPS - 1)
            hidden(TRIPS - 1)
            curvature(TRIPS - 1)
            project(TRIPS - 1)

        @block.scalar
        def _(act):
            def keys(j):
                wait(act, s.sim_full, at(j, GROUP, 0))
                for h in OF_ACT:
                    nc.scalar.activation(kT[:, h, :, :], A.knT[:, bass.ds(j * GROUP, KEYS), :], ACT.Identity, scale=A.head_of[:, h:h + 1])
                nc.scalar.copy(qT[:, :], A.qnT[:, bass.ds(j * GROUP, GROUP), :].rearrange("p t d -> p (t d)")).then_inc(s.keys_ready, 1)

            def roots(j, t):
                act.wait_ge(s.clipped, at(j, GROUP, t + 1))
                nc.scalar.activation(dist[:, t], dist[:, t], ACT.Sqrt).then_inc(s.roots, 1)

            def exps(j, t):
                act.wait_ge(s.roots, at(j, GROUP, t + 1))
                wait(act, s.summed, at(j, GROUP, t + 1 - GROUP))
                wait(act, s.expT_full, at(j, GROUP, t + 1 - GROUP))
                nc.scalar.activation(expd[:, t], dist[:, t], ACT.Exp, scale=-1.0).then_inc(s.exps, 1)

            def keep_exps(j, t):
                act.wait_ge(s.expT_full, at(j, GROUP, t + 1))
                wait(act, s.o_full, at(j, GROUP, t - 1))
                nc.scalar.copy(expT[t % 2], exp_ps[0:WIDE, :, :].rearrange("p k d -> p (k d)")).then_inc(s.expT_ready, 1)

            def tail_1(j):
                act.wait_ge(s.outT_full, j + 1)
                wait(act, s.z_full, j)
                nc.scalar.copy(outT, tail_ps[:, :]).then_inc(s.outT_ready, 1)

            def tail_2(j):
                act.wait_ge(s.h_full, j + 1)
                wait(act, s.curv_full, j)
                nc.scalar.activation(hid, tail_ps[0:64, :], ACT.Relu, bias=A.b1[:, :]).then_inc(s.h_ready, 1)

            def tail_3(j):
                act.wait_ge(s.z_full, j + 1)
                nc.scalar.copy(A.soft[0][:, bass.ds(j * GROUP, GROUP), :], tail_ps[:, :].rearrange("p (t d) -> p t d", d=P)).then_inc(s.z_ready, 1)

            def trip(j, p):
                if not last_of(j):
                    keys(j + 1)
                for t in range(GROUP):
                    exps(j, t)
                for t in range(GROUP):
                    keep_exps(j, t)
                    if not first_of(j):
                        if t == 1:
                            tail_1(j - 1)
                        if t == 2:
                            tail_2(j - 1)
                    if not last_of(j) and t >= 2:
                        roots(j + 1, t - 2)
                if not last_of(j):
                    roots(j + 1, 2)
                    roots(j + 1, 3)
                if not first_of(j):
                    tail_3(j - 1)

            keys(0)
            for t in range(GROUP):
                roots(0, t)
            in_trips(act, trip)
            tail_1(TRIPS - 1)
            tail_2(TRIPS - 1)
            tail_3(TRIPS - 1)

        @block.gpsimd
        def _(pool):
            def keys(j):
                wait(pool, s.sim_full, at(j, GROUP, 0))
                for h in OF_POOL:
                    last = nc.gpsimd.tensor_tensor(kT[:, h, :, :], A.knT[:, bass.ds(j * GROUP, KEYS), :],
                                                   A.head_of[:, h:h + 1].unsqueeze(2).broadcast_to([P, KEYS, P]), ALU.mult)
                last.then_inc(s.keys_ready, 1)

            def trip(j, p):
                if not last_of(j):
                    keys(j + 1)

            keys(0)
            in_trips(pool, trip)

        @block.vector
        def _(dve):
            def squared(j, t):
                dve.wait_ge(s.sim_full, at(j, GROUP, t + 1))
                wait(dve, s.exps, at(j, GROUP, t + 1 - GROUP))
                tile = dist[:, t].rearrange("p (g h) m -> p g (h m)", g=2)
                nc.vector.tensor_scalar(tile, sim_ps[t % 2][:, :, 0:4 * WIDE], 2.0, 0.0, ALU.add, ALU.max).then_inc(s.clipped, 1)

            def weights(j, t):
                dve.wait_ge(s.exps, at(j, GROUP, t + 1))
                edge = 0 if first_of(j) and t == 0 else 2 if last_of(j) and t == GROUP - 1 else 1
                nc.vector.scalar_tensor_tensor(out=expd[:, t], in0=expd[:, t], scalar=float(np.exp(-2.0)), op0=ALU.max,
                                               in1=A.band[:, edge, :].unsqueeze(1).broadcast_to([P, B_HEADS, WIDE]), op1=ALU.mult).then_inc(s.masked, 1)
                dve.wait_ge(s.masked, at(j, GROUP, t + 1))
                nc.vector.tensor_reduce(esum[:, t * B_HEADS:(t + 1) * B_HEADS], expd[:, t], AX.X, ALU.add).then_inc(s.summed, 1)

            def factors(j):
                step = lambda k: at(j, 4, k)
                dve.wait_ge(s.summed, at(j, GROUP, GROUP))
                nc.vector.reciprocal(erec[:, :], esum[:, :]).then_inc(s.esum_step, 1)
                dve.wait_ge(s.esum_step, step(1))
                nc.vector.tensor_scalar(grec[:, :], erec[:, :], A.gate[:, :], None, ALU.mult).then_inc(s.esum_step, 1)
                dve.wait_ge(s.esum_step, step(2))
                nc.vector.tensor_tensor(eden[:, :], grec[:, :], esum[:, :], ALU.mult).then_inc(s.esum_step, 1)
                dve.wait_ge(s.esum_step, step(3))
                nc.vector.tensor_scalar(eden[:, :], eden[:, :], 1e-10, None, ALU.add).then_inc(s.esum_step, 1)
                dve.wait_ge(s.esum_step, step(4))
                nc.vector.reciprocal(eden[:, :], eden[:, :]).then_inc(s.recip_ready, 1)
                dve.wait_ge(s.recip_ready, j + 1)
                nc.vector.tensor_tensor(factor[:, :], eden[:, :], grec[:, :], ALU.mult).then_inc(s.factor_ready, 1)

            def output(j):
                dve.wait_ge(s.factor_ready, j + 1)
                dve.wait_ge(s.o_full, at(j, GROUP, GROUP))
                wait(dve, s.curv_full, j)
                nc.vector.tensor_tensor(out[:, :, :].rearrange("p t (h d) -> p (t h) d", d=B_DH), o_ps[:, :].rearrange("p (r d) -> p r d", d=B_DH),
                                        factor[:, :].unsqueeze(2).broadcast_to([P, ROWS_T, B_DH]), ALU.mult).then_inc(s.out_ready, 1)

            def curvature(j):
                dve.wait_ge(s.curv_full, j + 1)
                nc.vector.tensor_copy(A.curv[:, bass.ds(j * GROUP, GROUP)], tail_ps[:, 0:GROUP]).then_inc(s.curv_ready, 1)

            def keys(j):
                wait(dve, s.sim_full, at(j, GROUP, 0))
                for h in OF_DVE:
                    last = nc.vector.tensor_scalar(kT[:, h, :, :], A.knT[:, bass.ds(j * GROUP, KEYS), :], A.head_of[:, h:h + 1], None, ALU.mult)
                last.then_inc(s.keys_ready, 1)

            def copy_v(j, p):
                wait(dve, s.o_full, at(j, GROUP, -GROUP))
                for b in range(BATCH):
                    for k in range(WINDOW):
                        last = nc.vector.tensor_copy(v[p][b][SEG * k:SEG * (k + 1), :, :], A.v[SEG * b:SEG * (b + 1), bass.ds(j * GROUP + k, GROUP), :])
                last.then_inc(s.v_ready, 1)

            def trip(j, p):
                if not last_of(j):
                    keys(j + 1)
                for t in range(GROUP):
                    weights(j, t)
                    if t == 0 and not first_of(j):
                        output(j - 1)
                    if not last_of(j):
                        squared(j + 1, t)
                    if t == 2 and not first_of(j):
                        curvature(j - 1)
                factors(j)
                if not last_of(j):
                    copy_v(j + 1, 1 - p)

            keys(0)
            copy_v(0, 0)
            for t in range(GROUP):
                squared(0, t)
            in_trips(dve, trip)
            output(TRIPS - 1)
            curvature(TRIPS - 1)


def band_sum(nc, K, A):
    X = K.X
    with ExitStack() as ctx:
        sb = lambda name, shape, dt=F32: ctx.enter_context(nc.sbuf_tensor(f"bs_{name}", shape, dt))
        curved, social, penalty = sb("curved", [P, TILES]), sb("social", [P, 1]), sb("penalty", [P, 4])
        sum_ps = ctx.enter_context(nc.psum_tensor("bs_sum", [P, 512], F32))
        s = stage_sems(nc, ctx, "bs", "curved_ready social_full exp_ready step")
        block = ctx.enter_context(nc.Block())

        @block.scalar
        def _(act):
            nc.scalar.activation(curved[:, :], A.curv[:, :], ACT.Sigmoid, bias=A.b2[:, :]).then_inc(s.curved_ready, 1)
            act.wait_ge(s.social_full, 1)
            nc.scalar.activation(penalty[:, 0:1], sum_ps[:, 0:1], ACT.Exp, scale=-1.0 / 0.5 / (BATCH * SEQ)).then_inc(s.exp_ready, 1)

        @block.tensor
        def _(pe):
            pe.wait_ge(s.step, 1)
            nc.tensor.matmul(sum_ps[:, 0:1], A.ones[:, :], social[:, :], start=True, stop=True).then_inc(s.social_full, 1)

        @block.vector
        def _(dve):
            dve.wait_ge(s.curved_ready, 1)
            nc.vector.tensor_reduce(social[:, :], curved[:, :], AX.X, ALU.add).then_inc(s.step, 1)
            dve.wait_ge(s.exp_ready, 1)
            nc.vector.tensor_scalar(penalty[:, 1:2], penalty[:, 0:1], 0.5, 1.5, ALU.max, ALU.min).then_inc(s.step, 1)
            dve.wait_ge(s.step, 2)
            nc.vector.tensor_scalar(penalty[:, 2:3], penalty[:, 1:2], -1.0, 1.0, ALU.mult, ALU.add).then_inc(s.step, 1)
            dve.wait_ge(s.step, 3)
            nc.vector.tensor_scalar(penalty[:, 3:4], penalty[:, 2:3], -0.3, 1.0, ALU.mult, ALU.add).then_inc(s.step, 1)
            dve.wait_ge(s.step, 4)
            nc.vector.scalar_tensor_tensor(out=X[:, :, :], in0=A.soft[0][:, :, :], scalar=penalty[:, 3:4], in1=X[:, :, :],
                                           op0=ALU.mult, op1=ALU.add).then_inc(s.step, 1)
            dve.wait_ge(s.step, 5)
            nc.vector.tensor_tensor(X[:, :, :], X[:, :, :], A.o_bias[:, :].unsqueeze(1).broadcast_to([P, TILES, P]), ALU.add).then_inc(s.step, 1)
def load_stage(nc, K, io):
    X, c, w0 = K.X, K.c, K.w0
    with ExitStack() as ctx:
        sb = lambda name, shape, dt=F32: ctx.enter_context(nc.sbuf_tensor(f"ld_{name}", shape, dt))
        BLOCKS = 5 * NE
        natural = sb("natural", [P, BLOCKS, D])
        gate_natural = sb("gate_natural", [E, D])
        banks = [ctx.enter_context(nc.psum_tensor(f"ld_ps{i}", [P, 512], F32)) for i in range(2)]
        s = stage_sems(nc, ctx, "ld", "const x natural small turned kept")
        block = ctx.enter_context(nc.Block())
        up = [natural[:, m * 2 * NE:(m + 1) * 2 * NE, :].rearrange("p (e two) d -> p e two d", two=2) for m in range(2)]
        down = natural[:, 4 * NE:5 * NE, :]
        quads = [(i, min(4, BLOCKS - i)) for i in range(0, BLOCKS, 4)]
        turned = w0.turned[:, :, :].rearrange("p k f -> p (k f)")

        @block.sync
        def _(sp):
            for dst, name in ((c.ident, "c_ident"), (c.iota, "c_iota"), (c.minus_half, "c_minus_half"), (c.eps, "c_eps")):
                sp.dma_start(dst[:, :], io[name]).then_inc(s.const, 16)
            for m, (routed, shared) in enumerate((("L0_ffn_w1", "L0_ffn_sw1"), ("L0_ffn_w3", "L0_ffn_sw3"))):
                sp.dma_start(up[m][:, 0:E], io[routed].rearrange("e (p two) d -> p e two d", two=2)).then_inc(s.natural, 16)
                sp.dma_start(up[m][:, E], io[shared].rearrange("(p two) d -> p two d", two=2)).then_inc(s.natural, 16)
            sp.dma_start(down[:, 0:E, :], io["L0_ffn_w2"].rearrange("e d f -> d e f")).then_inc(s.natural, 16)
            sp.dma_start(down[:, E, :], io["L0_ffn_sw2"]).then_inc(s.natural, 16)
            sp.dma_start(gate_natural[:, :], io["L0_ffn_gate_w"]).then_inc(s.natural, 16)
            for b in range(BATCH):
                sp.dma_start(X[SEG * b:SEG * (b + 1), :, :], io["L0_attn_x"][b].rearrange("(w n) d -> n w d", n=SEG)).then_inc(s.x, 16)
            sp.wait_ge(s.x, 16 * BATCH)

        @block.scalar
        def _(act):
            n = 0
            with nc.allow_non_contiguous_dma(reason="biases, one element per partition"):
                for dst, src in ((w0.b1[:, 0:E, :], io["L0_ffn_b1"].rearrange("e (p two) -> p e two", two=2)),
                                 (w0.b1[:, E, :], io["L0_ffn_sb1"].rearrange("(p two) -> p two", two=2)),
                                 (w0.b3[:, 0:E, :], io["L0_ffn_b3"].rearrange("e (p two) -> p e two", two=2)),
                                 (w0.b3[:, E, :], io["L0_ffn_sb3"].rearrange("(p two) -> p two", two=2)),
                                 (w0.b2[0:E, :], io["L0_ffn_b2"]), (w0.b2[E:NE, :], io["L0_ffn_sb2"].unsqueeze(0)),
                                 (w0.router_bias[:, :], io["L0_ffn_gate_b"].partition_broadcast(P))):
                    act.dma_start(dst, src).then_inc(s.small, 16)
                    n += 16
            act.wait_ge(s.small, n)

        @block.tensor
        def _(pe):
            pe.wait_ge(s.const, 64)
            pe.wait_ge(s.natural, 16 * 7)
            for q, (first, count) in enumerate(quads):
                if q >= 2:
                    pe.wait_ge(s.kept, q - 1)
                for k in range(count):
                    last = nc.tensor.transpose(banks[q % 2][:, k * P:(k + 1) * P], natural[:, first + k, :], c.ident[:, :])
                last.then_inc(s.turned, 1)
            pe.wait_ge(s.kept, len(quads) - 1)
            nc.tensor.transpose(banks[len(quads) % 2][:, 0:E], gate_natural[:, :], c.ident[0:E, 0:E]).then_inc(s.turned, 1)

        @block.vector
        def _(dve):
            for q, (first, count) in enumerate(quads):
                dve.wait_ge(s.turned, q + 1)
                nc.vector.tensor_copy(turned[:, first * P:(first + count) * P], banks[q % 2][:, 0:count * P]).then_inc(s.kept, 1)
            dve.wait_ge(s.turned, len(quads) + 1)
            nc.vector.tensor_copy(w0.router[:, :], banks[len(quads) % 2][:, 0:E]).then_inc(s.kept, 1)


def load_silu_weights(nc, eng, io, w, loaded):
    n = 0
    with nc.allow_non_contiguous_dma(reason="biases, one element per partition"):
        for dst, src in ((w.router1[:, :], io["L1_ffn_Wr1"]), (w.router1_bias[:, :], io["L1_ffn_br1"].unsqueeze(1)),
                         (w.router2[:, :], io["L1_ffn_Wr2"]), (w.router2_bias[:, :], io["L1_ffn_br2"].partition_broadcast(P)),
                         (w.be1[:, 0:E, :], io["L1_ffn_be1"].rearrange("e (k p) -> p e k", p=P)),
                         (w.be1[:, E, :], io["L1_ffn_bs1"].rearrange("(k p) -> p k", p=P)),
                         (w.be2[0:E, :], io["L1_ffn_be2"]), (w.be2[E:NE, :], io["L1_ffn_bs2"].unsqueeze(0)),
                         (w.we1[:, 0:E, :], io["L1_ffn_We1"].rearrange("e c i -> c e i")), (w.we1[:, E, :], io["L1_ffn_Ws1"]),
                         (w.we2[:, E, :, :], io["L1_ffn_Ws2"].rearrange("(k p) c -> p k c", p=P)),
                         *((w.we2[:, e, :, :], io["L1_ffn_We2"][e].rearrange("(k p) c -> p k c", p=P)) for e in range(E))):
            eng.dma_start(dst, src).then_inc(loaded, 16)
            n += 16
    eng.wait_ge(loaded, n)


def store_stage(nc, K, out):
    with ExitStack() as ctx:
        stored = ctx.enter_context(nc.semaphore("stored"))
        block = ctx.enter_context(nc.Block())

        @block.sync
        def _(sp):
            for b in range(BATCH):
                sp.dma_start(out[b].rearrange("(w n) d -> n w d", n=SEG), K.X[SEG * b:SEG * (b + 1), :, :]).then_inc(stored, 16)
            sp.wait_ge(stored, 16 * BATCH)


def allocate_silu_weights(sb, K):
    K.w1 = w1 = Named()
    w1.we1 = sb("w1_we1", [P, NE, 512])
    w1.we2 = sb("w1_we2", [P, NE, 4, D])
    w1.be1 = sb("w1_be1", [P, NE, 4])
    w1.be2 = sb("w1_be2", [NE, D])
    w1.router1 = sb("w1_router1", [P, 32])
    w1.router1_bias = sb("w1_router1_bias", [32, 1])
    w1.router2 = sb("w1_router2", [32, E])
    w1.router2_bias = sb("w1_router2_bias", [P, E])


def allocate_gated_weights(sb, K):
    K.w0 = w0 = Named()
    w0.turned = sb("w0_turned", [P, 5 * NE, P])
    w0.w13T = w0.turned[:, 0:4 * NE, :].rearrange("p (m e two) f -> p m e two f", m=2, two=2)
    w0.w2T = w0.turned[:, 4 * NE:5 * NE, :]
    w0.router = sb("w0_router", [P, E])
    w0.router_bias = sb("w0_router_bias", [P, E])
    w0.b1 = sb("w0_b1", [P, NE, 2])
    w0.b3 = sb("w0_b3", [P, NE, 2])
    w0.b2 = sb("w0_b2", [NE, D])


def build_program(nc, io, out):
    with ExitStack() as ctx:
        sb = lambda name, shape, dt=F32: ctx.enter_context(nc.sbuf_tensor(name, shape, dt))
        K = Named()
        K.X = sb("X", [P, TILES, D])
        K.c = c = Named()
        c.ident = sb("ident", [P, P])
        c.iota = sb("iota", [P, E])
        c.minus_half = sb("minus_half", [P, 8])
        c.eps = sb("eps", [P, 8])
        allocate_gated_weights(sb, K)
        K.s0 = make_sems(nc, ctx, "f0", ROUTE_SEMS + " t3g_ready t3l_ready pg_ready pl_ready g_ready l_ready gl_ready sig_ready "
                                                     "full_g1 full_g3 full_l1 full_l3 a_ready y_full y_done x_done")
        K.s1 = make_sems(nc, ctx, "f1", ROUTE_SEMS + " pair_mult loaded x_high x_parts w_high w_parts y_full y_done x_done", "h_full a_ready")
        load_stage(nc, K, io)
        gated_stage(nc, K, 0, io)
        memory_attention_stage(nc, K, io)
        allocate_silu_weights(sb, K)
        gated_stage(nc, K, 1, io)
        silu_stage(nc, K, 0)
        band_attention_stage(nc, K, io)
        silu_stage(nc, K, 1)
        store_stage(nc, K, out)


def constants():
    place = np.arange(P) % SEG
    angle = np.outer(10000.0 ** (-np.arange(0, DH, 2) / DH), place)
    rows = np.arange(P) % DH // 2
    key = np.arange(WINDOW * SEG) - SEG
    near = np.abs(place[:, None] - key[None, :]) <= 32
    band = np.stack([near & (key >= 0), near, near & (key < SEG)], axis=1)
    return {"c_ident": np.eye(P, dtype=np.float32),
            "c_iota": np.tile(np.arange(E, dtype=np.float32), (P, 1)),
            "c_minus_half": np.full((P, 8), -0.5, np.float32),
            "c_eps": np.full((P, 8), LN_EPS, np.float32),
            "c_cos": np.cos(angle)[rows].astype(np.float32), "c_sin": np.sin(angle)[rows].astype(np.float32),
            "c_causal": np.where(np.arange(SEG)[None, :] <= place[:, None], 0.0, -1e30).astype(np.float32),
            "c_row_ones": (np.arange(P)[:, None] // SEG == np.arange(P)[None, :] // SEG).astype(np.float32),
            "c_row_of": (np.arange(P)[:, None] // SEG == np.arange(BATCH)[None, :]).astype(np.float32),
            "c_head_of": np.where(np.arange(P)[:, None] // B_DH == np.arange(B_HEADS)[None, :], -2.0, 0.0).astype(np.float32),
            "c_band": band.astype(np.float32)}


def kernel(**inputs):
    import concourse.bacc as bacc
    from concourse.bass_utils import run_bass_kernel_spmd

    nc = bacc.Bacc("TRN2", target_bir_lowering=False, num_devices=1)
    arrays = {name: np.ascontiguousarray(a) for name, a in inputs.items()} | constants()
    io = {name: nc.dram_tensor(name, a.shape, F32, kind="ExternalInput").ap() for name, a in arrays.items()}
    out = nc.dram_tensor("out", (BATCH, SEQ, D), F32, kind="ExternalOutput").ap()
    build_program(nc, io, out)
    return run_bass_kernel_spmd(nc, [arrays], core_ids=[0]).results[0]["out"]
```
